# Optimizing a Trainium2 kernel written in Bass

```python
import numpy as np
import jax
import jax.numpy as jnp

def _softmax(x, axis=-1):
    return jax.nn.softmax(x, axis=axis)

def _gelu(x):
    return jax.nn.gelu(x, approximate=True)

def _silu(x):
    return jax.nn.silu(x)

def _sigmoid(x):
    return jax.nn.sigmoid(x)

def _layernorm(x, axis=-1, eps=1e-05):
    m = jnp.mean(x, axis=axis, keepdims=True)
    v = jnp.var(x, axis=axis, keepdims=True)
    return (x - m) / jnp.sqrt(v + eps)

def _scatter_add(tgt, idx, src, axis=0):
    return tgt.at[idx].add(src)

def _segment_sum(src, seg, n):
    return jax.ops.segment_sum(src, seg, n)
kernel_name = 'mk_decoder_preln_d2_seqx_r8_5aea9e'

def setup_inputs(seed: int=0):
    np.random.seed(seed)
    _w = jnp.asarray

    def _rec_inputs():
        import jax
        import jax.numpy as jnp
        _rk = jax.random.key(seed)
        x = -0.0002928 + 1 * jax.random.normal(jax.random.fold_in(_rk, 1), (4, 256, 512), jnp.float32)
        _lenS = 256 - jax.random.randint(jax.random.fold_in(_rk, 7), (4,), 0, max(1, 256 // 4) + 1, jnp.int32)
        _lenS2 = 64 - jax.random.randint(jax.random.fold_in(_rk, 8), (4,), 0, max(1, 64 // 4) + 1, jnp.int32)
        _ctx_4096P = jax.random.normal(jax.random.fold_in(_rk, 11), (4, 16, 512), jnp.float32)
        _ctx_4096c = jax.random.dirichlet(jax.random.fold_in(_rk, 511), 0.3 * jnp.ones((16,), jnp.float32), (4, 64))
        _ctx_4096t = jnp.einsum('bsk,bkd->bsd', _ctx_4096c, _ctx_4096P)
        _ctx_4096t = _ctx_4096t * jax.lax.rsqrt(jnp.mean(jnp.square(_ctx_4096t)) + 1e-12) * 0.953939
        ctx_4096 = -2.8382e-05 + 0.999851 * (_ctx_4096t + 0.3 * jax.random.normal(jax.random.fold_in(_rk, 611), (4, 64, 512), jnp.float32))
        _validS = jnp.arange(256)[None, :] < _lenS[:, None]
        _validS2 = jnp.arange(64)[None, :] < _lenS2[:, None]
        _causal = jnp.tril(jnp.ones((256, 256), dtype=bool))
        mask_1x1xSxS2_ff0 = jnp.where(jnp.ones((1, 1, 256, 64), dtype=bool), 0.0, -1000000000.0).astype(jnp.float32)
        return (x, ctx_4096, mask_1x1xSxS2_ff0)
    x, ctx_4096, mask_1x1xSxS2_ff0 = _rec_inputs()

    def _L0_attn_setup():
        import jax, jax.numpy as jnp
        import numpy as np
        B, N, D = (2, 256, 512)
        H, HD = (32, 128)
        EPS = 1e-06

        def rmsnorm(x, w):
            xf = x.astype(jnp.float32)
            var = jnp.mean(xf * xf, axis=-1, keepdims=True)
            return (w * (xf * jax.lax.rsqrt(var + EPS))).astype(x.dtype)
        key = jax.random.key(seed)
        ks = jax.random.split(key, 11)
        s = 1.0 / np.sqrt(D)
        return {'hidden_states': jax.random.normal(ks[0], (B, N, D), jnp.float32), 'Wq': jax.random.normal(ks[1], (D, H * HD), jnp.float32) * s, 'bq': jax.random.normal(ks[2], (H * HD,), jnp.float32) * 0.01, 'Wk': jax.random.normal(ks[3], (D, H * HD), jnp.float32) * s, 'bk': jax.random.normal(ks[4], (H * HD,), jnp.float32) * 0.01, 'Wv': jax.random.normal(ks[5], (D, H * HD), jnp.float32) * s, 'bv': jax.random.normal(ks[6], (H * HD,), jnp.float32) * 0.01, 'Wo': jax.random.normal(ks[7], (H * HD, D), jnp.float32) * s, 'bo': jax.random.normal(ks[8], (D,), jnp.float32) * 0.01, 'gq': jnp.ones((HD,), jnp.float32), 'gk': jnp.ones((HD,), jnp.float32)}
    _L0_attn_all = _L0_attn_setup()
    _L0_attn_in = {k: v for k, v in _L0_attn_all.items() if k in ('Wq', 'bq', 'Wk', 'bk', 'Wv', 'bv', 'Wo', 'bo', 'gq', 'gk')}
    del _L0_attn_all

    def _L0_xattn_setup():
        import jax, jax.numpy as jnp
        import numpy as np
        NUM_HEADS = 32
        NUM_KV_HEADS = 8
        HEAD_DIM = 128
        HIDDEN = 512
        EPS = 1e-05

        def rmsnorm(x, w, eps=EPS):
            xf = x.astype(jnp.float32)
            var = jnp.mean(xf * xf, axis=-1, keepdims=True)
            return w * (xf * jax.lax.rsqrt(var + eps)).astype(x.dtype)
        key = jax.random.key(seed)
        ks = jax.random.split(key, 10)
        B, Q, KV = (1, 128, 6404)
        s = 1.0 / np.sqrt(HIDDEN)
        return {'hidden_states': jax.random.normal(ks[0], (B, Q, HIDDEN), jnp.float32), 'cross_attention_states': jax.random.normal(ks[1], (B, KV, HIDDEN), jnp.float32), 'attention_mask': jnp.zeros((B, 1, Q, KV), jnp.float32), 'q_proj_w': jax.random.normal(ks[2], (NUM_HEADS * HEAD_DIM, HIDDEN), jnp.float32) * s, 'k_proj_w': jax.random.normal(ks[3], (NUM_KV_HEADS * HEAD_DIM, HIDDEN), jnp.float32) * s, 'v_proj_w': jax.random.normal(ks[4], (NUM_KV_HEADS * HEAD_DIM, HIDDEN), jnp.float32) * s, 'o_proj_w': jax.random.normal(ks[5], (HIDDEN, NUM_HEADS * HEAD_DIM), jnp.float32) * s, 'q_norm_w': jnp.ones((HEAD_DIM,), jnp.float32), 'k_norm_w': jnp.ones((HEAD_DIM,), jnp.float32)}
    _L0_xattn_all = _L0_xattn_setup()
    _L0_xattn_in = {k: v for k, v in _L0_xattn_all.items() if k in ('q_proj_w', 'k_proj_w', 'v_proj_w', 'o_proj_w', 'q_norm_w', 'k_norm_w')}
    del _L0_xattn_all

    def _L0_ffn_setup():
        import jax, jax.numpy as jnp
        import numpy as np
        TOP_K = 2
        key = jax.random.key(seed)
        k1, k2, k3 = jax.random.split(key, 3)
        B, S, H, O, E = (1024, 1, 512, 512, 8)
        x = jax.random.normal(k1, (B, S, H), dtype=jnp.float32)
        gate_w = jax.random.normal(k2, (H, E), dtype=jnp.float32) * 0.02
        expert_w = jax.random.normal(k3, (E, H, O), dtype=jnp.float32) * 0.02
        return {'x': x, 'gate_w': gate_w, 'expert_w': expert_w}
    _L0_ffn_all = _L0_ffn_setup()
    _L0_ffn_in = {k: v for k, v in _L0_ffn_all.items() if k in ('gate_w', 'expert_w')}
    del _L0_ffn_all

    def _L1_attn_setup():
        import jax, jax.numpy as jnp
        import numpy as np
        HIDDEN = 512
        NUM_HEADS = 32
        HEAD_DIM = HIDDEN // NUM_HEADS

        def _fp8_roundtrip(x):
            return x.astype(jnp.float8_e4m3fn).astype(jnp.float32)
        key = jax.random.key(seed)
        ks = jax.random.split(key, 10)
        B, S = (2, 512)
        hidden_states = jax.random.normal(ks[0], (B, S, HIDDEN), dtype=jnp.float32)
        scale = 0.02

        def lin(kw, kb):
            w = jax.random.normal(kw, (HIDDEN, HIDDEN), dtype=jnp.float32) * scale
            b = jax.random.normal(kb, (HIDDEN,), dtype=jnp.float32) * scale
            return (w, b)
        wq, bq = lin(ks[1], ks[2])
        wk, bk = lin(ks[3], ks[4])
        wv, bv = lin(ks[5], ks[6])
        wl, bl = lin(ks[7], ks[8])
        wq, bq = (_fp8_roundtrip(wq), _fp8_roundtrip(bq))
        wk, bk = (_fp8_roundtrip(wk), _fp8_roundtrip(bk))
        wv, bv = (_fp8_roundtrip(wv), _fp8_roundtrip(bv))
        return {'hidden_states': hidden_states, 'wq': wq, 'bq': bq, 'wk': wk, 'bk': bk, 'wv': wv, 'bv': bv, 'wl': wl, 'bl': bl}
    _L1_attn_all = _L1_attn_setup()
    _L1_attn_in = {k: v for k, v in _L1_attn_all.items() if k in ('wq', 'bq', 'wk', 'bk', 'wv', 'bv', 'wl', 'bl')}
    del _L1_attn_all

    def _L1_xattn_setup():
        import jax, jax.numpy as jnp
        import numpy as np
        B, Q, D = (8, 64, 512)
        CTX = 512
        H, KV, HD = (16, 4, 96)
        G = H // KV
        key = jax.random.key(seed)
        ks = jax.random.split(key, 6)
        s = 0.02
        return {'latents': jax.random.normal(ks[0], (B, Q, D), jnp.float32), 'context': jax.random.normal(ks[1], (B, CTX, D), jnp.float32), 'Wq': jax.random.normal(ks[2], (H * HD, D), jnp.float32) * s, 'Wk': jax.random.normal(ks[3], (KV * HD, D), jnp.float32) * s, 'Wv': jax.random.normal(ks[4], (KV * HD, D), jnp.float32) * s, 'Wo': jax.random.normal(ks[5], (D, H * HD), jnp.float32) * s}
    _L1_xattn_all = _L1_xattn_setup()
    _L1_xattn_in = {k: v for k, v in _L1_xattn_all.items() if k in ('Wq', 'Wk', 'Wv', 'Wo')}
    del _L1_xattn_all

    def _L1_ffn_setup():
        import jax, jax.numpy as jnp
        import numpy as np
        BATCH, TOK, DIM, OUT = (4, 256, 512, 512)
        E, R, TOP_K = (8, 16, 2)
        SCALING = 16.0 / R
        key = jax.random.key(seed)
        ks = jax.random.split(key, 6)
        return {'x': jax.random.normal(ks[0], (BATCH, TOK, DIM), dtype=jnp.float32), 'W_base': jax.random.normal(ks[1], (OUT, DIM), dtype=jnp.float32) / np.sqrt(DIM), 'b_base': jax.random.normal(ks[2], (OUT,), dtype=jnp.float32) * 0.01, 'W_gate': jax.random.normal(ks[3], (E, DIM), dtype=jnp.float32) * 0.01, 'A': jax.random.normal(ks[4], (E, R, DIM), dtype=jnp.float32) / np.sqrt(DIM), 'B': jax.random.normal(ks[5], (OUT, OUT // OUT * R * 0 + R), dtype=jnp.float32)[None].repeat(E, 0) * 0.0 + jax.random.normal(ks[5], (E, OUT, R), dtype=jnp.float32) * 0.02}
    _L1_ffn_all = _L1_ffn_setup()
    _L1_ffn_in = {k: v for k, v in _L1_ffn_all.items() if k in ('W_base', 'b_base', 'W_gate', 'A', 'B')}
    del _L1_ffn_all
    return {'x': x, 'ctx_4096': ctx_4096, 'mask_1x1xSxS2_ff0': mask_1x1xSxS2_ff0, 'L0_attn_Wq': _L0_attn_in['Wq'], 'L0_attn_bq': _L0_attn_in['bq'], 'L0_attn_Wk': _L0_attn_in['Wk'], 'L0_attn_bk': _L0_attn_in['bk'], 'L0_attn_Wv': _L0_attn_in['Wv'], 'L0_attn_bv': _L0_attn_in['bv'], 'L0_attn_Wo': _L0_attn_in['Wo'], 'L0_attn_bo': _L0_attn_in['bo'], 'L0_attn_gq': _L0_attn_in['gq'], 'L0_attn_gk': _L0_attn_in['gk'], 'L0_xattn_q_proj_w': _L0_xattn_in['q_proj_w'], 'L0_xattn_k_proj_w': _L0_xattn_in['k_proj_w'], 'L0_xattn_v_proj_w': _L0_xattn_in['v_proj_w'], 'L0_xattn_o_proj_w': _L0_xattn_in['o_proj_w'], 'L0_xattn_q_norm_w': _L0_xattn_in['q_norm_w'], 'L0_xattn_k_norm_w': _L0_xattn_in['k_norm_w'], 'L0_ffn_gate_w': _L0_ffn_in['gate_w'], 'L0_ffn_expert_w': _L0_ffn_in['expert_w'], 'L1_attn_wq': _L1_attn_in['wq'], 'L1_attn_bq': _L1_attn_in['bq'], 'L1_attn_wk': _L1_attn_in['wk'], 'L1_attn_bk': _L1_attn_in['bk'], 'L1_attn_wv': _L1_attn_in['wv'], 'L1_attn_bv': _L1_attn_in['bv'], 'L1_attn_wl': _L1_attn_in['wl'], 'L1_attn_bl': _L1_attn_in['bl'], 'L1_xattn_Wq': _L1_xattn_in['Wq'], 'L1_xattn_Wk': _L1_xattn_in['Wk'], 'L1_xattn_Wv': _L1_xattn_in['Wv'], 'L1_xattn_Wo': _L1_xattn_in['Wo'], 'L1_ffn_W_base': _L1_ffn_in['W_base'], 'L1_ffn_b_base': _L1_ffn_in['b_base'], 'L1_ffn_W_gate': _L1_ffn_in['W_gate'], 'L1_ffn_A': _L1_ffn_in['A'], 'L1_ffn_B': _L1_ffn_in['B']}

def reference(x, ctx_4096, mask_1x1xSxS2_ff0, L0_attn_Wq, L0_attn_bq, L0_attn_Wk, L0_attn_bk, L0_attn_Wv, L0_attn_bv, L0_attn_Wo, L0_attn_bo, L0_attn_gq, L0_attn_gk, L0_xattn_q_proj_w, L0_xattn_k_proj_w, L0_xattn_v_proj_w, L0_xattn_o_proj_w, L0_xattn_q_norm_w, L0_xattn_k_norm_w, L0_ffn_gate_w, L0_ffn_expert_w, L1_attn_wq, L1_attn_bq, L1_attn_wk, L1_attn_bk, L1_attn_wv, L1_attn_bv, L1_attn_wl, L1_attn_bl, L1_xattn_Wq, L1_xattn_Wk, L1_xattn_Wv, L1_xattn_Wo, L1_ffn_W_base, L1_ffn_b_base, L1_ffn_W_gate, L1_ffn_A, L1_ffn_B):
    import jax
    import jax.numpy as jnp

    def _L0_attn_ref(hidden_states, Wq, bq, Wk, bk, Wv, bv, Wo, bo, gq, gk):
        import jax, jax.numpy as jnp
        import numpy as np
        B, N, D = (2, 256, 512)
        H, HD = (32, 128)
        EPS = 1e-06

        def rmsnorm(x, w):
            xf = x.astype(jnp.float32)
            var = jnp.mean(xf * xf, axis=-1, keepdims=True)
            return (w * (xf * jax.lax.rsqrt(var + EPS))).astype(x.dtype)
        b, n, _ = hidden_states.shape
        q = (hidden_states @ Wq + bq).reshape(b, n, H, HD)
        k = (hidden_states @ Wk + bk).reshape(b, n, H, HD)
        v = (hidden_states @ Wv + bv).reshape(b, n, H, HD)
        q = rmsnorm(q, gq)
        k = rmsnorm(k, gk)
        scale = 1.0 / np.sqrt(HD)
        scores = jnp.einsum('bnhd,bmhd->bhnm', q, k) * scale
        attn = jax.nn.softmax(scores.astype(jnp.float32), axis=-1).astype(q.dtype)
        out = jnp.einsum('bhnm,bmhd->bnhd', attn, v).reshape(b, n, H * HD)
        return out @ Wo + bo

    def _L0_xattn_ref(hidden_states, cross_attention_states, attention_mask, q_proj_w, k_proj_w, v_proj_w, o_proj_w, q_norm_w, k_norm_w):
        import jax, jax.numpy as jnp
        import numpy as np
        NUM_HEADS = 32
        NUM_KV_HEADS = 8
        HEAD_DIM = 128
        HIDDEN = 512
        EPS = 1e-05

        def rmsnorm(x, w, eps=EPS):
            xf = x.astype(jnp.float32)
            var = jnp.mean(xf * xf, axis=-1, keepdims=True)
            return w * (xf * jax.lax.rsqrt(var + eps)).astype(x.dtype)
        B, Q, _ = hidden_states.shape
        KV = cross_attention_states.shape[1]
        n_rep = NUM_HEADS // NUM_KV_HEADS
        q = (hidden_states @ q_proj_w.T).reshape(B, Q, NUM_HEADS, HEAD_DIM).transpose(0, 2, 1, 3)
        k = (cross_attention_states @ k_proj_w.T).reshape(B, KV, NUM_KV_HEADS, HEAD_DIM).transpose(0, 2, 1, 3)
        v = (cross_attention_states @ v_proj_w.T).reshape(B, KV, NUM_KV_HEADS, HEAD_DIM).transpose(0, 2, 1, 3)
        q = rmsnorm(q, q_norm_w)
        k = jnp.repeat(k, n_rep, axis=1)
        v = jnp.repeat(v, n_rep, axis=1)
        k = rmsnorm(k, k_norm_w)
        scale = 1.0 / np.sqrt(HEAD_DIM)
        scores = jnp.einsum('bhqd,bhkd->bhqk', q, k) * scale + attention_mask
        attn = jax.nn.softmax(scores.astype(jnp.float32), axis=-1).astype(q.dtype)
        out = jnp.einsum('bhqk,bhkd->bhqd', attn, v)
        out = out.transpose(0, 2, 1, 3).reshape(B, Q, NUM_HEADS * HEAD_DIM)
        return out @ o_proj_w.T

    def _L0_ffn_ref(x, gate_w, expert_w):
        import jax, jax.numpy as jnp
        import numpy as np
        TOP_K = 2
        E = gate_w.shape[-1]
        logits = jnp.einsum('bsh,he->bse', x, gate_w)
        topv, topi = jax.lax.top_k(logits, TOP_K)
        w = jax.nn.softmax(topv, axis=-1)
        onehot = jax.nn.one_hot(topi, E, dtype=x.dtype)
        w_e = jnp.einsum('bske,bsk->bse', onehot, w)
        out = jnp.einsum('bsh,eho,bse->bso', x, expert_w, w_e)
        return out

    def _L1_attn_ref(hidden_states, wq, bq, wk, bk, wv, bv, wl, bl):
        import jax, jax.numpy as jnp
        import numpy as np
        HIDDEN = 512
        NUM_HEADS = 32
        HEAD_DIM = HIDDEN // NUM_HEADS

        def _fp8_roundtrip(x):
            return x.astype(jnp.float8_e4m3fn).astype(jnp.float32)
        B, S, E = hidden_states.shape
        H, D = (NUM_HEADS, HEAD_DIM)
        q = (hidden_states @ wq.T + bq).reshape(B, S, H, D)
        k = (hidden_states @ wk.T + bk).reshape(B, S, H, D)
        v = (hidden_states @ wv.T + bv).reshape(B, S, H, D)
        latent = hidden_states @ wl.T + bl
        scores = jnp.einsum('bshd,bstd->bsht', q, k) / np.sqrt(D).astype(np.float32)
        probs = jax.nn.softmax(scores, axis=-1)
        context = jnp.einsum('bsht,bstd->bshd', probs, v).reshape(B, S, E)
        return context

    def _L1_xattn_ref(latents, context, Wq, Wk, Wv, Wo):
        import jax, jax.numpy as jnp
        import numpy as np
        B, Q, D = (8, 64, 512)
        CTX = 512
        H, KV, HD = (16, 4, 96)
        G = H // KV
        b, q_len, _ = latents.shape
        hidden = jnp.concatenate([context, latents], axis=1)
        s_len = hidden.shape[1]
        q = (latents @ Wq.T).reshape(b, q_len, H, HD)
        k = (hidden @ Wk.T).reshape(b, s_len, KV, HD)
        v = (hidden @ Wv.T).reshape(b, s_len, KV, HD)
        q = q.transpose(0, 2, 1, 3).reshape(b, KV, G, q_len, HD)
        k = k.transpose(0, 2, 1, 3)
        v = v.transpose(0, 2, 1, 3)
        scale = 1.0 / jnp.sqrt(jnp.asarray(HD, q.dtype))
        scores = jnp.einsum('bkgqd,bksd->bkgqs', q, k) * scale
        attn = jax.nn.softmax(scores.astype(jnp.float32), axis=-1).astype(q.dtype)
        out = jnp.einsum('bkgqs,bksd->bkgqd', attn, v)
        out = out.reshape(b, H, q_len, HD).transpose(0, 2, 1, 3).reshape(b, q_len, H * HD)
        return out @ Wo.T

    def _L1_ffn_ref(x, W_base, b_base, W_gate, A, B):
        import jax, jax.numpy as jnp
        import numpy as np
        BATCH, TOK, DIM, OUT = (4, 256, 512, 512)
        E, R, TOP_K = (8, 16, 2)
        SCALING = 16.0 / R
        result = jnp.einsum('bnd,od->bno', x, W_base) + b_base
        logits = jnp.einsum('bnd,ed->bne', x, W_gate)
        probs = jax.nn.softmax(logits.astype(jnp.float32), axis=-1)
        top_p, top_i = jax.lax.top_k(probs, TOP_K)
        top_p = top_p / jnp.sum(top_p, axis=-1, keepdims=True)
        top_p = top_p.astype(x.dtype)
        route_w = jnp.sum(jax.nn.one_hot(top_i, E, dtype=x.dtype) * top_p[..., None], axis=-2)
        h = jnp.einsum('bnd,erd->bner', x, A)
        hw = h * route_w[..., None]
        delta = jnp.einsum('bner,eor->bno', hw, B)
        return result + delta * SCALING
    x = x + _L0_attn_ref(_layernorm(x, axis=-1), L0_attn_Wq, L0_attn_bq, L0_attn_Wk, L0_attn_bk, L0_attn_Wv, L0_attn_bv, L0_attn_Wo, L0_attn_bo, L0_attn_gq, L0_attn_gk)
    x = x + _L0_xattn_ref(_layernorm(x, axis=-1), ctx_4096, mask_1x1xSxS2_ff0, L0_xattn_q_proj_w, L0_xattn_k_proj_w, L0_xattn_v_proj_w, L0_xattn_o_proj_w, L0_xattn_q_norm_w, L0_xattn_k_norm_w)
    x = x + _L0_ffn_ref(_layernorm(x, axis=-1), L0_ffn_gate_w, L0_ffn_expert_w)
    x = x + _L1_attn_ref(_layernorm(x, axis=-1), L1_attn_wq, L1_attn_bq, L1_attn_wk, L1_attn_bk, L1_attn_wv, L1_attn_bv, L1_attn_wl, L1_attn_bl)
    x = x + _L1_xattn_ref(_layernorm(x, axis=-1), ctx_4096, L1_xattn_Wq, L1_xattn_Wk, L1_xattn_Wv, L1_xattn_Wo)
    x = x + _L1_ffn_ref(_layernorm(x, axis=-1), L1_ffn_W_base, L1_ffn_b_base, L1_ffn_W_gate, L1_ffn_A, L1_ffn_B)
    return x

_drawn_inputs = setup_inputs


def setup_inputs(seed=0):
    import zlib

    import numpy as np

    out = dict(_drawn_inputs(seed))
    spreads = {'L0_attn_gq': (1.0, 0.2),
     'L0_attn_gk': (1.0, 0.2),
     'L0_xattn_q_norm_w': (1.0, 0.2),
     'L0_xattn_k_norm_w': (1.0, 0.2)}
    factors = {'L0_attn_bq': 7.208,
     'L0_attn_bk': 64.0,
     'L0_attn_bo': 4.841,
     'L1_attn_wq': 6.593,
     'L1_attn_bq': 8.0,
     'L1_attn_wk': 6.289,
     'L1_attn_bk': 8.0,
     'L1_attn_bv': 8.0,
     'L1_xattn_Wq': 8.0,
     'L1_xattn_Wk': 8.0,
     'L1_ffn_b_base': 8.0,
     'L1_ffn_W_gate': 2.674}
    for name, (base, spread) in spreads.items():
        noise = np.random.default_rng([zlib.crc32(name.encode()), seed]).standard_normal(out[name].shape)
        drawn = base * np.exp(spread * noise) if base else spread * noise
        out[name] = jnp.asarray(drawn.astype(out[name].dtype))
    for name, factor in factors.items():
        out[name] = (out[name] * factor).astype(out[name].dtype)
    return out
```

```python
from contextlib import ExitStack

import concourse.bass as bass
from concourse import mybir

F32 = mybir.dt.float32
U32 = mybir.dt.uint32
ALU = mybir.AluOpType
ACT = mybir.ActivationFunctionType
AX = mybir.AxisListType
ds = bass.ds

P = 128
B, SEQ, D = 4, 256, 512
T = B * SEQ
TC = T // P
KC = D // P
CTX = 64
LN_EPS = 1e-5
QC = SEQ // P
HG = 4
RING = 2


class Core:

    def __init__(self, nc, ctx):
        self.nc = nc
        self.hold = ctx

        def sb(name, shape, dt=F32):
            return ctx.enter_context(nc.sbuf_tensor(name, shape, dt))

        self.x = sb("x_res", [P, TC, D])
        self.hT = sb("hT", [P, KC, T])
        self.ident = sb("ident", [P, P])
        self.neg_half = sb("neg_half", [P, 32])
        self.mv = sb("ln_mean_var", [P, TC, 2])
        self.stats = sb("ln_stats", [P, TC, 6])
        self.vareps = sb("ln_var_eps", [P, TC])
        self.rstd = sb("ln_rstd", [P, TC])
        self.h = sb("ln_h", [P, 2, D])
        self.norms = 0
        self.norm_sems = [ctx.enter_context(nc.semaphore(f"ln_{n}")) for n in
                          ("stats", "mean", "var_eps", "rstd", "h", "turned", "hT")]
        bank = lambda name: ctx.enter_context(nc.psum_tensor(name, [P, D], F32))
        self.proj = [bank(f"proj{i}") for i in range(RING)]
        self.score = [bank(f"score{i}") for i in range(RING)]
        self.turn = [bank(f"turn{i}") for i in range(RING)]
        self.outp = [bank(f"outp{i}") for i in range(RING)]


class Norm:

    def __init__(self, core, bias=None, bias_loaded=None):
        self.c = core
        self.bias, self.bias_loaded = bias, bias_loaded
        (self.stats_ready, self.mean_ready, self.var_eps_ready, self.rstd_ready, self.h_ready, self.turned,
         self.hT_ready) = core.norm_sems
        self.n0 = core.norms * TC
        self.hT_done = self.n0 + TC
        core.norms += 1

    def vector(self, dve):
        c = self.c
        for i in range(TC):
            dve.bn_stats(c.stats[:, i, :], c.x[:, i, :]).then_inc(self.stats_ready, 1)
            dve.wait_ge(self.stats_ready, self.n0 + i + 1)
            dve.bn_aggr(c.mv[:, i, :], c.stats[:, i, :]).then_inc(self.mean_ready, 1)
        for i in range(TC):
            dve.wait_ge(self.rstd_ready, self.n0 + i + 1)
            dve.wait_ge(self.mean_ready, self.n0 + i + 1)
            if i >= 2:
                dve.wait_ge(self.turned, self.n0 + i - 1)
            dve.tensor_scalar(c.h[:, i % 2, :], c.x[:, i, :], c.mv[:, i, 0:1], c.rstd[:, i:i + 1],
                              ALU.subtract, ALU.mult).then_inc(self.h_ready, 1)
            if self.bias is not None:
                if i == 0:
                    dve.wait_ge(self.bias_loaded, 16)
                dve.wait_ge(self.h_ready, self.n0 + i + 1)
                dve.tensor_tensor(c.x[:, i, :], c.x[:, i, :], self.bias, ALU.add)

    def gpsimd(self, pool):
        c = self.c
        for i in range(TC):
            pool.wait_ge(self.mean_ready, self.n0 + i + 1)
            pool.tensor_scalar(c.vareps[:, i:i + 1], c.mv[:, i, 1:2], LN_EPS, None, ALU.add)\
                .then_inc(self.var_eps_ready, 1)
            pool.wait_ge(self.var_eps_ready, self.n0 + i + 1)
            pool.tensor_tensor(c.rstd[:, i:i + 1], c.vareps[:, i:i + 1], c.neg_half[:, 0:1], ALU.pow)\
                .then_inc(self.rstd_ready, 1)

    def tensor(self, pe):
        c = self.c
        for i in range(TC):
            pe.wait_ge(self.h_ready, self.n0 + i + 1)
            if i >= 2:
                pe.wait_ge(self.hT_ready, self.n0 + i - 1)
            for k in range(KC):
                last = pe.transpose(c.turn[i % 2][:, k * P:(k + 1) * P], c.h[:, i % 2, k * P:(k + 1) * P],
                                    c.ident[:])
            last.then_inc(self.turned, 1)

    def scalar(self, act):
        c = self.c
        for i in range(TC):
            act.wait_ge(self.turned, self.n0 + i + 1)
            act.copy(c.hT[:, :, i * P:(i + 1) * P],
                     c.turn[i % 2][:].rearrange("p (k t) -> p k t", k=KC)).then_inc(self.hT_ready, 1)


class Attention:

    UNITS = HG * B * QC

    def __init__(self, core, ctx, name, dh, key_sizes, turn_base, proj_base, units=HG * B * QC):
        nc = core.nc
        self.c = core
        self.dh, self.key_sizes = dh, key_sizes
        self.keys = sum(key_sizes)
        self.turn_base, self.proj_base = turn_base, proj_base
        self.turn_uses = turn_base + units
        self.proj_uses = proj_base + TC
        sb = lambda n, shape: ctx.enter_context(nc.sbuf_tensor(f"{name}_{n}", shape, F32))
        sem = lambda n: core.hold.enter_context(nc.semaphore(f"{name}_{n}"))
        self.qT = sb("qT", [dh, HG, T])
        self.outT = sb("outT", [dh, HG, T])
        self.probs = sb("probs", [P, 4, self.keys])
        self.nmax = sb("nmax", [P, 4])
        self.sums = sb("sums", [P, 4])
        self.rsum = sb("rsum", [P, 4])
        self.probsT = sb("probsT", [P, 2, len(key_sizes), SEQ])
        self.wo = sb("wo", [dh, HG, D])
        self.proj_ready = sem("proj_ready")
        self.proj_free = sem("proj_free")
        self.turn_ready = sem("turn_ready")
        self.turn_free = sem("turn_free")
        self.score_ready = sem("score_ready")
        self.score_free = sem("score_free")
        self.max_ready = sem("max_ready")
        self.rsum_ready = sem("rsum_ready")
        self.probs_ready = sem("probs_ready")
        self.outp_ready = sem("outp_ready")
        self.outp_free = sem("outp_free")
        self.wo_loaded = sem("wo_loaded")

    def unit(self, s):
        return s // (B * QC), s // QC % B, s % QC

    def tensor(self, pe, g, kT, v):
        c = self.c
        for s in range(self.UNITS + 4):
            if s < self.UNITS:
                h, b, qc = self.unit(s)
                pe.wait_ge(self.score_free, g * self.UNITS + s + 1)
                t0 = b * SEQ + qc * P
                pe.matmul(c.score[s % 2][:, 0:self.keys], self.qT[:, h, t0:t0 + P], kT(h, b),
                          start=True, stop=True).then_inc(self.score_ready, 1)
            if s >= 2 and s - 2 < self.UNITS:
                r = s - 2
                pe.wait_ge(self.probs_ready, g * self.UNITS + r + 1)
                pe.wait_ge(self.turn_free, g * self.turn_uses + self.turn_base + r + 1)
                k0 = 0
                for k, n in enumerate(self.key_sizes):
                    last = pe.transpose(c.turn[r % 2][0:n, k * P:(k + 1) * P],
                                        self.probs[:, r % 4, k0:k0 + n], c.ident[:])
                    k0 += n
                last.then_inc(self.turn_ready, 1)
            if s >= 4 and s % 2 == 0 and (s - 4) // 2 < self.UNITS // 2:
                u = (s - 4) // 2
                h, b, _ = self.unit(2 * u)
                pe.wait_ge(self.turn_free, g * self.turn_uses + self.turn_base + 2 * u + 4)
                pe.wait_ge(self.outp_free, g * (self.UNITS // 2) + u + 1)
                for k, n in enumerate(self.key_sizes):
                    last = pe.matmul(c.outp[u % 2][0:self.dh, 0:SEQ], v(h, b, k),
                                     self.probsT[0:n, u % 2, k, :],
                                     start=(k == 0), stop=(k == len(self.key_sizes) - 1))
                last.then_inc(self.outp_ready, 1)
        pe.wait_ge(self.outp_free, (g + 1) * (self.UNITS // 2) + 2)
        self.project(pe, g)

    def project(self, pe, g):
        c = self.c
        pe.wait_ge(self.wo_loaded, g * 16 + 16)
        for i in range(TC):
            pe.wait_ge(self.proj_free, g * self.proj_uses + self.proj_base + i + 1)
            for h in range(HG):
                last = pe.matmul(c.proj[(self.proj_base + i) % 2][:, :],
                                 self.outT[:, h, i * P:(i + 1) * P], self.wo[:, h, :],
                                 start=(h == 0), stop=(h == HG - 1))
            last.then_inc(self.proj_ready, 1)

    def vector(self, dve, g):
        c = self.c
        for s in range(self.UNITS + 4):
            if s < self.UNITS:
                dve.wait_ge(self.score_ready, g * self.UNITS + s + 1)
                dve.tensor_reduce(self.nmax[:, s % 4:s % 4 + 1], c.score[s % 2][:, 0:self.keys],
                                  AX.X, ALU.max, negate=True).then_inc(self.max_ready, 1)
            if s >= 1 and s - 1 < self.UNITS:
                r = s - 1
                dve.wait_ge(self.score_free, g * self.UNITS + r + 3)
                dve.reciprocal(self.rsum[:, r % 4:r % 4 + 1], self.sums[:, r % 4:r % 4 + 1])\
                    .then_inc(self.rsum_ready, 1)
                dve.wait_ge(self.rsum_ready, g * self.UNITS + r + 1)
                dve.tensor_scalar(self.probs[:, r % 4, :], self.probs[:, r % 4, :],
                                  self.rsum[:, r % 4:r % 4 + 1], None, ALU.mult)\
                    .then_inc(self.probs_ready, 1)
            if s >= 5 and s % 2 == 1:
                u = (s - 5) // 2
                h, b, _ = self.unit(2 * u)
                dve.wait_ge(self.outp_ready, g * (self.UNITS // 2) + u + 1)
                dve.tensor_copy(self.outT[:, h, b * SEQ:(b + 1) * SEQ],
                                c.outp[u % 2][0:self.dh, 0:SEQ]).then_inc(self.outp_free, 1)
        self.add_to_x(dve, g)

    def add_to_x(self, dve, g):
        c = self.c
        for i in range(TC):
            dve.wait_ge(self.proj_ready, g * self.proj_uses + self.proj_base + i + 1)
            dve.tensor_tensor(c.x[:, i, :], c.proj[(self.proj_base + i) % 2][:, :], c.x[:, i, :],
                              ALU.add).then_inc(self.proj_free, 1)

    def scalar(self, act, g):
        c = self.c
        for s in range(self.UNITS + 2):
            if s < self.UNITS:
                act.wait_ge(self.max_ready, g * self.UNITS + s + 1)
                act.activation(self.probs[:, s % 4, :], c.score[s % 2][:, 0:self.keys], ACT.Exp,
                               bias=self.nmax[:, s % 4:s % 4 + 1],
                               accum_out=self.sums[:, s % 4:s % 4 + 1]).then_inc(self.score_free, 1)
            if s >= 2:
                r = s - 2
                qc = r % QC
                u = r // QC
                act.wait_ge(self.turn_ready, g * self.turn_uses + self.turn_base + r + 1)
                full = sum(1 for n in self.key_sizes if n == P)
                copies = [(P, 0, full)] if full else []
                if self.key_sizes[-1] < P:
                    copies.append((self.key_sizes[-1], len(self.key_sizes) - 1, len(self.key_sizes)))
                for n, k0, k1 in copies:
                    last = act.copy(self.probsT[0:n, u % 2, k0:k1, qc * P:(qc + 1) * P],
                                    c.turn[r % 2][0:n, k0 * P:k1 * P].rearrange("p (k t) -> p k t", t=P))
                last.then_inc(self.turn_free, 1)


class ContextAttention(Attention):

    ROWS = B * QC

    def __init__(self, core, ctx, name, turn_base, proj_base):
        super().__init__(core, ctx, name, P, [CTX], turn_base, proj_base, units=HG)
        sb = lambda n, shape: ctx.enter_context(core.nc.sbuf_tensor(f"{name}_{n}", shape, F32))
        sem = lambda n: core.hold.enter_context(core.nc.semaphore(f"{name}_{n}"))
        self.mask = sb("mask", [P, B // 2, QC, 2, CTX])
        self.logits = sb("logits", [P, 2, self.ROWS * CTX])
        self.exps = sb("exps", [P, 2, self.ROWS * CTX])
        self.top = sb("top", [P, 2, self.ROWS])
        self.total = sb("total", [P, 2, self.ROWS])
        self.turned = sb("turned", [P, 2, B // 2, SEQ])
        self.mask_loaded = sem("mask_loaded")
        self.logits_ready = sem("logits_ready")
        self.shifted_ready = sem("shifted_ready")
        self.exps_ready = sem("exps_ready")
        self.total_ready = sem("total_ready")

    def tensor(self, pe, g, kT, v):
        c = self.c
        for h in range(HG + 2):
            if h < HG:
                pe.wait_ge(self.score_free, g * HG + h + 1)
                for b in range(B):
                    for qc in range(QC):
                        t0 = b * SEQ + qc * P
                        at = ((b // 2 * QC + qc) * 2 + b % 2) * CTX
                        last = pe.matmul(c.score[h % 2][:, at:at + CTX], self.qT[:, h, t0:t0 + P], kT(b),
                                         start=True, stop=True)
                last.then_inc(self.score_ready, 1)
            if h >= 1 and h - 1 < HG:
                r = h - 1
                pe.wait_ge(self.probs_ready, g * HG + r + 1)
                pe.wait_ge(self.turn_free, g * self.turn_uses + self.turn_base + r + 1)
                for a in range(B // 2 * QC):
                    last = pe.transpose(c.turn[r % 2][:, a * P:(a + 1) * P],
                                        self.exps[:, r % 2, a * P:(a + 1) * P], c.ident[:])
                last.then_inc(self.turn_ready, 1)
            if h >= 2:
                r = h - 2
                pe.wait_ge(self.turn_free, g * self.turn_uses + self.turn_base + r + 3)
                pe.wait_ge(self.outp_free, g * HG + r + 1)
                for b in range(B):
                    rows = slice(b % 2 * CTX, (b % 2 + 1) * CTX)
                    last = pe.matmul(c.outp[b % 2][:, b // 2 * SEQ:(b // 2 + 1) * SEQ], v(b),
                                     self.turned[rows, r % 2, b // 2, :], start=True, stop=True)
                last.then_inc(self.outp_ready, 1)
        pe.wait_ge(self.outp_free, (g + 1) * HG + 1)
        self.project(pe, g)

    def vector(self, dve, g):
        c = self.c
        rows = lambda a: a.rearrange("p (r k) -> p r k", k=CTX)
        each = lambda a: a.unsqueeze(2).broadcast_to([P, self.ROWS, CTX])
        for h in range(HG + 1):
            if h < HG:
                s = h % 2
                dve.wait_ge(self.score_ready, g * HG + h + 1)
                dve.tensor_tensor(self.logits[:, s, :], c.score[s][:, :],
                                  self.mask[:].rearrange("p a q b k -> p (a q b k)"), ALU.add)\
                    .then_inc(self.score_free, 1)
                dve.wait_ge(self.score_free, g * HG + h + 1 + RING)
                dve.tensor_reduce(self.top[:, s, :], rows(self.logits[:, s, :]), AX.X, ALU.max)\
                    .then_inc(self.max_ready, 1)
                dve.wait_ge(self.max_ready, g * HG + h + 1)
                dve.tensor_tensor(rows(self.logits[:, s, :]), rows(self.logits[:, s, :]),
                                  each(self.top[:, s, :]), ALU.subtract).then_inc(self.shifted_ready, 1)
            if h >= 1:
                r = h - 1
                s = r % 2
                dve.wait_ge(self.exps_ready, g * HG + r + 1)
                dve.tensor_reduce(self.total[:, s, :], rows(self.exps[:, s, :]), AX.X, ALU.add)\
                    .then_inc(self.total_ready, 1)
                dve.wait_ge(self.total_ready, g * HG + r + 1)
                dve.reciprocal(self.total[:, s, :], self.total[:, s, :]).then_inc(self.rsum_ready, 1)
                dve.wait_ge(self.rsum_ready, g * HG + r + 1)
                dve.tensor_tensor(rows(self.exps[:, s, :]), rows(self.exps[:, s, :]),
                                  each(self.total[:, s, :]), ALU.mult).then_inc(self.probs_ready, 1)
        self.add_to_x(dve, g)

    def scalar(self, act, g):
        c = self.c
        for h in range(HG + 2):
            if h < HG:
                act.wait_ge(self.shifted_ready, g * HG + h + 1)
                act.activation(self.exps[:, h % 2, :], self.logits[:, h % 2, :], ACT.Exp)\
                    .then_inc(self.exps_ready, 1)
            if h >= 1 and h - 1 < HG:
                r = h - 1
                act.wait_ge(self.turn_ready, g * self.turn_uses + self.turn_base + r + 1)
                act.copy(self.turned[:, r % 2, :, :].rearrange("p a q -> p (a q)"), c.turn[r % 2][:, :])\
                    .then_inc(self.turn_free, 1)
            if h >= 2:
                r = h - 2
                act.wait_ge(self.outp_ready, g * HG + r + 1)
                outT = self.outT[:, r, :].rearrange("p (a b t) -> p a b t", a=B // 2, b=2)
                for b in range(2):
                    last = act.copy(outT[:, :, b, :], c.outp[b][:, :].rearrange("p (a t) -> p a t", t=SEQ))
                last.then_inc(self.outp_free, 1)


def self_attention(nc, core, io, name, eps):
    GROUPS = 8
    W = HG * P
    NTURN, NPROJ = 2 * TC, 3 * TC
    with ExitStack() as ctx:
        sb = lambda n, shape: ctx.enter_context(nc.sbuf_tensor(f"{name}_{n}", shape, F32))
        sem = lambda n: core.hold.enter_context(nc.semaphore(f"{name}_{n}"))
        wqkv = sb("wqkv", [P, 3, KC, W])
        bias = sb("bias", [P, 3, W])
        bo = sb("bo", [P, D])
        gains = sb("gains", [P, 2])
        gain = sb("gain", [P, 1])
        qk = sb("qk", [P, 4, 2 * W])
        sq = sb("sq", [P, 2, 2 * W])
        ss = sb("ss", [P, 2, 2 * HG])
        ms = sb("ms", [P, 2, 2 * HG])
        rms = sb("rms", [P, 2, 2 * HG])
        epsilon = sb("epsilon", [P, 2 * HG])
        kT = sb("kT", [P, HG, T])
        v = sb("v", [P, TC, W])

        x_loaded = sem("x_loaded")
        const_ready = sem("const_ready")
        bo_loaded = sem("bo_loaded")
        gain_loaded = sem("gain_loaded")
        gain_ready = sem("gain_ready")
        w_loaded = [sem(f"w{n}_loaded") for n in "qkv"]
        bias_loaded = sem("bias_loaded")
        qk_ready = sem("qk_ready")
        sq_ready = sem("sq_ready")
        ss_ready = sem("ss_ready")
        ms_ready = sem("ms_ready")
        rms_ready = sem("rms_ready")
        qk_normed = sem("qk_normed")

        norm = Norm(core, bo[:, :], bo_loaded)
        att = Attention(core, ctx, name, P, [P, P], NTURN, NPROJ)
        w_dram = [io[n].rearrange("(k p) n -> p k n", p=P) for n in ("L0_attn_Wq", "L0_attn_Wk", "L0_attn_Wv")]
        b_dram = [io[n].partition_broadcast(P) for n in ("L0_attn_bq", "L0_attn_bk", "L0_attn_bv")]
        wo_dram = io["L0_attn_Wo"].rearrange("(n p) d -> p n d", p=P)

        with nc.Block() as block:

            @block.sync
            def _(sp):
                def load_w(g):
                    for j in range(3):
                        sp.dma_start(wqkv[:, j, :, :], w_dram[j][:, :, ds(g * W, W)]).then_inc(w_loaded[j], 16)
                    for j in range(3):
                        sp.dma_start(bias[:, j, :], b_dram[j][:, ds(g * W, W)]).then_inc(bias_loaded, 16)

                sp.dma_start(core.x[:], io["x"].rearrange("(c p) d -> p c d", p=P)).then_inc(x_loaded, 16)
                sp.dma_start(core.ident[:], io["ident"]).then_inc(x_loaded, 16)
                sp.dma_start(bo[:], io["L0_attn_bo"].partition_broadcast(P)).then_inc(bo_loaded, 16)
                sp.dma_start(gains[:, 0:1], io["L0_attn_gq"].unsqueeze(1)).then_inc(gain_loaded, 16)
                sp.dma_start(gains[:, 1:2], io["L0_attn_gk"].unsqueeze(1)).then_inc(gain_loaded, 16)
                load_w(0)
                sp.dma_start(att.wo[:], wo_dram[:, 0:HG, :]).then_inc(att.wo_loaded, 16)
                with sp.Fori(1, GROUPS) as g:
                    sp.wait_ge(att.proj_free, (g - 1) * att.proj_uses + NPROJ + RING)
                    load_w(g)
                    sp.wait_ge(att.proj_ready, g * att.proj_uses)
                    sp.dma_start(att.wo[:], wo_dram[:, ds(g * HG, HG), :]).then_inc(att.wo_loaded, 16)

            @block.gpsimd
            def _(pool):
                pool.memset(core.neg_half[:], -0.5).then_inc(const_ready, 1)
                pool.memset(epsilon[:], eps).then_inc(const_ready, 1)
                pool.wait_ge(const_ready, 2)
                norm.gpsimd(pool)
                with pool.Fori(0, GROUPS) as g:
                    for i in range(TC):
                        pool.wait_ge(ss_ready, g * TC + i + 1)
                        pool.tensor_tensor(ms[:, i % 2, :], ss[:, i % 2, :], epsilon[:], ALU.add)\
                            .then_inc(ms_ready, 1)
                        pool.wait_ge(ms_ready, g * TC + i + 1)
                        pool.tensor_tensor(rms[:, i % 2, :], ms[:, i % 2, :], core.neg_half[:, 0:2 * HG],
                                           ALU.pow).then_inc(rms_ready, 1)

            @block.vector
            def _(dve):
                dve.wait_ge(x_loaded, 32)
                dve.sem_inc(att.proj_free, RING)
                dve.sem_inc(att.outp_free, RING)
                norm.vector(dve)
                dve.wait_ge(gain_loaded, 32)
                dve.scalar_tensor_tensor(gain[:], gains[:, 0:1], float(P) ** -0.5, gains[:, 1:2],
                                         ALU.mult, ALU.mult).then_inc(gain_ready, 1)

                def normalise(g, i):
                    dve.wait_ge(rms_ready, g * TC + i + 1)
                    t = qk[:, i % 4, :].rearrange("p (h d) -> p h d", d=P)
                    dve.tensor_tensor(t, t, rms[:, i % 2, :].unsqueeze(2).broadcast_to([P, 2 * HG, P]),
                                      ALU.mult).then_inc(qk_normed, 1)

                with dve.Fori(0, GROUPS) as g:
                    dve.wait_ge(bias_loaded, g * 48 + 48)
                    for i in range(TC):
                        for j in range(3):
                            n = 3 * i + j
                            dve.wait_ge(att.proj_ready, g * att.proj_uses + n + 1)
                            dst = qk[:, i % 4, j * W:(j + 1) * W] if j < 2 else v[:, i, :]
                            ins = dve.tensor_tensor(dst, core.proj[n % 2][:, :], bias[:, j, :], ALU.add)
                            ins.then_inc(att.proj_free, 1)
                        dve.wait_ge(sq_ready, g * TC + i + 1)
                        dve.tensor_reduce(ss[:, i % 2, :], sq[:, i % 2, :].rearrange("p (h d) -> p h d", d=P),
                                          AX.X, ALU.add).then_inc(ss_ready, 1)
                        if i >= 1:
                            normalise(g, i - 1)
                    normalise(g, TC - 1)
                    att.vector(dve, g)

            @block.scalar
            def _(act):
                act.sem_inc(att.turn_free, RING)
                act.sem_inc(att.score_free, RING)
                norm.scalar(act)
                act.wait_ge(gain_ready, 1)

                def turn_out(g, i):
                    for j in range(2):
                        n = 2 * i + j
                        act.wait_ge(att.turn_ready, g * att.turn_uses + n + 1)
                        src = core.turn[n % 2][:, :].rearrange("p (h t) -> p h t", t=P)
                        if j == 0:
                            ins = act.activation(att.qT[:, :, i * P:(i + 1) * P], src, ACT.Copy, scale=gain[:, 0:1])
                        else:
                            ins = act.copy(kT[:, :, i * P:(i + 1) * P], src)
                        ins.then_inc(att.turn_free, 1)

                with act.Fori(0, GROUPS) as g:
                    for i in range(TC + 2):
                        if i < TC:
                            act.wait_ge(att.proj_free, g * att.proj_uses + 3 * i + 2 + RING)
                            act.activation(sq[:, i % 2, :], qk[:, i % 4, :], ACT.Square, scale=float(P) ** -0.5)\
                                .then_inc(sq_ready, 1)
                        if i >= 2:
                            turn_out(g, i - 2)
                    att.scalar(act, g)

            @block.tensor
            def _(pe):
                norm.tensor(pe)
                pe.wait_ge(norm.hT_ready, norm.hT_done)

                def turn(g, i):
                    pe.wait_ge(qk_normed, g * TC + i + 1)
                    for j in range(2):
                        n = 2 * i + j
                        pe.wait_ge(att.turn_free, g * att.turn_uses + n + 1)
                        for h in range(HG):
                            last = pe.transpose(core.turn[n % 2][:, h * P:(h + 1) * P],
                                                qk[:, i % 4, j * W + h * P:j * W + (h + 1) * P], core.ident[:])
                        last.then_inc(att.turn_ready, 1)

                with pe.Fori(0, GROUPS) as g:
                    for i in range(TC + 2):
                        if i < TC:
                            for j in range(3):
                                n = 3 * i + j
                                if i == 0:
                                    pe.wait_ge(w_loaded[j], g * 16 + 16)
                                pe.wait_ge(att.proj_free, g * att.proj_uses + n + 1)
                                for k in range(KC):
                                    last = pe.matmul(core.proj[n % 2][:, :], core.hT[:, k, i * P:(i + 1) * P],
                                                     wqkv[:, j, k, :], start=(k == 0), stop=(k == KC - 1))
                                last.then_inc(att.proj_ready, 1)
                        if i >= 2:
                            turn(g, i - 2)
                    pe.wait_ge(att.turn_free, g * att.turn_uses + NTURN + RING)
                    pe.wait_ge(att.proj_free, g * att.proj_uses + NPROJ + RING)
                    att.tensor(pe, g, lambda h, b: kT[:, h, b * SEQ:(b + 1) * SEQ],
                               lambda h, b, k: v[:, QC * b + k, h * P:(h + 1) * P])


def context_attention(nc, core, io, name, eps):
    GROUPS = 8
    W = HG * P
    ITEMS = 1 + TC
    KCH = B * CTX // P
    NTURN, NPROJ = KCH + TC, 2 + TC
    with ExitStack() as ctx:
        sb = lambda n, shape: ctx.enter_context(nc.sbuf_tensor(f"{name}_{n}", shape, F32))
        sem = lambda n: core.hold.enter_context(nc.semaphore(f"{name}_{n}"))
        wq = sb("wq", [P, KC, W])
        wkv = sb("wkv", [P, 2, KC, P])
        ctxT = sb("ctxT", [P, KC, B * CTX])
        gains = sb("gains", [P, 2])
        gain = sb("gain", [P, 1])
        epsilon = sb("epsilon", [P, HG])
        tok = sb("tok", [P, 3, W])
        sq = sb("sq", [P, 3, W])
        ss = sb("ss", [P, 3, HG])
        ms = sb("ms", [P, 3, HG])
        rms = sb("rms", [P, 3, HG])
        kT = sb("kT", [P, B * CTX])
        v = sb("v", [P, KCH, P])

        ctx_loaded = sem("ctx_loaded")
        gain_loaded = sem("gain_loaded")
        const_ready = sem("const_ready")
        gain_ready = sem("gain_ready")
        wq_loaded = sem("wq_loaded")
        wkv_loaded = sem("wkv_loaded")
        sq_ready = sem("sq_ready")
        ss_ready = sem("ss_ready")
        ms_ready = sem("ms_ready")
        rms_ready = sem("rms_ready")
        normed = sem("normed")

        norm = Norm(core)
        att = ContextAttention(core, ctx, name, NTURN, NPROJ)
        wq_dram = io["L0_xattn_q"].rearrange("(k p) n -> p k n", p=P)
        wk_dram = io["L0_xattn_k"].rearrange("(k p) n -> p k n", p=P)
        wv_dram = io["L0_xattn_v"].rearrange("(k p) n -> p k n", p=P)
        wo_dram = io["L0_xattn_o"].rearrange("(n p) d -> p n d", p=P)

        width = lambda n: KCH * P if n == 0 else W

        with nc.Block() as block:

            @block.sync
            def _(sp):
                def load_w(g):
                    sp.dma_start(wkv[:, 0, :, :], wk_dram[:, :, ds(g * P, P)]).then_inc(wkv_loaded, 16)
                    sp.dma_start(wkv[:, 1, :, :], wv_dram[:, :, ds(g * P, P)]).then_inc(wkv_loaded, 16)
                    sp.dma_start(wq[:], wq_dram[:, :, ds(g * W, W)]).then_inc(wq_loaded, 16)

                sp.dma_start(ctxT[:], io["ctxT"].rearrange("(k p) n -> p k n", p=P)).then_inc(ctx_loaded, 16)
                load_w(0)
                sp.dma_start(att.wo[:], wo_dram[:, 0:HG, :]).then_inc(att.wo_loaded, 16)
                sp.dma_start(gains[:, 0:1], io["L0_xattn_gq"].unsqueeze(1)).then_inc(gain_loaded, 16)
                sp.dma_start(gains[:, 1:2], io["L0_xattn_gk"].unsqueeze(1)).then_inc(gain_loaded, 16)
                for a in range(B // 2):
                    for b in range(2):
                        sp.dma_start(att.mask[:, a, :, b, :], io["mask"].rearrange("(c p) k -> p c k", p=P))\
                            .then_inc(att.mask_loaded, 16)
                with sp.Fori(1, GROUPS) as g:
                    sp.wait_ge(att.proj_free, (g - 1) * att.proj_uses + NPROJ + RING)
                    load_w(g)
                    sp.wait_ge(att.proj_ready, g * att.proj_uses)
                    sp.dma_start(att.wo[:], wo_dram[:, ds(g * HG, HG), :]).then_inc(att.wo_loaded, 16)

            @block.gpsimd
            def _(pool):
                pool.memset(epsilon[:], eps).then_inc(const_ready, 1)
                pool.wait_ge(const_ready, 1)
                norm.gpsimd(pool)
                with pool.Fori(0, GROUPS) as g:
                    for n in range(ITEMS):
                        hs = width(n) // P
                        pool.wait_ge(ss_ready, g * ITEMS + n + 1)
                        pool.tensor_tensor(ms[:, n % 3, 0:hs], ss[:, n % 3, 0:hs], epsilon[:, 0:hs], ALU.add)\
                            .then_inc(ms_ready, 1)
                        pool.wait_ge(ms_ready, g * ITEMS + n + 1)
                        pool.tensor_tensor(rms[:, n % 3, 0:hs], ms[:, n % 3, 0:hs], core.neg_half[:, 0:hs],
                                           ALU.pow).then_inc(rms_ready, 1)

            @block.vector
            def _(dve):
                dve.sem_inc(att.proj_free, RING)
                dve.sem_inc(att.score_free, RING)
                norm.vector(dve)
                dve.wait_ge(gain_loaded, 32)
                dve.scalar_tensor_tensor(gain[:], gains[:, 0:1], float(P) ** -0.5, gains[:, 1:2],
                                         ALU.mult, ALU.mult).then_inc(gain_ready, 1)
                dve.wait_ge(att.mask_loaded, 16 * B)

                def normalise(g, n):
                    hs = width(n) // P
                    dve.wait_ge(rms_ready, g * ITEMS + n + 1)
                    t = tok[:, n % 3, 0:hs * P].rearrange("p (h d) -> p h d", d=P)
                    dve.tensor_tensor(t, t, rms[:, n % 3, 0:hs].unsqueeze(2).broadcast_to([P, hs, P]),
                                      ALU.mult).then_inc(normed, 1)

                with dve.Fori(0, GROUPS) as g:
                    for n in range(ITEMS):
                        hs = width(n) // P
                        use = 0 if n == 0 else n + 1
                        dve.wait_ge(att.proj_ready, g * att.proj_uses + use + 1)
                        dve.tensor_copy(tok[:, n % 3, 0:hs * P], core.proj[use % 2][:, 0:hs * P])\
                            .then_inc(att.proj_free, 1)
                        if n == 0:
                            dve.wait_ge(att.proj_ready, g * att.proj_uses + 2)
                            dve.tensor_copy(v[:], core.proj[1][:, 0:KCH * P].rearrange("p (c d) -> p c d", d=P))\
                                .then_inc(att.proj_free, 1)
                        dve.wait_ge(sq_ready, g * ITEMS + n + 1)
                        dve.tensor_reduce(ss[:, n % 3, 0:hs], sq[:, n % 3, 0:hs * P].rearrange("p (h d) -> p h d", d=P),
                                          AX.X, ALU.add).then_inc(ss_ready, 1)
                        if n >= 1:
                            normalise(g, n - 1)
                    normalise(g, ITEMS - 1)
                    att.vector(dve, g)

            @block.scalar
            def _(act):
                act.sem_inc(att.turn_free, RING)
                act.sem_inc(att.outp_free, 1)
                norm.scalar(act)
                act.wait_ge(gain_ready, 1)

                def turn_out(g, n):
                    for use in ([0, 1] if n == 0 else [n + 1]):
                        act.wait_ge(att.turn_ready, g * att.turn_uses + use + 1)
                        if n == 0:
                            ins = act.copy(kT[:, use * P:(use + 1) * P], core.turn[use % 2][:, 0:P])
                        else:
                            src = core.turn[use % 2][:, :].rearrange("p (h t) -> p h t", t=P)
                            ins = act.activation(att.qT[:, :, (n - 1) * P:n * P], src, ACT.Copy, scale=gain[:, 0:1])
                        ins.then_inc(att.turn_free, 1)

                with act.Fori(0, GROUPS) as g:
                    for n in range(ITEMS + 2):
                        if n < ITEMS:
                            use = 0 if n == 0 else n + 1
                            act.wait_ge(att.proj_free, g * att.proj_uses + use + 1 + RING)
                            act.activation(sq[:, n % 3, 0:width(n)], tok[:, n % 3, 0:width(n)], ACT.Square,
                                           scale=float(P) ** -0.5).then_inc(sq_ready, 1)
                        if n >= 2:
                            turn_out(g, n - 2)
                    att.scalar(act, g)

            @block.tensor
            def _(pe):
                norm.tensor(pe)
                pe.wait_ge(norm.hT_ready, norm.hT_done)
                pe.wait_ge(ctx_loaded, 16)

                def turn(g, n):
                    pe.wait_ge(normed, g * ITEMS + n + 1)
                    for use in ([0, 1] if n == 0 else [n + 1]):
                        pe.wait_ge(att.turn_free, g * att.turn_uses + use + 1)
                        for h in ([use] if n == 0 else range(HG)):
                            at = 0 if n == 0 else h * P
                            last = pe.transpose(core.turn[use % 2][:, at:at + P],
                                                tok[:, n % 3, h * P:(h + 1) * P], core.ident[:])
                        last.then_inc(att.turn_ready, 1)

                with pe.Fori(0, GROUPS) as g:
                    for n in range(ITEMS + 2):
                        if n == 0:
                            pe.wait_ge(wkv_loaded, g * 32 + 32)
                            for j in range(2):
                                pe.wait_ge(att.proj_free, g * att.proj_uses + j + 1)
                                for i in range(KCH):
                                    for k in range(KC):
                                        last = pe.matmul(core.proj[j][:, i * P:(i + 1) * P],
                                                         ctxT[:, k, i * P:(i + 1) * P], wkv[:, j, k, :],
                                                         start=(k == 0), stop=(k == KC - 1))
                                last.then_inc(att.proj_ready, 1)
                        elif n < ITEMS:
                            i = n - 1
                            if i == 0:
                                pe.wait_ge(wq_loaded, g * 16 + 16)
                            pe.wait_ge(att.proj_free, g * att.proj_uses + n + 2)
                            for k in range(KC):
                                last = pe.matmul(core.proj[(n + 1) % 2][:, :], core.hT[:, k, i * P:(i + 1) * P],
                                                 wq[:, k, :], start=(k == 0), stop=(k == KC - 1))
                            last.then_inc(att.proj_ready, 1)
                        if n >= 2:
                            turn(g, n - 2)
                    pe.wait_ge(att.turn_free, g * att.turn_uses + NTURN + RING)
                    pe.wait_ge(att.proj_free, g * att.proj_uses + NPROJ + RING)
                    att.tensor(pe, g, lambda b: kT[:, b * CTX:(b + 1) * CTX],
                               lambda b: v[b % 2 * CTX:(b % 2 + 1) * CTX, b // 2, :])


def latent_attention(nc, core, io, name):
    GROUPS, DH = 4, 96
    KEYS = SEQ + CTX
    VPACK = 4
    NTURN = 0
    HALVES = T // D
    NPROJ = HG * HALVES + HALVES + 1 + TC // VPACK + 1
    with ExitStack() as ctx:
        sb = lambda n, shape: ctx.enter_context(nc.sbuf_tensor(f"{name}_{n}", shape, F32))
        sem = lambda n: core.hold.enter_context(nc.semaphore(f"{name}_{n}"))
        wq = sb("wq", [P, KC, HG * DH])
        wkv = sb("wkv", [P, 2, KC, DH])
        ctxT = sb("ctxT", [P, KC, B * CTX])
        kT = sb("kT", [DH, B, KEYS])
        v = sb("v", [P, TC, DH])
        vc = sb("vc", [CTX, B, DH])

        w_loaded = sem("w_loaded")
        ctx_loaded = sem("ctx_loaded")

        norm = Norm(core)
        att = Attention(core, ctx, name, DH, [P, P, CTX], NTURN, NPROJ)
        wq_dram = io["L1_xattn_q"].rearrange("(k p) n -> p k n", p=P)
        wk_dram = io["L1_xattn_k"].rearrange("(k p) n -> p k n", p=P)
        wv_dram = io["L1_xattn_v"].rearrange("(k p) n -> p k n", p=P)
        wo_dram = io["L1_xattn_o"].rearrange("(n p) d -> p n d", p=DH)

        with nc.Block() as block:

            @block.sync
            def _(sp):
                def load_w(g):
                    sp.dma_start(wkv[:, 0, :, :], wk_dram[:, :, ds(g * DH, DH)]).then_inc(w_loaded, 16)
                    sp.dma_start(wkv[:, 1, :, :], wv_dram[:, :, ds(g * DH, DH)]).then_inc(w_loaded, 16)
                    sp.dma_start(wq[:], wq_dram[:, :, ds(g * HG * DH, HG * DH)]).then_inc(w_loaded, 16)

                load_w(0)
                sp.dma_start(ctxT[:], io["ctxT"].rearrange("(k p) n -> p k n", p=P)).then_inc(ctx_loaded, 16)
                sp.dma_start(att.wo[:], wo_dram[:, 0:HG, :]).then_inc(att.wo_loaded, 16)
                with sp.Fori(1, GROUPS) as g:
                    sp.wait_ge(att.proj_free, (g - 1) * att.proj_uses + NPROJ + RING)
                    load_w(g)
                    sp.wait_ge(att.proj_ready, g * att.proj_uses)
                    sp.dma_start(att.wo[:], wo_dram[:, ds(g * HG, HG), :]).then_inc(att.wo_loaded, 16)

            @block.gpsimd
            def _(pool):
                norm.gpsimd(pool)

            @block.vector
            def _(dve):
                dve.sem_inc(att.proj_free, RING)
                dve.sem_inc(att.outp_free, RING)
                norm.vector(dve)
                with dve.Fori(0, GROUPS) as g:
                    n = 0
                    for h in range(HG):
                        for i in range(HALVES):
                            dve.wait_ge(att.proj_ready, g * att.proj_uses + n + 1)
                            dve.tensor_scalar(att.qT[:, h, i * D:(i + 1) * D], core.proj[n % 2][0:DH, :],
                                              float(DH) ** -0.5, None, ALU.mult).then_inc(att.proj_free, 1)
                            n += 1
                    for i in range(HALVES):
                        dve.wait_ge(att.proj_ready, g * att.proj_uses + n + 1)
                        bs = D // SEQ
                        dve.tensor_copy(kT[:, i * bs:(i + 1) * bs, 0:SEQ],
                                        core.proj[n % 2][0:DH, :].rearrange("p (b t) -> p b t", t=SEQ))\
                            .then_inc(att.proj_free, 1)
                        n += 1
                    dve.wait_ge(att.proj_ready, g * att.proj_uses + n + 1)
                    dve.tensor_copy(kT[:, :, SEQ:KEYS],
                                    core.proj[n % 2][0:DH, 0:B * CTX].rearrange("p (b t) -> p b t", t=CTX))\
                        .then_inc(att.proj_free, 1)
                    n += 1
                    for i in range(TC // VPACK):
                        dve.wait_ge(att.proj_ready, g * att.proj_uses + n + 1)
                        dve.tensor_copy(v[:, i * VPACK:(i + 1) * VPACK, :],
                                        core.proj[n % 2][:, 0:VPACK * DH].rearrange("p (c d) -> p c d", d=DH))\
                            .then_inc(att.proj_free, 1)
                        n += 1
                    dve.wait_ge(att.proj_ready, g * att.proj_uses + n + 1)
                    dve.tensor_copy(vc[:], core.proj[n % 2][0:CTX, 0:B * DH].rearrange("p (b d) -> p b d", d=DH))\
                        .then_inc(att.proj_free, 1)
                    att.vector(dve, g)

            @block.scalar
            def _(act):
                act.sem_inc(att.turn_free, RING)
                act.sem_inc(att.score_free, RING)
                norm.scalar(act)
                with act.Fori(0, GROUPS) as g:
                    att.scalar(act, g)

            @block.tensor
            def _(pe):
                norm.tensor(pe)
                pe.wait_ge(norm.hT_ready, norm.hT_done)
                pe.wait_ge(ctx_loaded, 16)
                with pe.Fori(0, GROUPS) as g:
                    n = 0
                    pe.wait_ge(w_loaded, g * 48 + 48)
                    for h in range(HG + 1):
                        for i in range(HALVES):
                            pe.wait_ge(att.proj_free, g * att.proj_uses + n + 1)
                            for k in range(KC):
                                w = wq[:, k, h * DH:(h + 1) * DH] if h < HG else wkv[:, 0, k, :]
                                last = pe.matmul(core.proj[n % 2][0:DH, :], w, core.hT[:, k, i * D:(i + 1) * D],
                                                 start=(k == 0), stop=(k == KC - 1))
                            last.then_inc(att.proj_ready, 1)
                            n += 1
                    pe.wait_ge(att.proj_free, g * att.proj_uses + n + 1)
                    for k in range(KC):
                        last = pe.matmul(core.proj[n % 2][0:DH, 0:B * CTX], wkv[:, 0, k, :], ctxT[:, k, :],
                                         start=(k == 0), stop=(k == KC - 1))
                    last.then_inc(att.proj_ready, 1)
                    n += 1
                    for i in range(TC // VPACK):
                        pe.wait_ge(att.proj_free, g * att.proj_uses + n + 1)
                        for j in range(VPACK):
                            t0 = (i * VPACK + j) * P
                            for k in range(KC):
                                last = pe.matmul(core.proj[n % 2][:, j * DH:(j + 1) * DH],
                                                 core.hT[:, k, t0:t0 + P], wkv[:, 1, k, :],
                                                 start=(k == 0), stop=(k == KC - 1))
                        last.then_inc(att.proj_ready, 1)
                        n += 1
                    pe.wait_ge(att.proj_free, g * att.proj_uses + n + 1)
                    for b in range(B):
                        for k in range(KC):
                            last = pe.matmul(core.proj[n % 2][0:CTX, b * DH:(b + 1) * DH],
                                             ctxT[:, k, b * CTX:(b + 1) * CTX], wkv[:, 1, k, :],
                                             start=(k == 0), stop=(k == KC - 1))
                    last.then_inc(att.proj_ready, 1)
                    pe.wait_ge(att.proj_free, g * att.proj_uses + NPROJ + RING)
                    att.tensor(pe, g, lambda h, b: kT[:, b, :],
                               lambda h, b, k: v[:, QC * b + k, :] if k < QC else vc[:, b, :])


E = 8


class Router:

    def __init__(self, core, ctx, name, probabilities):
        nc = core.nc
        self.c = core
        self.probabilities = probabilities
        sb = lambda n, shape, dt=F32: ctx.enter_context(nc.sbuf_tensor(f"{name}_{n}", shape, dt))
        sem = lambda n: core.hold.enter_context(nc.semaphore(f"{name}_{n}"))
        self.gate = sb("gate", [P, KC, E])
        self.ids = sb("ids", [P, E])
        self.logits = sb("logits", [P, TC, E])
        self.shifted = sb("shifted", [P, TC, E])
        self.row = sb("row", [P, TC])
        self.top = sb("top", [P, TC, 8])
        self.where = sb("where", [P, TC, 8], U32)
        self.wheref = sb("wheref", [P, TC, 2])
        self.share = sb("share", [P, TC, 2])
        self.chosen = sb("chosen", [P, 2, TC, E])
        self.weight = sb("weight", [P, TC, E])
        self.loaded = sem("gate_loaded")
        self.logits_ready = sem("logits_ready")
        self.exp_in_ready = sem("exp_in_ready")
        self.exp_ready = sem("exp_ready")
        self.step = sem("route_step")
        self.steps = 0

    def tensor(self, pe):
        c = self.c
        pe.wait_ge(self.loaded, 32)
        for i in range(TC):
            for k in range(KC):
                last = pe.matmul(c.score[0][:, i * E:(i + 1) * E], c.hT[:, k, i * P:(i + 1) * P],
                                 self.gate[:, k, :], start=(k == 0), stop=(k == KC - 1))
        last.then_inc(self.logits_ready, 1)

    def scalar(self, act):
        act.wait_ge(self.exp_in_ready, 1)
        if self.probabilities:
            act.activation(self.logits[:], self.shifted[:], ACT.Exp).then_inc(self.exp_ready, 1)
        else:
            act.activation(self.share[:, :, 1], self.row[:], ACT.Exp).then_inc(self.exp_ready, 1)

    def vector(self, dve):
        per_row = lambda a: a.unsqueeze(2).broadcast_to([P, TC, E])

        def link(ins):
            self.steps += 1
            ins.then_inc(self.step, 1)
            dve.wait_ge(self.step, self.steps)

        dve.wait_ge(self.logits_ready, 1)
        link(dve.tensor_copy(self.logits[:], self.c.score[0][:, 0:TC * E].rearrange("p (c e) -> p c e", e=E)))
        if self.probabilities:
            link(dve.tensor_reduce(self.row[:], self.logits[:], AX.X, ALU.max))
            dve.tensor_tensor(self.shifted[:], self.logits[:], per_row(self.row[:]), ALU.subtract)\
                .then_inc(self.exp_in_ready, 1)
            dve.wait_ge(self.exp_ready, 1)
            link(dve.tensor_reduce(self.row[:], self.logits[:], AX.X, ALU.add))
            link(dve.reciprocal(self.row[:], self.row[:]))
            link(dve.tensor_tensor(self.logits[:], self.logits[:], per_row(self.row[:]), ALU.mult))
        for i in range(TC):
            ins = dve.max(self.top[:, i, :], self.logits[:, i, :])
        link(ins)
        for i in range(TC):
            ins = dve.max_index(self.where[:, i, :], self.top[:, i, :], self.logits[:, i, :])
        link(ins)
        link(dve.tensor_copy(self.wheref[:], self.where[:, :, 0:2]))
        if self.probabilities:
            link(dve.tensor_tensor(self.row[:], self.top[:, :, 0], self.top[:, :, 1], ALU.add))
            link(dve.reciprocal(self.row[:], self.row[:]))
            for j in range(2):
                ins = dve.tensor_tensor(self.share[:, :, j], self.top[:, :, j], self.row[:], ALU.mult)
            link(ins)
        else:
            dve.tensor_tensor(self.row[:], self.top[:, :, 1], self.top[:, :, 0], ALU.subtract)\
                .then_inc(self.exp_in_ready, 1)
            dve.wait_ge(self.exp_ready, 1)
            link(dve.tensor_scalar(self.row[:], self.share[:, :, 1], 1.0, None, ALU.add))
            link(dve.reciprocal(self.share[:, :, 0], self.row[:]))
            link(dve.tensor_tensor(self.share[:, :, 1], self.share[:, :, 1], self.share[:, :, 0], ALU.mult))
        for j in range(2):
            link(dve.tensor_tensor(self.chosen[:, j, :, :], self.ids[:].unsqueeze(1).broadcast_to([P, TC, E]),
                                   per_row(self.wheref[:, :, j]), ALU.is_equal))
            link(dve.tensor_tensor(self.chosen[:, j, :, :], self.chosen[:, j, :, :],
                                   per_row(self.share[:, :, j]), ALU.mult))
        link(dve.tensor_tensor(self.weight[:], self.chosen[:, 0, :, :], self.chosen[:, 1, :, :], ALU.add))


def expert_mixture(nc, core, io, name):
    with ExitStack() as ctx:
        sb = lambda n, shape: ctx.enter_context(nc.sbuf_tensor(f"{name}_{n}", shape, F32))
        sem = lambda n: core.hold.enter_context(nc.semaphore(f"{name}_{n}"))
        w = sb("experts", [P, E, KC, D])
        w_loaded = sem("experts_loaded")
        out_ready = sem("out_ready")
        out_free = sem("out_free")
        norm = Norm(core)
        route = Router(core, ctx, name, probabilities=False)

        with nc.Block() as block:

            @block.sync
            def _(sp):
                sp.dma_start(route.gate[:], io["L0_gate"].rearrange("(k p) e -> p k e", p=P)).then_inc(route.loaded, 16)
                sp.dma_start(route.ids[:], io["expert_ids"].partition_broadcast(P)).then_inc(route.loaded, 16)
                for e in range(E):
                    sp.dma_start(w[:, e, :, :], io["L0_experts"][e].rearrange("(k p) n -> p k n", p=P))\
                        .then_inc(w_loaded, 16)

            @block.gpsimd
            def _(pool):
                norm.gpsimd(pool)

            @block.vector
            def _(dve):
                dve.sem_inc(out_free, RING)
                norm.vector(dve)
                route.vector(dve)
                with dve.Fori(0, E) as e:
                    for i in range(TC):
                        dve.wait_ge(out_ready, e * TC + i + 1)
                        dve.scalar_tensor_tensor(core.x[:, i, :], core.proj[i % 2][:, :],
                                                 route.weight[:, i, ds(e, 1)], core.x[:, i, :],
                                                 ALU.mult, ALU.add).then_inc(out_free, 1)

            @block.scalar
            def _(act):
                norm.scalar(act)
                route.scalar(act)

            @block.tensor
            def _(pe):
                norm.tensor(pe)
                pe.wait_ge(norm.hT_ready, norm.hT_done)
                route.tensor(pe)
                pe.wait_ge(w_loaded, E * 16)
                with pe.Fori(0, E) as e:
                    for i in range(TC):
                        pe.wait_ge(out_free, e * TC + i + 1)
                        for k in range(KC):
                            last = pe.matmul(core.proj[i % 2][:, :], core.hT[:, k, i * P:(i + 1) * P],
                                             w[:, ds(e, 1), k, :].rearrange("p a n -> p (a n)"),
                                             start=(k == 0), stop=(k == KC - 1))
                        last.then_inc(out_ready, 1)


def adapted_linear(nc, core, io, name, out):
    R = 16
    SCALING = 16.0 / R
    with ExitStack() as ctx:
        sb = lambda n, shape: ctx.enter_context(nc.sbuf_tensor(f"{name}_{n}", shape, F32))
        sem = lambda n: core.hold.enter_context(nc.semaphore(f"{name}_{n}"))
        w = sb("base", [P, KC, D])
        wa = sb("a", [P, KC, E * R])
        wb = sb("b", [E * R, D])
        bias = sb("bias", [P, D])
        low = sb("low", [P, 2, E * R])
        lowT = sb("lowT", [E * R, 2, P])
        w_loaded = sem("w_loaded")
        bias_loaded = sem("bias_loaded")
        down_ready = sem("down_ready")
        low_ready = sem("low_ready")
        turned = sem("turned")
        lowT_ready = sem("lowT_ready")
        out_ready = sem("out_ready")
        x_ready = sem("x_ready")
        stored = sem("stored")
        norm = Norm(core, bias[:, :], bias_loaded)
        route = Router(core, ctx, name, probabilities=True)
        out_dram = out.rearrange("(c p) d -> c p d", p=P)

        with nc.Block() as block:

            @block.sync
            def _(sp):
                sp.dma_start(bias[:], io["L1_ffn_b_base"].partition_broadcast(P)).then_inc(bias_loaded, 16)
                sp.dma_start(route.gate[:], io["L1_gate"].rearrange("(k p) e -> p k e", p=P)).then_inc(route.loaded, 16)
                sp.dma_start(route.ids[:], io["expert_ids"].partition_broadcast(P)).then_inc(route.loaded, 16)
                sp.dma_start(wa[:], io["L1_A"].rearrange("(k p) n -> p k n", p=P)).then_inc(w_loaded, 16)
                sp.dma_start(wb[:], io["L1_B"]).then_inc(w_loaded, 16)
                sp.dma_start(w[:], io["L1_base"].rearrange("(k p) n -> p k n", p=P)).then_inc(w_loaded, 16)
                for i in range(TC):
                    sp.wait_ge(x_ready, i + 1)
                    sp.dma_start(out_dram[i], core.x[:, i, :]).then_inc(stored, 16)
                sp.wait_ge(stored, TC * 16)

            @block.gpsimd
            def _(pool):
                norm.gpsimd(pool)

            @block.vector
            def _(dve):
                norm.vector(dve)
                route.vector(dve)
                for i in range(TC + 1):
                    if i < TC:
                        dve.wait_ge(down_ready, i + 1)
                        dve.scalar_tensor_tensor(low[:, i % 2, :].rearrange("p (e r) -> p e r", r=R),
                                                 core.score[i % 2][:, 0:E * R].rearrange("p (e r) -> p e r", r=R),
                                                 SCALING, route.weight[:, i, :].unsqueeze(2).broadcast_to([P, E, R]),
                                                 ALU.mult, ALU.mult).then_inc(low_ready, 1)
                    if i >= 1:
                        dve.wait_ge(out_ready, i)
                        dve.tensor_tensor(core.x[:, i - 1, :], core.proj[(i - 1) % 2][:, :], core.x[:, i - 1, :],
                                          ALU.add).then_inc(x_ready, 1)

            @block.scalar
            def _(act):
                norm.scalar(act)
                route.scalar(act)
                for i in range(TC):
                    act.wait_ge(turned, i + 1)
                    act.copy(lowT[:, i % 2, :], core.turn[i % 2][:, 0:P]).then_inc(lowT_ready, 1)

            @block.tensor
            def _(pe):
                norm.tensor(pe)
                pe.wait_ge(norm.hT_ready, norm.hT_done)
                route.tensor(pe)
                pe.wait_ge(w_loaded, 48)

                def down(i):
                    if i == 0:
                        pe.wait_ge(route.exp_in_ready, 1)
                    if i >= 2:
                        pe.wait_ge(low_ready, i - 1)
                    for k in range(KC):
                        last = pe.matmul(core.score[i % 2][:, 0:E * R], core.hT[:, k, i * P:(i + 1) * P],
                                         wa[:, k, :], start=(k == 0), stop=(k == KC - 1))
                    last.then_inc(down_ready, 1)

                def base(i):
                    if i >= 2:
                        pe.wait_ge(x_ready, i - 1)
                    for k in range(KC):
                        pe.matmul(core.proj[i % 2][:, :], core.hT[:, k, i * P:(i + 1) * P], w[:, k, :],
                                  start=(k == 0), stop=False)

                down(0)
                for i in range(TC):
                    if i + 1 < TC:
                        down(i + 1)
                    base(i)
                    pe.wait_ge(low_ready, i + 1)
                    if i >= 2:
                        pe.wait_ge(lowT_ready, i - 1)
                    pe.transpose(core.turn[i % 2][:, 0:P], low[:, i % 2, :], core.ident[:]).then_inc(turned, 1)
                    pe.wait_ge(lowT_ready, i + 1)
                    pe.matmul(core.proj[i % 2][:, :], lowT[:, i % 2, :], wb[:, :], start=False, stop=True)\
                        .then_inc(out_ready, 1)


def head_attention(nc, core, io, name):
    H, DH = 32, 16
    PACK = P // H
    GROUP = P // B
    ROWS = DH + PACK
    PACKS = D // P
    TOKENS = PACKS * PACK
    BLOCKS = SEQ // TOKENS
    UNITS = BLOCKS * B
    HPC = P // DH
    HALVES = T // D
    BACK = D // P
    with ExitStack() as ctx:
        sb = lambda n, shape: ctx.enter_context(nc.sbuf_tensor(f"{name}_{n}", shape, F32))
        sem = lambda n: core.hold.enter_context(nc.semaphore(f"{name}_{n}"))
        w = sb("w", [P, 3, KC, D])
        bias = sb("bias", [P, 3, KC])
        stage = sb("stage", [P, KC, T])
        spread = [sb(f"spread_{n}", [P, H, SEQ]) for n in "qkv"]
        context = spread[2]
        tags = sb("tags", [P, 2, TOKENS, H])
        slot = [sb(f"slot_{n}", [P, RING, TOKENS, H]) for n in "qkv"]
        values = sb("values", [P, RING, PACKS, B, GROUP])
        nmax = sb("nmax", [P, RING, PACKS])
        shifted = sb("shifted", [P, RING, D])
        probs = sb("probs", [P, RING, D])
        probsT = sb("probsT", [P, RING, D])
        rsum = sb("rsum", [P, RING, B, BACK])
        part = sb("part", [P, RING, B, BACK, DH])
        scratch = [nc.dram_tensor(f"{name}_scratch_{n}", (D, T), F32, kind="Internal").ap() for n in "qkv"]

        w_loaded = [sem(f"w{n}_loaded") for n in "qkv"]
        bias_loaded = sem("bias_loaded")
        tags_loaded = sem("tags_loaded")
        zeroed = sem("zeroed")
        ones_ready = sem("ones_ready")
        proj_ready = sem("proj_ready")
        proj_free = sem("proj_free")
        to_dram = [sem(f"to_dram{c}") for c in range(KC)]
        spread_loaded = [sem(f"spread_{n}_loaded") for n in "qkv"]
        slot_ready = sem("slot_ready")
        v_turned = sem("v_turned")
        v_ready = sem("v_ready")
        score_ready = sem("score_ready")
        max_ready = sem("max_ready")
        shifted_ready = sem("shifted_ready")
        probs_ready = sem("probs_ready")
        probs_turned = sem("probs_turned")
        probsT_ready = sem("probsT_ready")
        out_ready = sem("out_ready")
        out_copied = sem("out_copied")
        back_ready = sem("back_ready")
        rsum_ready = sem("rsum_ready")
        part_ready = sem("part_ready")
        added = sem("added")
        norm = Norm(core)

        def block_of(t, tile):
            return tile[:, :, ds(t * TOKENS, TOKENS)].rearrange("p h t -> p t h")

        def packs(tile):
            return tile.rearrange("p (a k) -> p a k", a=PACKS)

        def each_unit(engine, step):
            for j in range(RING * B):
                step(0, j, True)
            with engine.Fori(1, BLOCKS // RING) as i:
                for j in range(RING * B):
                    step(i, j, False)

        def place(i, j):
            return i * RING * B + j, j % RING, i * RING + j // B, j // B % RING, j % B

        with nc.Block() as block:

            @block.sync
            def _(sp):
                for j, n in enumerate("qkv"):
                    sp.dma_start(w[:, j, :, :], io[f"L1_attn_w{n}"].rearrange("(k p) n -> p k n", p=P))\
                        .then_inc(w_loaded[j], 16)
                    sp.dma_start(bias[:, j, :], io[f"L1_attn_b{n}"]).then_inc(bias_loaded, 16)
                sp.dma_start(tags[:], io["tags"].rearrange("j p (t h) -> p j t h", h=H)).then_inc(tags_loaded, 16)
                for j in range(3):
                    for c in range(KC):
                        sp.wait_ge(proj_free, j * KC * HALVES + (c + 1) * HALVES + RING)
                        sp.dma_start(scratch[j][c * P:(c + 1) * P, :], stage[:, c, :]).then_inc(to_dram[c], 16)
                    for c in range(KC):
                        sp.wait_ge(to_dram[c], 16 * (j + 1))
                    sp.wait_ge(zeroed, 3)
                    for b in range(B):
                        sp.dma_start(spread[j][b * GROUP:b * GROUP + DH, :, :],
                                     scratch[j].rearrange("(h d) t -> d h t", d=DH)[:, :, b * SEQ:(b + 1) * SEQ])\
                            .then_inc(spread_loaded[j], 16)

            @block.gpsimd
            def _(pool):
                norm.gpsimd(pool)
                for j in range(3):
                    pool.memset(spread[j][:], 0.0).then_inc(zeroed, 1)
                pool.memset(values[:], 0.0).then_inc(zeroed, 1)
                pool.wait_ge(zeroed, 4)
                for r in range(RING):
                    pool.memset(values[:, r, :, :, DH:DH + 1], 1.0).then_inc(ones_ready, 1)
                for j in range(3):
                    pool.wait_ge(spread_loaded[j], 16 * B)

                def fill_slots(i, j, peeled):
                    _, _, t, r, b = place(i, j)
                    if b:
                        return
                    pool.wait_ge(tags_loaded, 16)
                    if not peeled:
                        pool.wait_ge(score_ready, (t - 1) * B)
                    pool.tensor_copy(slot[2][:, r, :, :], block_of(t, spread[2]))
                    for n in range(2):
                        last = pool.tensor_tensor(slot[n][:, r, :, :], block_of(t, spread[n]),
                                                  tags[:, n, :, :], ALU.add)
                    last.then_inc(slot_ready, 1)

                each_unit(pool, fill_slots)

            @block.vector
            def _(dve):
                dve.sem_inc(proj_free, RING)
                norm.vector(dve)
                dve.wait_ge(bias_loaded, 48)
                for j in range(3):
                    scale = float(DH) ** -0.5 if j == 0 else 1.0
                    for c in range(KC):
                        if j >= 1:
                            dve.wait_ge(to_dram[c], 16 * j)
                        for i in range(HALVES):
                            n = (j * KC + c) * HALVES + i
                            dve.wait_ge(proj_ready, n + 1)
                            dve.tensor_scalar(stage[:, c, i * D:(i + 1) * D], core.proj[n % 2][:, :],
                                              bias[:, j, c:c + 1], scale, ALU.add, ALU.mult)\
                                .then_inc(proj_free, 1)

                def copy_out(t, r):
                    dve.wait_ge(tags_loaded, 16)
                    dve.wait_ge(out_ready, (t + 1) * B)
                    dve.tensor_copy(block_of(t, context), core.proj[r][:, :].rearrange("p (t h) -> p t h", h=H))\
                        .then_inc(out_copied, 1)

                def softmax(i, j, peeled):
                    u, ur, t, r, b = place(i, j)
                    dve.wait_ge(score_ready, u + 1)
                    dve.tensor_reduce(nmax[:, ur, :], packs(core.score[ur][:, :]), AX.X, ALU.max)\
                        .then_inc(max_ready, 1)
                    if b == B - 2 and not (peeled and j < B):
                        copy_out(t - 1, 1 - r)
                    dve.wait_ge(max_ready, u + 1)
                    dve.tensor_tensor(packs(shifted[:, ur, :]), packs(core.score[ur][:, :]),
                                      nmax[:, ur, :].unsqueeze(2).broadcast_to([P, PACKS, P]), ALU.subtract)\
                        .then_inc(shifted_ready, 1)

                each_unit(dve, softmax)
                copy_out(BLOCKS - 1, (BLOCKS - 1) % RING)
                for n in range(QC * H // BACK):
                    r, qc, h0 = n % RING, n % QC, n // QC * BACK
                    turned = core.turn[r][:, :].rearrange("p (h b s) -> p b h s", h=BACK, b=B)
                    dve.wait_ge(back_ready, n + 1)
                    dve.reciprocal(rsum[:, r, :, :], turned[:, :, :, DH]).then_inc(rsum_ready, 1)
                    dve.wait_ge(rsum_ready, n + 1)
                    dve.tensor_tensor(part[:, r, :, :, :], turned[:, :, :, 0:DH],
                                      rsum[:, r, :, :].unsqueeze(3).broadcast_to([P, B, BACK, DH]),
                                      ALU.mult).then_inc(part_ready, 1)
                    dve.wait_ge(part_ready, n + 1)
                    x = core.x[:].rearrange("p (b q) d -> p b q d", q=QC)[:, :, qc, h0 * DH:(h0 + BACK) * DH]
                    dve.tensor_tensor(x, x, part[:, r, :, :, :].rearrange("p b h d -> p b (h d)"), ALU.add)

            @block.scalar
            def _(act):
                norm.scalar(act)
                act.wait_ge(ones_ready, RING)

                def turn_out(u, ur):
                    act.wait_ge(probs_turned, u + 1)
                    act.copy(probsT[:, ur, :], core.outp[ur][:, :]).then_inc(probsT_ready, 1)

                def softmax(i, j, peeled):
                    u, ur, t, r, b = place(i, j)
                    act.wait_ge(shifted_ready, u + 1)
                    act.activation(probs[:, ur, :], shifted[:, ur, :], ACT.Exp).then_inc(probs_ready, 1)
                    if not (peeled and j < 1):
                        turn_out(u - 1, 1 - ur)
                    if b == 0:
                        act.wait_ge(v_turned, t + 1)
                        if not peeled:
                            act.wait_ge(out_ready, (t - 1) * B)
                        act.copy(values[:, r, :, :, 0:DH],
                                 core.turn[r][:, :].rearrange("p (a b s) -> p a b s", a=PACKS, b=B)[:, :, :, 0:DH])\
                            .then_inc(v_ready, 1)

                each_unit(act, softmax)
                turn_out(UNITS - 1, (UNITS - 1) % RING)

            @block.tensor
            def _(pe):
                norm.tensor(pe)
                pe.wait_ge(norm.hT_ready, norm.hT_done)
                for j in range(3):
                    pe.wait_ge(w_loaded[j], 16)
                    for c in range(KC):
                        for i in range(HALVES):
                            n = (j * KC + c) * HALVES + i
                            pe.wait_ge(proj_free, n + 1)
                            for k in range(KC):
                                last = pe.matmul(core.proj[n % 2][:, :], w[:, j, k, c * P:(c + 1) * P],
                                                 core.hT[:, k, i * D:(i + 1) * D],
                                                 start=(k == 0), stop=(k == KC - 1))
                            last.then_inc(proj_ready, 1)

                def turn(u, ur, bank_used):
                    pe.wait_ge(probs_ready, u + 1)
                    if bank_used:
                        pe.wait_ge(probsT_ready, u - 1)
                    for a in range(PACKS):
                        last = pe.transpose(core.outp[ur][:, a * P:(a + 1) * P], probs[:, ur, a * P:(a + 1) * P],
                                            core.ident[:])
                    last.then_inc(probs_turned, 1)

                def product(u, ur, t, r, b, bank_used):
                    pe.wait_ge(probsT_ready, u + 1)
                    if b == 0:
                        pe.wait_ge(v_ready, t + 1)
                        if bank_used:
                            pe.wait_ge(out_copied, t - 1)
                    for a in range(PACKS):
                        last = pe.matmul(core.proj[r][b * GROUP:(b + 1) * GROUP, a * P:(a + 1) * P],
                                         values[:, r, a, b, :], probsT[:, ur, a * P:(a + 1) * P],
                                         start=True, stop=True)
                    last.then_inc(out_ready, 1)

                def scores(i, j, peeled):
                    u, ur, t, r, b = place(i, j)
                    if b == 0:
                        pe.wait_ge(slot_ready, t + 1)
                        if not peeled:
                            pe.wait_ge(v_ready, t - 1)
                        for a in range(PACKS):
                            last = pe.transpose(core.turn[r][:, a * P:(a + 1) * P],
                                                slot[2][:, r, a * PACK:(a + 1) * PACK, :].rearrange("p t h -> p (t h)"),
                                                core.ident[:])
                        last.then_inc(v_turned, 1)
                    if not (peeled and j < RING):
                        pe.wait_ge(shifted_ready, u - 1)
                    rows = slice(b * GROUP, b * GROUP + ROWS)
                    for a in range(PACKS):
                        q, k = (slot[n][rows, r, a * PACK:(a + 1) * PACK, :].rearrange("p t h -> p (t h)")
                                for n in range(2))
                        last = pe.matmul(core.score[ur][:, a * P:(a + 1) * P], q, k, start=True, stop=True)
                    last.then_inc(score_ready, 1)
                    if not (peeled and j < 1):
                        turn(u - 1, 1 - ur, not (peeled and j - 1 < RING))
                    if not (peeled and j < 2):
                        _, _, t2, r2, b2 = place(i, j - 2)
                        product(u - 2, ur, t2, r2, b2, not peeled)

                pe.wait_ge(proj_free, 3 * KC * HALVES + RING)
                each_unit(pe, scores)
                turn(UNITS - 1, (UNITS - 1) % RING, True)
                for u in (UNITS - 2, UNITS - 1):
                    product(u, u % RING, u // B, u // B % RING, u % B, True)
                pe.wait_ge(out_copied, BLOCKS)
                for n in range(QC * H // BACK):
                    qc, h0 = n % QC, n // QC * BACK
                    if n >= RING:
                        pe.wait_ge(part_ready, n - 1)
                    for h in range(BACK):
                        last = pe.transpose(core.turn[n % RING][:, h * P:(h + 1) * P],
                                            context[:, h0 + h, qc * P:(qc + 1) * P], core.ident[:])
                    last.then_inc(back_ready, 1)


def build_program(nc, io, out):
    with ExitStack() as ctx:
        core = Core(nc, ctx)
        self_attention(nc, core, io, "self", 1e-6)
        context_attention(nc, core, io, "context", 1e-5)
        expert_mixture(nc, core, io, "experts")
        head_attention(nc, core, io, "heads")
        latent_attention(nc, core, io, "latent")
        adapted_linear(nc, core, io, "adapted", out)


def layout(inputs):
    import numpy as np

    a = {n: np.asarray(v) for n, v in inputs.items()}
    flat = {n: a[n] for n in ("L0_attn_Wq", "L0_attn_bq", "L0_attn_Wk", "L0_attn_bk", "L0_attn_Wv",
                              "L0_attn_bv", "L0_attn_Wo", "L0_attn_bo", "L0_attn_gq", "L0_attn_gk")}
    flat["x"] = a["x"].reshape(T, D)
    flat["ident"] = np.eye(P, dtype=np.float32)
    flat["expert_ids"] = np.arange(E, dtype=np.float32)
    flat["ctxT"] = a["ctx_4096"].reshape(B * CTX, D).T
    flat["mask"] = a["mask_1x1xSxS2_ff0"].reshape(SEQ, CTX)
    for n in "qkvo":
        flat[f"L0_xattn_{n}"] = a[f"L0_xattn_{n}_proj_w"].T
        flat[f"L1_xattn_{n}"] = a[f"L1_xattn_W{n}"].T
        if n != "o":
            flat[f"L1_attn_w{n}"] = a[f"L1_attn_w{n}"].T
            flat[f"L1_attn_b{n}"] = a[f"L1_attn_b{n}"].reshape(KC, P).T
    tags = np.zeros((2, B, P // B, 4, 32), np.float32)
    for t in range(4):
        tags[0, :, 16 + t, t, :] = 1.0
        tags[1, :, 16 + t, :, :] = -1e30
        tags[1, :, 16 + t, t, :] = 0.0
    flat["tags"] = np.tile(tags.reshape(2, P, P), (1, 1, 4))
    flat["L0_xattn_gq"] = a["L0_xattn_q_norm_w"]
    flat["L0_xattn_gk"] = a["L0_xattn_k_norm_w"]
    flat["L0_gate"] = a["L0_ffn_gate_w"]
    flat["L0_experts"] = a["L0_ffn_expert_w"]
    flat["L1_gate"] = a["L1_ffn_W_gate"].T
    flat["L1_base"] = a["L1_ffn_W_base"].T
    flat["L1_ffn_b_base"] = a["L1_ffn_b_base"]
    flat["L1_A"] = a["L1_ffn_A"].reshape(-1, D).T
    flat["L1_B"] = a["L1_ffn_B"].transpose(0, 2, 1).reshape(-1, D)
    return {n: np.ascontiguousarray(v) for n, v in flat.items()}


def kernel(**inputs):
    import concourse.bacc as bacc
    from concourse.bass_utils import run_bass_kernel_spmd

    nc = bacc.Bacc("TRN2", target_bir_lowering=False, num_devices=1)
    arrays = {f"in_{n}_dram": v for n, v in layout(inputs).items()}
    io = {n[3:-5]: nc.dram_tensor(n, v.shape, mybir.dt.from_np(v.dtype), kind="ExternalInput").ap()
          for n, v in arrays.items()}
    out = nc.dram_tensor("out_dram", (T, D), F32, kind="ExternalOutput").ap()
    build_program(nc, io, out)
    result = run_bass_kernel_spmd(nc, [arrays], core_ids=[0])
    return result.results[0]["out_dram"].reshape(B, SEQ, D)
```

```python
from contextlib import ExitStack

import concourse.bass as bass
from concourse import mybir

F32 = mybir.dt.float32
F32R = mybir.dt.float32r
U32 = mybir.dt.uint32
ALU = mybir.AluOpType
ACT = mybir.ActivationFunctionType
AX = mybir.AxisListType
ds = bass.ds

P = 128
B, SEQ, D = 4, 256, 512
T = B * SEQ
TC = T // P
KC = D // P
CTX = 64
LN_EPS = 1e-5
QC = SEQ // P
HG = 4
RING = 2


class Core:

    def __init__(self, nc, ctx):
        self.nc = nc
        self.hold = ctx

        def sb(name, shape, dt=F32):
            return ctx.enter_context(nc.sbuf_tensor(name, shape, dt))

        self.x = sb("x_res", [P, TC, D])
        self.hT = None
        self.ident = sb("ident", [P, P])
        self.neg_half = sb("neg_half", [P, 32])
        self.mv = sb("ln_mean_var", [P, TC, 2])
        self.stats = sb("ln_stats", [P, TC, 6])
        self.vareps = sb("ln_var_eps", [P, TC])
        self.rstd = sb("ln_rstd", [P, TC])
        self.h = None
        self.norms = 0
        self.pair_norms = 0
        self.norm_sems = [ctx.enter_context(nc.semaphore(f"ln_{n}")) for n in
                          ("stats", "mean", "var_eps", "rstd", "h", "turned", "hi", "hT")]
        bank = lambda name: ctx.enter_context(nc.psum_tensor(name, [P, D], F32))
        self.proj = [bank(f"proj{i}") for i in range(RING)]
        self.score = [bank(f"score{i}") for i in range(RING)]
        self.turn = [bank(f"turn{i}") for i in range(RING)]
        self.outp = [bank(f"outp{i}") for i in range(RING)]


class Pair:

    def __init__(self, nc, ctx, name, shape):
        self.hi = ctx.enter_context(nc.sbuf_tensor(f"{name}_hi", shape, F32R))
        self.lo = ctx.enter_context(nc.sbuf_tensor(f"{name}_lo", shape, F32R))


def product(pe, out, a_hi, a_lo, b_hi, b_lo, start, stop):
    pe.matmul(out, a_hi, b_lo, start=start, stop=False)
    pe.matmul(out, a_lo, b_hi, start=False, stop=False)
    return pe.matmul(out, a_hi, b_hi, start=False, stop=stop)


class Norm:

    def __init__(self, core, bias=None, bias_loaded=None, pair=None, column=lambda i: i * P):
        self.c = core
        self.bias, self.bias_loaded = bias, bias_loaded
        self.pair = pair
        self.columns = lambda i: slice(column(i), column(i) + P)
        (self.stats_ready, self.mean_ready, self.var_eps_ready, self.rstd_ready, self.h_ready, self.turned,
         self.hi_ready, self.hT_ready) = core.norm_sems
        self.n0 = core.norms * TC
        self.hT_done = self.n0 + TC
        core.norms += 1
        self.hi0 = core.pair_norms * TC
        core.pair_norms += 1 if pair else 0

    def vector(self, dve):
        c, n0 = self.c, self.n0
        for i in range(TC):
            dve.bn_stats(c.stats[:, i, :], c.x[:, i, :]).then_inc(self.stats_ready, 1)
            dve.wait_ge(self.stats_ready, n0 + i + 1)
            dve.bn_aggr(c.mv[:, i, :], c.stats[:, i, :]).then_inc(self.mean_ready, 1)
        for i in range(TC + 1):
            if i < TC:
                dve.wait_ge(self.rstd_ready, n0 + i + 1)
                dve.wait_ge(self.mean_ready, n0 + i + 1)
                if i >= 2:
                    dve.wait_ge(self.turned, n0 + i - 1)
                dve.tensor_scalar(c.h[:, i % 2, :], c.x[:, i, :], c.mv[:, i, 0:1], c.rstd[:, i:i + 1],
                                  ALU.subtract, ALU.mult).then_inc(self.h_ready, 1)
                if self.bias is not None:
                    if i == 0:
                        dve.wait_ge(self.bias_loaded, 16)
                    dve.wait_ge(self.h_ready, n0 + i + 1)
                    dve.tensor_tensor(c.x[:, i, :], c.x[:, i, :], self.bias, ALU.add)
            if i >= 1 and self.pair:
                j = i - 1
                dve.wait_ge(self.hi_ready, self.hi0 + j + 1)
                chunk = self.columns(j)
                dve.tensor_tensor(self.pair.lo[:, :, chunk], c.turn[j % 2][:].rearrange("p (k t) -> p k t", k=KC),
                                  self.pair.hi[:, :, chunk].bitcast(F32), ALU.subtract).then_inc(self.hT_ready, 1)

    def gpsimd(self, pool):
        c, n0 = self.c, self.n0
        for i in range(TC):
            pool.wait_ge(self.mean_ready, n0 + i + 1)
            pool.tensor_scalar(c.vareps[:, i:i + 1], c.mv[:, i, 1:2], LN_EPS, None, ALU.add)\
                .then_inc(self.var_eps_ready, 1)
            pool.wait_ge(self.var_eps_ready, n0 + i + 1)
            pool.tensor_tensor(c.rstd[:, i:i + 1], c.vareps[:, i:i + 1], c.neg_half[:, 0:1], ALU.pow)\
                .then_inc(self.rstd_ready, 1)

    def tensor(self, pe, after=lambda i: None):
        c, n0 = self.c, self.n0
        for i in range(TC):
            pe.wait_ge(self.h_ready, n0 + i + 1)
            if i >= 2:
                pe.wait_ge(self.hT_ready, n0 + i - 1)
            for k in range(KC):
                last = pe.transpose(c.turn[i % 2][:, k * P:(k + 1) * P], c.h[:, i % 2, k * P:(k + 1) * P],
                                    c.ident[:])
            last.then_inc(self.turned, 1)
            after(i)

    def scalar(self, act):
        c, n0 = self.c, self.n0
        hT, ready = (self.pair.hi, self.hi_ready) if self.pair else (c.hT, self.hT_ready)
        for i in range(TC):
            act.wait_ge(self.turned, n0 + i + 1)
            act.copy(hT[:, :, self.columns(i)],
                     c.turn[i % 2][:].rearrange("p (k t) -> p k t", k=KC)).then_inc(ready, 1)


def self_attention(nc, core, io, name, eps):
    HPG = 2
    GROUPS = 32 // HPG
    W = HPG * P
    UNITS = B * HPG * QC
    OUTS = UNITS // QC
    PIECES = KC
    OUT_STEPS = {4: 0, 5: 1, 6: 2, 7: 3}
    PROJ = []
    for c in range(TC):
        PROJ += [("qk", c), ("v", c)] + ([("out", OUT_STEPS[c])] if c in OUT_STEPS else [])
    PROJ += [("out", i) for i in range(len(OUT_STEPS), TC)]
    TURNS = []
    for c in range(TC):
        TURNS += [("qk", c - 2)] * (c >= 2)
        TURNS += [("probs", s - 2) for s in (2 * c, 2 * c + 1) if s >= 2]
    TURNS += [("probs", UNITS - 2), ("probs", UNITS - 1), ("qk", TC - 2), ("qk", TC - 1)]

    with ExitStack() as ctx:
        sb = lambda n, shape: ctx.enter_context(nc.sbuf_tensor(f"{name}_{n}", shape, F32))
        sem = lambda n: core.hold.enter_context(nc.semaphore(f"{name}_{n}"))
        hT = Pair(nc, ctx, f"{name}_hT", [P, KC, T])
        raw = sb("raw", [P, KC, 3 * W])
        raw_o = sb("raw_o", [P, HPG, D])
        w = Pair(nc, ctx, f"{name}_w", [P, 2, KC, 3 * W])
        wo = Pair(nc, ctx, f"{name}_wo", [P, HPG, D])
        bias = sb("bias", [P, 2, 3 * W])
        gains = sb("gains", [P, 2])
        gain = sb("gain", [P, 1])
        epsilon = sb("epsilon", [P, 2 * HPG])
        tok = sb("tok", [P, 3, 2 * W])
        sq = sb("sq", [P, 2 * W])
        bo = sq
        ss = sb("ss", [P, 2, 2 * HPG])
        ms = sb("ms", [P, 2, 2 * HPG])
        rms = sb("rms", [P, 2, 2 * HPG])
        qT = sb("qT", [P, 2, HPG, T])
        kT = sb("kT", [P, 2, HPG, T])
        v = sb("v", [P, 2, TC, W])
        probs = sb("probs", [P, 4, SEQ])
        core.h = probs[:].rearrange("p (a b) k -> p a (b k)", a=2)
        nmax = sb("nmax", [P, 4])
        sums = sb("sums", [P, 4])
        rsum = sb("rsum", [P, 4])
        probsT = sb("probsT", [P, 2, QC, SEQ])
        outT = Pair(nc, ctx, f"{name}_outT", [P, HPG, T])

        x_loaded = sem("x_loaded")
        const_ready = sem("const_ready")
        bo_loaded = sem("bo_loaded")
        gain_loaded = sem("gain_loaded")
        gain_ready = sem("gain_ready")
        raw_loaded = sem("raw_loaded")
        raw_o_loaded = sem("raw_o_loaded")
        bias_loaded = [sem(f"bias{i}_loaded") for i in range(2)]
        w_hi_ready = sem("w_hi_ready")
        w_ready = sem("w_ready")
        wo_hi_ready = sem("wo_hi_ready")
        wo_ready = sem("wo_ready")
        proj_ready = sem("proj_ready")
        proj_free = sem("proj_free")
        sq_ready = sem("sq_ready")
        ss_ready = sem("ss_ready")
        ms_ready = sem("ms_ready")
        rms_ready = sem("rms_ready")
        qk_normed = sem("qk_normed")
        turn_ready = sem("turn_ready")
        turn_free = sem("turn_free")
        score_ready = sem("score_ready")
        score_free = sem("score_free")
        max_ready = sem("max_ready")
        rsum_ready = sem("rsum_ready")
        probs_ready = sem("probs_ready")
        outp_ready = sem("outp_ready")
        out_hi_ready = sem("out_hi_ready")
        outp_free = sem("outp_free")

        norm = Norm(core, bo[:, :], bo_loaded, pair=hT)
        w_dram = [io[n].rearrange("(k p) n -> p k n", p=P) for n in ("L0_attn_Wq", "L0_attn_Wk", "L0_attn_Wv")]
        b_dram = [io[n].partition_broadcast(P) for n in ("L0_attn_bq", "L0_attn_bk", "L0_attn_bv")]
        wo_dram = io["L0_attn_Wo"].rearrange("(n p) d -> p n d", p=P)

        proj_base = lambda k: 2 * TC + k * 3 * TC if not isinstance(k, int) or k >= 0 else 0

        def proj_use(k, what, project, attend):
            order = [u for u in PROJ if (u[0] == "out" and attend) or (u[0] != "out" and project)]
            n = order.index(what)
            return proj_base(k) + n, core.proj[n % 2]

        def turn_use(k, what, project, attend):
            order = [t for t in TURNS if (t[0] == "qk" and project) or (t[0] == "probs" and attend)]
            n = order.index(what)
            base = TC + k * len(TURNS) if not isinstance(k, int) or k >= 0 else 0
            return base + n, n % 2

        unit = lambda s: (s // (HPG * QC), s // QC % HPG, s % QC)

        def all_iterations(engine, iteration):
            iteration(-1, 1, True, False, True)
            with engine.Fori(0, (GROUPS - 2) // 2) as i:
                for par in range(2):
                    iteration(i * 2 + par, par, True, True, True)
            iteration(GROUPS - 2, 0, True, True, False)
            iteration(GROUPS - 1, 1, False, True, False)

        with nc.Block() as block:

            @block.sync
            def _(sp):
                def load_w(g):
                    for j in range(3):
                        sp.dma_start(raw[:, :, j * W:(j + 1) * W], w_dram[j][:, :, ds(g * W, W)])\
                            .then_inc(raw_loaded, 16)

                def load_bias(g, par):
                    for j in range(3):
                        sp.dma_start(bias[:, par, j * W:(j + 1) * W], b_dram[j][:, ds(g * W, W)])\
                            .then_inc(bias_loaded[par], 16)

                def load_wo(g):
                    sp.dma_start(raw_o[:], wo_dram[:, ds(g * HPG, HPG), :]).then_inc(raw_o_loaded, 16)

                sp.dma_start(core.x[:], io["x"].rearrange("(c p) d -> p c d", p=P)).then_inc(x_loaded, 16)
                sp.dma_start(core.ident[:], io["ident"]).then_inc(x_loaded, 16)
                load_w(0)
                sp.dma_start(bo[:], io["L0_attn_bo"].partition_broadcast(P)).then_inc(bo_loaded, 16)
                sp.dma_start(gains[:, 0:1], io["L0_attn_gq"].unsqueeze(1)).then_inc(gain_loaded, 16)
                sp.dma_start(gains[:, 1:2], io["L0_attn_gk"].unsqueeze(1)).then_inc(gain_loaded, 16)
                load_bias(0, 0)
                load_bias(1, 1)
                load_wo(0)

                def loads(k, par, more_w, more_bias):
                    if more_bias:
                        sp.wait_ge(proj_free, proj_base(k) + RING)
                        load_bias(k + 2, par)
                    if more_w:
                        sp.wait_ge(w_ready, (k + 3) * PIECES)
                        load_w(k + 3)
                    sp.wait_ge(wo_ready, k + 1)
                    load_wo(k + 1)

                for g in (1, 2):
                    sp.wait_ge(w_ready, g * PIECES)
                    load_w(g)
                with sp.Fori(0, (GROUPS - 4) // 2) as i:
                    for par in range(2):
                        loads(i * 2 + par, par, True, True)
                loads(GROUPS - 4, 0, True, True)
                loads(GROUPS - 3, 1, False, True)
                loads(GROUPS - 2, 0, False, False)

            @block.gpsimd
            def _(pool):
                pool.memset(core.neg_half[:], -0.5).then_inc(const_ready, 1)
                pool.memset(epsilon[:], eps).then_inc(const_ready, 1)
                pool.wait_ge(const_ready, 2)

                def split_w(g, par, piece):
                    pool.wait_ge(w_hi_ready, g * PIECES + piece + 1)
                    pool.tensor_tensor(w.lo[:, par, piece, :], raw[:, piece, :], w.hi[:, par, piece, :].bitcast(F32),
                                       ALU.subtract).then_inc(w_ready, 1)

                def iteration(k, par, project, attend, split):
                    for c in range(TC):
                        if project:
                            n = (k + 1) * TC + c
                            pool.wait_ge(ss_ready, n + 1)
                            pool.tensor_tensor(ms[:, c % 2, :], ss[:, c % 2, :], epsilon[:], ALU.add)\
                                .then_inc(ms_ready, 1)
                            pool.wait_ge(ms_ready, n + 1)
                            pool.tensor_tensor(rms[:, c % 2, :], ms[:, c % 2, :], core.neg_half[:, 0:2 * HPG],
                                               ALU.pow).then_inc(rms_ready, 1)
                        if split and c < PIECES:
                            split_w(k + 2, par, c)
                        if attend and c == 1:
                            pool.wait_ge(wo_hi_ready, k + 1)
                            pool.tensor_tensor(wo.lo[:], raw_o[:], wo.hi[:].bitcast(F32), ALU.subtract)\
                                .then_inc(wo_ready, 1)

                norm.gpsimd(pool)
                for piece in range(PIECES):
                    split_w(0, 0, piece)
                all_iterations(pool, iteration)

            @block.vector
            def _(dve):
                dve.wait_ge(x_loaded, 32)
                dve.sem_inc(proj_free, RING)
                dve.sem_inc(outp_free, RING)
                norm.vector(dve)
                dve.wait_ge(gain_loaded, 32)
                dve.scalar_tensor_tensor(gain[:], gains[:, 0:1], float(P) ** -0.5, gains[:, 1:2],
                                         ALU.mult, ALU.mult).then_inc(gain_ready, 1)

                def normalise(k, c):
                    dve.wait_ge(rms_ready, (k + 1) * TC + c + 1)
                    t = tok[:, c % 3, :].rearrange("p (h d) -> p h d", d=P)
                    dve.tensor_tensor(t, t, rms[:, c % 2, :].unsqueeze(2).broadcast_to([P, 2 * HPG, P]),
                                      ALU.mult).then_inc(qk_normed, 1)

                def divide(k, s):
                    dve.wait_ge(score_free, k * UNITS + s + 1 + RING)
                    dve.reciprocal(rsum[:, s % 4:s % 4 + 1], sums[:, s % 4:s % 4 + 1]).then_inc(rsum_ready, 1)
                    dve.wait_ge(rsum_ready, k * UNITS + s + 1)
                    dve.tensor_scalar(probs[:, s % 4, :], probs[:, s % 4, :], rsum[:, s % 4:s % 4 + 1], None,
                                      ALU.mult).then_inc(probs_ready, 1)

                def out_lo(k, u):
                    b, h, _ = unit(2 * u)
                    dve.wait_ge(out_hi_ready, k * OUTS + u + 1)
                    at = slice(b * SEQ, (b + 1) * SEQ)
                    dve.tensor_tensor(outT.lo[:, h, at], core.outp[u % 2][:, 0:SEQ],
                                      outT.hi[:, h, at].bitcast(F32), ALU.subtract).then_inc(outp_free, 1)

                def iteration(k, par, project, attend, split):
                    for c in range(TC):
                        if attend and c - 1 in OUT_STEPS:
                            add_out(k, OUT_STEPS[c - 1], project)
                        if project:
                            if c == 0:
                                dve.wait_ge(bias_loaded[1 - par], 48 * bias_round(k, par))
                            n, bank = proj_use(k, ("qk", c), project, attend)
                            dve.wait_ge(proj_ready, n + 1)
                            dve.tensor_tensor(tok[:, c % 3, :], bank[:, :], bias[:, 1 - par, 0:2 * W],
                                              ALU.add).then_inc(proj_free, 1)
                            n, bank = proj_use(k, ("v", c), project, attend)
                            dve.wait_ge(proj_ready, n + 1)
                            dve.tensor_tensor(v[:, 1 - par, c, :], bank[:, 0:W],
                                              bias[:, 1 - par, 2 * W:3 * W], ALU.add).then_inc(proj_free, 1)
                            dve.wait_ge(sq_ready, (k + 1) * TC + c + 1)
                            dve.tensor_reduce(ss[:, c % 2, :], sq[:].rearrange("p (h d) -> p h d", d=P),
                                              AX.X, ALU.add).then_inc(ss_ready, 1)
                            if c >= 1:
                                normalise(k, c - 1)
                        if attend:
                            for s in (2 * c, 2 * c + 1):
                                if s >= 1:
                                    divide(k, s - 1)
                                dve.wait_ge(score_ready, k * UNITS + s + 1)
                                dve.tensor_reduce(nmax[:, s % 4:s % 4 + 1], core.score[s % 2][:, 0:SEQ],
                                                  AX.X, ALU.max, negate=True).then_inc(max_ready, 1)
                                if s >= 5 and s % 2 == 1:
                                    out_lo(k, (s - 5) // 2)
                    if attend:
                        divide(k, UNITS - 1)
                        add_out(k, OUT_STEPS[TC - 1], project)
                        out_lo(k, OUTS - 2)
                        add_out(k, len(OUT_STEPS), project)
                    if project:
                        normalise(k, TC - 1)
                    if attend:
                        out_lo(k, OUTS - 1)
                        for i in range(len(OUT_STEPS) + 1, TC):
                            add_out(k, i, project)

                def add_out(k, i, project):
                    n, bank = proj_use(k, ("out", i), project, True)
                    dve.wait_ge(proj_ready, n + 1)
                    dve.tensor_tensor(core.x[:, i, :], bank[:, :], core.x[:, i, :], ALU.add).then_inc(proj_free, 1)

                def bias_round(k, par):
                    if isinstance(k, int):
                        return (k + 1) // 2 + 1
                    return (k - par) // 2 + 1 + par

                all_iterations(dve, iteration)

            @block.scalar
            def _(act):
                act.sem_inc(turn_free, RING)
                act.sem_inc(score_free, RING)

                def split_w(g, par, piece):
                    if piece == 0:
                        act.wait_ge(raw_loaded, (g + 1) * 48)
                    act.copy(w.hi[:, par, piece, :], raw[:, piece, :]).then_inc(w_hi_ready, 1)

                def qk_out(k, c, par, project, attend):
                    n, bank = turn_use(k, ("qk", c), project, attend)
                    act.wait_ge(turn_ready, n + 1)
                    at = slice(c * P, (c + 1) * P)
                    q, kk = (core.turn[bank][:, j * W:(j + 1) * W].rearrange("p (h t) -> p h t", t=P) for j in range(2))
                    act.activation(qT[:, 1 - par, :, at], q, ACT.Copy, scale=gain[:, 0:1])
                    act.copy(kT[:, 1 - par, :, at], kk).then_inc(turn_free, 1)

                def probs_out(k, s, project, attend):
                    n, bank = turn_use(k, ("probs", s), project, attend)
                    act.wait_ge(turn_ready, n + 1)
                    qc = s % QC
                    act.copy(probsT[:, s // QC % 2, :, qc * P:(qc + 1) * P],
                             core.turn[bank][:, 0:SEQ].rearrange("p (k t) -> p k t", t=P)).then_inc(turn_free, 1)

                def out_hi(k, u):
                    b, h, _ = unit(2 * u)
                    act.wait_ge(outp_ready, k * OUTS + u + 1)
                    act.copy(outT.hi[:, h, b * SEQ:(b + 1) * SEQ], core.outp[u % 2][:, 0:SEQ])\
                        .then_inc(out_hi_ready, 1)

                def iteration(k, par, project, attend, split):
                    for c in range(TC):
                        if project:
                            n, _ = proj_use(k, ("qk", c), project, attend)
                            act.wait_ge(proj_free, n + 1 + RING)
                            if not (isinstance(k, int) and k < 0 and c == 0):
                                act.wait_ge(ss_ready, (k + 1) * TC + c)
                            act.activation(sq[:], tok[:, c % 3, :], ACT.Square,
                                           scale=float(P) ** -0.5).then_inc(sq_ready, 1)
                            if c >= 2:
                                qk_out(k, c - 2, par, project, attend)
                        if split and c < PIECES:
                            split_w(k + 2, par, c)
                        if attend and c == 1:
                            act.wait_ge(raw_o_loaded, (k + 1) * 16)
                            act.copy(wo.hi[:], raw_o[:]).then_inc(wo_hi_ready, 1)
                        if attend:
                            for s in (2 * c, 2 * c + 1):
                                act.wait_ge(max_ready, k * UNITS + s + 1)
                                act.activation(probs[:, s % 4, :], core.score[s % 2][:, 0:SEQ], ACT.Exp,
                                               bias=nmax[:, s % 4:s % 4 + 1],
                                               accum_out=sums[:, s % 4:s % 4 + 1]).then_inc(score_free, 1)
                                if s >= 2:
                                    probs_out(k, s - 2, project, attend)
                                if s >= 5 and s % 2 == 1:
                                    out_hi(k, (s - 5) // 2)
                    if attend:
                        probs_out(k, UNITS - 2, project, attend)
                        out_hi(k, OUTS - 2)
                        probs_out(k, UNITS - 1, project, attend)
                        out_hi(k, OUTS - 1)
                    if project:
                        for c in (TC - 2, TC - 1):
                            qk_out(k, c, par, project, attend)

                for piece in range(PIECES):
                    split_w(0, 0, piece)
                norm.scalar(act)
                act.wait_ge(gain_ready, 1)
                all_iterations(act, iteration)

            @block.tensor
            def _(pe):
                def project_chunk(k, c, par, project, attend):
                    at = slice(c * P, (c + 1) * P)
                    for what, cols in (("qk", slice(0, 2 * W)), ("v", slice(2 * W, 3 * W))):
                        n, bank = proj_use(k, (what, c), project, attend)
                        pe.wait_ge(proj_free, n + 1)
                        out = bank[:, 0:cols.stop - cols.start]
                        for i in range(KC):
                            last = product(pe, out, hT.hi[:, i, at], hT.lo[:, i, at],
                                           w.hi[:, 1 - par, i, cols], w.lo[:, 1 - par, i, cols],
                                           start=(i == 0), stop=(i == KC - 1))
                        last.then_inc(proj_ready, 1)

                def qk_turn(k, c, project, attend):
                    n, bank = turn_use(k, ("qk", c), project, attend)
                    pe.wait_ge(qk_normed, (k + 1) * TC + c + 1)
                    pe.wait_ge(turn_free, n + 1)
                    for h in range(2 * HPG):
                        last = pe.transpose(core.turn[bank][:, h * P:(h + 1) * P],
                                            tok[:, c % 3, h * P:(h + 1) * P], core.ident[:])
                    last.then_inc(turn_ready, 1)

                def scores(k, s, par):
                    b, h, qc = unit(s)
                    t0 = b * SEQ + qc * P
                    pe.wait_ge(score_free, k * UNITS + s + 1)
                    pe.matmul(core.score[s % 2][:, 0:SEQ], qT[:, par, h, t0:t0 + P],
                              kT[:, par, h, b * SEQ:(b + 1) * SEQ], start=True, stop=True).then_inc(score_ready, 1)

                def probs_turn(k, s, project, attend):
                    n, bank = turn_use(k, ("probs", s), project, attend)
                    pe.wait_ge(probs_ready, k * UNITS + s + 1)
                    pe.wait_ge(turn_free, n + 1)
                    for i in range(QC):
                        last = pe.transpose(core.turn[bank][:, i * P:(i + 1) * P],
                                            probs[:, s % 4, i * P:(i + 1) * P], core.ident[:])
                    last.then_inc(turn_ready, 1)

                def weigh(k, u, par, project, attend):
                    b, h, _ = unit(2 * u)
                    n, _ = turn_use(k, ("probs", 2 * u + 1), project, attend)
                    pe.wait_ge(turn_free, n + 1 + RING)
                    pe.wait_ge(outp_free, k * OUTS + u + 1)
                    for i in range(QC):
                        last = pe.matmul(core.outp[u % 2][:, 0:SEQ], v[:, par, QC * b + i, h * P:(h + 1) * P],
                                         probsT[:, u % 2, i, :], start=(i == 0), stop=(i == QC - 1))
                    last.then_inc(outp_ready, 1)

                def output(k, i, project):
                    if i % QC == 0:
                        pe.wait_ge(outp_free, k * OUTS + (i // QC + 1) * HPG + RING)
                    if i == 0:
                        pe.wait_ge(wo_ready, k + 1)
                    n, bank = proj_use(k, ("out", i), project, True)
                    pe.wait_ge(proj_free, n + 1)
                    at = slice(i * P, (i + 1) * P)
                    for h in range(HPG):
                        last = product(pe, bank[:, :], outT.hi[:, h, at], outT.lo[:, h, at],
                                       wo.hi[:, h, :], wo.lo[:, h, :], start=(h == 0), stop=(h == HPG - 1))
                    last.then_inc(proj_ready, 1)

                def iteration(k, par, project, attend, split):
                    if project:
                        pe.wait_ge(w_ready, (k + 2) * PIECES)
                    for c in range(TC):
                        if project:
                            project_chunk(k, c, par, project, attend)
                            if c >= 2:
                                qk_turn(k, c - 2, project, attend)
                        if attend:
                            if c == 0:
                                pe.wait_ge(turn_free, turn_base(k) + RING)
                                pe.wait_ge(proj_free, proj_base(k) + RING)
                            for s in (2 * c, 2 * c + 1):
                                scores(k, s, par)
                                if s >= 2:
                                    probs_turn(k, s - 2, project, attend)
                                if s >= 4 and s % 2 == 0:
                                    weigh(k, (s - 4) // 2, par, project, attend)
                            if c in OUT_STEPS:
                                output(k, OUT_STEPS[c], project)
                    if attend:
                        probs_turn(k, UNITS - 2, project, attend)
                        weigh(k, OUTS - 2, par, project, attend)
                        output(k, len(OUT_STEPS), project)
                        probs_turn(k, UNITS - 1, project, attend)
                        output(k, len(OUT_STEPS) + 1, project)
                        weigh(k, OUTS - 1, par, project, attend)
                    if project:
                        for c in (TC - 2, TC - 1):
                            qk_turn(k, c, project, attend)
                    if attend:
                        for i in range(len(OUT_STEPS) + 2, TC):
                            output(k, i, project)

                def turn_base(k):
                    return TC + k * len(TURNS)

                norm.tensor(pe)
                pe.wait_ge(norm.hT_ready, norm.hT_done)
                all_iterations(pe, iteration)


def context_attention(nc, core, io, name, eps):
    GROUPS = 8
    W = HG * P
    KCH = B * CTX // P
    ITEMS = KCH + TC
    ROWS = B * QC
    PIECES = KC
    SCORES = {2 * h: h for h in range(HG)}
    PROBS = {2 * h + 2: h for h in range(HG)}
    WEIGH = {2 * h + 3: h for h in range(HG)}
    TURNS = []
    for c in range(ITEMS):
        TURNS += [("item", c - 2)] * (c >= 2)
        TURNS += [("probs", PROBS[c])] if c in PROBS else []
    TURNS += [("item", ITEMS - 2), ("item", ITEMS - 1)]

    with ExitStack() as ctx:
        sb = lambda n, shape: ctx.enter_context(nc.sbuf_tensor(f"{name}_{n}", shape, F32))
        sem = lambda n: core.hold.enter_context(nc.semaphore(f"{name}_{n}"))
        hT = Pair(nc, ctx, f"{name}_hT", [P, KC, T])
        ctxT = Pair(nc, ctx, f"{name}_ctxT", [P, KC, B * CTX])
        w = Pair(nc, ctx, f"{name}_w", [P, KC, W + 2 * P])
        raw = sb("raw", [P, KC, W + 2 * P])
        raw_o = sb("raw_o", [P, HG, D])
        wo = Pair(nc, ctx, f"{name}_wo", [P, HG, D])
        mask = sb("mask", [P, B // 2, QC, 2, CTX])
        gains = sb("gains", [P, 2])
        gain = sb("gain", [P, 1])
        epsilon = sb("epsilon", [P, HG])
        tok = sb("tok", [P, 3, W])
        sq = sb("sq", [P, W])
        ss = sb("ss", [P, 2, HG])
        ms = sb("ms", [P, 2, HG])
        rms = sb("rms", [P, 2, HG])
        qT = sb("qT", [P, 2, HG, T])
        raw_ctx = qT[:, 1, 0, :].rearrange("p (k n) -> p k n", k=KC)
        kT = sb("kT", [P, 2, B * CTX])
        v = sb("v", [P, 2, KCH, P])
        logits = sb("logits", [P, ROWS * CTX])
        exps = sb("exps", [P, 2, ROWS * CTX])
        core.h = exps
        top = sb("top", [P, 2, ROWS])
        total = sb("total", [P, 2, ROWS])
        turned = sb("turned", [P, B // 2, SEQ])
        outT = Pair(nc, ctx, f"{name}_outT", [P, HG, T])

        ctx_loaded = sem("ctx_loaded")
        ctx_hi_ready = sem("ctx_hi_ready")
        ctx_ready = sem("ctx_ready")
        gain_loaded = sem("gain_loaded")
        mask_loaded = sem("mask_loaded")
        const_ready = sem("const_ready")
        gain_ready = sem("gain_ready")
        w_loaded = sem("w_loaded")
        wo_loaded = sem("wo_loaded")
        w_hi_ready = sem("w_hi_ready")
        w_ready = sem("w_ready")
        wo_hi_ready = sem("wo_hi_ready")
        wo_ready = sem("wo_ready")
        proj_ready = sem("proj_ready")
        proj_free = sem("proj_free")
        sq_ready = sem("sq_ready")
        ss_ready = sem("ss_ready")
        ms_ready = sem("ms_ready")
        rms_ready = sem("rms_ready")
        normed = sem("normed")
        turn_ready = sem("turn_ready")
        turn_free = sem("turn_free")
        score_ready = sem("score_ready")
        score_free = sem("score_free")
        max_ready = sem("max_ready")
        shifted_ready = sem("shifted_ready")
        exps_ready = sem("exps_ready")
        total_ready = sem("total_ready")
        rsum_ready = sem("rsum_ready")
        probs_ready = sem("probs_ready")
        outp_ready = sem("outp_ready")
        out_hi_ready = sem("out_hi_ready")
        outp_free = sem("outp_free")

        norm = Norm(core, pair=hT)
        w_dram = [io[f"L0_xattn_{n}"].rearrange("(k p) n -> p k n", p=P) for n in "qkv"]
        wo_dram = io["L0_xattn_o"].rearrange("(n p) d -> p n d", p=P)

        heads = lambda n: 1 if n < KCH else HG
        proj_base = lambda k: ITEMS + k * (ITEMS + TC) if not isinstance(k, int) or k >= 0 else 0
        out_use = lambda k, i, project: proj_base(k) + (ITEMS if project else 0) + i

        def turn_use(k, what, project, attend):
            order = [t for t in TURNS if (t[0] == "item" and project) or (t[0] == "probs" and attend)]
            n = order.index(what)
            base = ITEMS + k * len(TURNS) if not isinstance(k, int) or k >= 0 else 0
            return base + n, n % 2

        def all_iterations(engine, iteration):
            iteration(-1, 1, True, False, True)
            with engine.Fori(0, (GROUPS - 2) // 2) as i:
                for par in range(2):
                    iteration(i * 2 + par, par, True, True, True)
            iteration(GROUPS - 2, 0, True, True, False)
            iteration(GROUPS - 1, 1, False, True, False)

        with nc.Block() as block:

            @block.sync
            def _(sp):
                def load_w(g):
                    for j, (at, n) in enumerate(((0, W), (W, P), (W + P, P))):
                        sp.dma_start(raw[:, :, at:at + n], w_dram[j][:, :, ds(g * n, n)]).then_inc(w_loaded, 16)

                def load_wo(g):
                    sp.dma_start(raw_o[:], wo_dram[:, ds(g * HG, HG), :]).then_inc(wo_loaded, 16)

                sp.dma_start(raw_ctx, io["ctxT"].rearrange("(k p) n -> p k n", p=P)).then_inc(ctx_loaded, 16)
                load_w(0)
                sp.dma_start(gains[:, 0:1], io["L0_xattn_gq"].unsqueeze(1)).then_inc(gain_loaded, 16)
                sp.dma_start(gains[:, 1:2], io["L0_xattn_gk"].unsqueeze(1)).then_inc(gain_loaded, 16)
                for a in range(B // 2):
                    for b in range(2):
                        sp.dma_start(mask[:, a, :, b, :], io["mask"].rearrange("(c p) k -> p c k", p=P))\
                            .then_inc(mask_loaded, 16)
                load_wo(0)

                def loads(k):
                    sp.wait_ge(w_ready, (k + 2) * PIECES)
                    load_w(k + 2)
                    sp.wait_ge(wo_ready, (k + 1) * HG)
                    load_wo(k + 1)

                sp.wait_ge(w_ready, PIECES)
                load_w(1)
                with sp.Fori(0, GROUPS - 2) as k:
                    loads(k)
                sp.wait_ge(wo_ready, (GROUPS - 1) * HG)
                load_wo(GROUPS - 1)

            @block.gpsimd
            def _(pool):
                pool.memset(epsilon[:], eps).then_inc(const_ready, 1)
                pool.wait_ge(const_ready, 1)
                norm.gpsimd(pool)

                def split_w(g):
                    for piece in range(PIECES):
                        pool.wait_ge(w_hi_ready, g * PIECES + piece + 1)
                        pool.tensor_tensor(w.lo[:, piece, :], raw[:, piece, :], w.hi[:, piece, :].bitcast(F32),
                                           ALU.subtract).then_inc(w_ready, 1)

                def iteration(k, par, project, attend, split):
                    for c in range(ITEMS):
                        if project:
                            n, hs = (k + 1) * ITEMS + c, heads(c)
                            pool.wait_ge(ss_ready, n + 1)
                            pool.tensor_tensor(ms[:, c % 2, 0:hs], ss[:, c % 2, 0:hs], epsilon[:, 0:hs], ALU.add)\
                                .then_inc(ms_ready, 1)
                            pool.wait_ge(ms_ready, n + 1)
                            pool.tensor_tensor(rms[:, c % 2, 0:hs], ms[:, c % 2, 0:hs], core.neg_half[:, 0:hs],
                                               ALU.pow).then_inc(rms_ready, 1)
                        if attend and c < HG:
                            pool.wait_ge(wo_hi_ready, k * HG + c + 1)
                            pool.tensor_tensor(wo.lo[:, c, :], raw_o[:, c, :], wo.hi[:, c, :].bitcast(F32),
                                               ALU.subtract).then_inc(wo_ready, 1)
                    if split:
                        split_w(k + 2)

                pool.wait_ge(ctx_hi_ready, 1)
                pool.tensor_tensor(ctxT.lo[:], raw_ctx, ctxT.hi[:].bitcast(F32), ALU.subtract).then_inc(ctx_ready, 1)
                split_w(0)
                all_iterations(pool, iteration)

            @block.vector
            def _(dve):
                rows = lambda a: a.rearrange("p (r k) -> p r k", k=CTX)
                each = lambda a: a.unsqueeze(2).broadcast_to([P, ROWS, CTX])
                norm.vector(dve)
                dve.wait_ge(gain_loaded, 32)
                dve.scalar_tensor_tensor(gain[:], gains[:, 0:1], float(P) ** -0.5, gains[:, 1:2],
                                         ALU.mult, ALU.mult).then_inc(gain_ready, 1)
                dve.wait_ge(mask_loaded, 16 * B)

                def normalise(k, c):
                    hs = heads(c)
                    dve.wait_ge(rms_ready, (k + 1) * ITEMS + c + 1)
                    t = tok[:, c % 3, 0:hs * P].rearrange("p (h d) -> p h d", d=P)
                    dve.tensor_tensor(t, t, rms[:, c % 2, 0:hs].unsqueeze(2).broadcast_to([P, hs, P]),
                                      ALU.mult).then_inc(normed, 1)

                def shift(k, h):
                    s = h % 2
                    dve.wait_ge(score_ready, k * HG + h + 1)
                    dve.tensor_tensor(logits[:], core.score[s][:, :],
                                      mask[:].rearrange("p a q b k -> p (a q b k)"), ALU.add).then_inc(score_free, 1)
                    dve.wait_ge(score_free, k * HG + h + 1 + RING)
                    dve.tensor_reduce(top[:, s, :], rows(logits[:]), AX.X, ALU.max).then_inc(max_ready, 1)
                    dve.wait_ge(max_ready, k * HG + h + 1)
                    dve.tensor_tensor(rows(logits[:]), rows(logits[:]), each(top[:, s, :]),
                                      ALU.subtract).then_inc(shifted_ready, 1)

                def divide(k, h):
                    s = h % 2
                    dve.wait_ge(exps_ready, k * HG + h + 1)
                    dve.tensor_reduce(total[:, s, :], rows(exps[:, s, :]), AX.X, ALU.add).then_inc(total_ready, 1)
                    dve.wait_ge(total_ready, k * HG + h + 1)
                    dve.reciprocal(total[:, s, :], total[:, s, :]).then_inc(rsum_ready, 1)
                    dve.wait_ge(rsum_ready, k * HG + h + 1)
                    dve.tensor_tensor(rows(exps[:, s, :]), rows(exps[:, s, :]), each(total[:, s, :]),
                                      ALU.mult).then_inc(probs_ready, 1)

                def out_lo(k, h):
                    dve.wait_ge(out_hi_ready, k * HG + h + 1)
                    hi, lo = (o[:, h, :].rearrange("p (a b t) -> p a b t", a=B // 2, b=2) for o in (outT.hi, outT.lo))
                    for b in range(2):
                        last = dve.tensor_tensor(lo[:, :, b, :], core.outp[b][:, :].rearrange("p (a t) -> p a t", t=SEQ),
                                                 hi[:, :, b, :].bitcast(F32), ALU.subtract)
                    last.then_inc(outp_free, 1)

                def iteration(k, par, project, attend, split):
                    for c in range(ITEMS):
                        if project:
                            hs = heads(c)
                            dve.wait_ge(sq_ready, (k + 1) * ITEMS + c + 1)
                            dve.tensor_reduce(ss[:, c % 2, 0:hs], sq[:, 0:hs * P].rearrange("p (h d) -> p h d", d=P),
                                              AX.X, ALU.add).then_inc(ss_ready, 1)
                            if c >= 1:
                                normalise(k, c - 1)
                        if attend:
                            if c in SCORES:
                                shift(k, SCORES[c])
                            if c - 1 in SCORES:
                                divide(k, SCORES[c - 1])
                            if c in WEIGH:
                                out_lo(k, WEIGH[c])
                    if project:
                        normalise(k, ITEMS - 1)
                    if attend:
                        for i in range(TC):
                            dve.wait_ge(proj_ready, out_use(k, i, project) + 1)
                            dve.tensor_tensor(core.x[:, i, :], core.proj[i % 2][:, :], core.x[:, i, :],
                                              ALU.add).then_inc(proj_free, 1)

                all_iterations(dve, iteration)

            @block.scalar
            def _(act):
                act.sem_inc(turn_free, RING)
                act.sem_inc(score_free, RING)
                act.sem_inc(proj_free, RING)
                act.sem_inc(outp_free, 1)

                def split_w(g):
                    act.wait_ge(w_loaded, (g + 1) * 48)
                    for piece in range(PIECES):
                        act.copy(w.hi[:, piece, :], raw[:, piece, :]).then_inc(w_hi_ready, 1)

                def item_out(k, c, par):
                    act.wait_ge(proj_ready, proj_base(k) + c + 1)
                    hs = heads(c)
                    if c < KCH:
                        act.copy(v[:, 1 - par, c, :], core.proj[c % 2][:, P:2 * P])
                    act.copy(tok[:, c % 3, 0:hs * P], core.proj[c % 2][:, 0:hs * P]).then_inc(proj_free, 1)
                    act.wait_ge(proj_free, proj_base(k) + c + 1 + RING)
                    if not (isinstance(k, int) and k < 0 and c == 0):
                        act.wait_ge(ss_ready, (k + 1) * ITEMS + c)
                    act.activation(sq[:, 0:hs * P], tok[:, c % 3, 0:hs * P], ACT.Square,
                                   scale=float(P) ** -0.5).then_inc(sq_ready, 1)

                def turn_out(k, c, par, project, attend):
                    n, bank = turn_use(k, ("item", c), project, attend)
                    act.wait_ge(turn_ready, n + 1)
                    if c < KCH:
                        ins = act.copy(kT[:, 1 - par, c * P:(c + 1) * P], core.turn[bank][:, 0:P])
                    else:
                        ins = act.activation(qT[:, 1 - par, :, (c - KCH) * P:(c - KCH + 1) * P],
                                             core.turn[bank][:, :].rearrange("p (h t) -> p h t", t=P),
                                             ACT.Copy, scale=gain[:, 0:1])
                    ins.then_inc(turn_free, 1)

                def iteration(k, par, project, attend, split):
                    for c in range(ITEMS):
                        if project:
                            item_out(k, c, par)
                            if c >= 2:
                                turn_out(k, c - 2, par, project, attend)
                        if attend and c < HG:
                            if c == 0:
                                act.wait_ge(proj_ready, proj_base(k))
                                act.wait_ge(wo_loaded, (k + 1) * 16)
                            act.copy(wo.hi[:, c, :], raw_o[:, c, :]).then_inc(wo_hi_ready, 1)
                        if attend:
                            if c in SCORES:
                                h = SCORES[c]
                                act.wait_ge(shifted_ready, k * HG + h + 1)
                                act.activation(exps[:, h % 2, :], logits[:], ACT.Exp).then_inc(exps_ready, 1)
                            if c in PROBS:
                                h = PROBS[c]
                                n, bank = turn_use(k, ("probs", h), project, attend)
                                act.wait_ge(turn_ready, n + 1)
                                act.copy(turned[:].rearrange("p a q -> p (a q)"), core.turn[bank][:, :])\
                                    .then_inc(turn_free, 1)
                            if c in WEIGH:
                                h = WEIGH[c]
                                act.wait_ge(outp_ready, k * HG + h + 1)
                                hi = outT.hi[:, h, :].rearrange("p (a b t) -> p a b t", a=B // 2, b=2)
                                for b in range(2):
                                    last = act.copy(hi[:, :, b, :], core.outp[b][:, :].rearrange("p (a t) -> p a t", t=SEQ))
                                last.then_inc(out_hi_ready, 1)
                    if project:
                        for c in (ITEMS - 2, ITEMS - 1):
                            turn_out(k, c, par, project, attend)
                    if split:
                        split_w(k + 2)

                act.wait_ge(ctx_loaded, 16)
                act.copy(ctxT.hi[:], raw_ctx).then_inc(ctx_hi_ready, 1)
                split_w(0)
                norm.scalar(act)
                act.wait_ge(gain_ready, 1)
                all_iterations(act, iteration)

            @block.tensor
            def _(pe):
                def project_item(k, c):
                    pe.wait_ge(proj_free, proj_base(k) + c + 1)
                    src, i, cols = (ctxT, c, slice(W, W + 2 * P)) if c < KCH else (hT, c - KCH, slice(0, W))
                    at = slice(i * P, (i + 1) * P)
                    for j in range(KC):
                        last = product(pe, core.proj[c % 2][:, 0:cols.stop - cols.start], src.hi[:, j, at],
                                       src.lo[:, j, at], w.hi[:, j, cols], w.lo[:, j, cols],
                                       start=(j == 0), stop=(j == KC - 1))
                    last.then_inc(proj_ready, 1)

                def turn_item(k, c, project, attend):
                    n, bank = turn_use(k, ("item", c), project, attend)
                    pe.wait_ge(normed, (k + 1) * ITEMS + c + 1)
                    pe.wait_ge(turn_free, n + 1)
                    for h in range(heads(c)):
                        last = pe.transpose(core.turn[bank][:, h * P:(h + 1) * P],
                                            tok[:, c % 3, h * P:(h + 1) * P], core.ident[:])
                    last.then_inc(turn_ready, 1)

                def scores(k, h, par):
                    pe.wait_ge(score_free, k * HG + h + 1)
                    for b in range(B):
                        for qc in range(QC):
                            t0 = b * SEQ + qc * P
                            at = ((b // 2 * QC + qc) * 2 + b % 2) * CTX
                            last = pe.matmul(core.score[h % 2][:, at:at + CTX], qT[:, par, h, t0:t0 + P],
                                             kT[:, par, b * CTX:(b + 1) * CTX], start=True, stop=True)
                    last.then_inc(score_ready, 1)

                def turn_probs(k, h, project, attend):
                    n, bank = turn_use(k, ("probs", h), project, attend)
                    pe.wait_ge(probs_ready, k * HG + h + 1)
                    pe.wait_ge(turn_free, n + 1)
                    for a in range(B // 2 * QC):
                        last = pe.transpose(core.turn[bank][:, a * P:(a + 1) * P],
                                            exps[:, h % 2, a * P:(a + 1) * P], core.ident[:])
                    last.then_inc(turn_ready, 1)

                def weigh(k, h, par, project, attend):
                    n, _ = turn_use(k, ("probs", h), project, attend)
                    pe.wait_ge(turn_free, n + 1 + RING)
                    pe.wait_ge(outp_free, k * HG + h + 1)
                    for b in range(B):
                        rows = slice(b % 2 * CTX, (b % 2 + 1) * CTX)
                        last = pe.matmul(core.outp[b % 2][:, b // 2 * SEQ:(b // 2 + 1) * SEQ],
                                         v[rows, par, b // 2, :], turned[rows, b // 2, :],
                                         start=True, stop=True)
                    last.then_inc(outp_ready, 1)

                def output(k, i, project):
                    if i == 0:
                        pe.wait_ge(wo_ready, (k + 1) * HG)
                    pe.wait_ge(proj_free, out_use(k, i, project) + 1)
                    at = slice(i * P, (i + 1) * P)
                    for h in range(HG):
                        if i == 0:
                            pe.wait_ge(outp_free, k * HG + h + 2)
                        last = product(pe, core.proj[i % 2][:, :], outT.hi[:, h, at], outT.lo[:, h, at],
                                       wo.hi[:, h, :], wo.lo[:, h, :], start=(h == 0), stop=(h == HG - 1))
                    last.then_inc(proj_ready, 1)

                def iteration(k, par, project, attend, split):
                    if attend:
                        pe.wait_ge(turn_free, ITEMS + k * len(TURNS) + RING)
                        pe.wait_ge(proj_free, proj_base(k) + RING)
                    if project:
                        pe.wait_ge(w_ready, (k + 2) * PIECES)
                    for c in range(ITEMS):
                        if project:
                            project_item(k, c)
                            if c >= 2:
                                turn_item(k, c - 2, project, attend)
                        if attend:
                            if c in SCORES:
                                scores(k, SCORES[c], par)
                            if c in PROBS:
                                turn_probs(k, PROBS[c], project, attend)
                            if c in WEIGH:
                                weigh(k, WEIGH[c], par, project, attend)
                    if project:
                        turn_item(k, ITEMS - 2, project, attend)
                    if attend:
                        output(k, 0, project)
                    if project:
                        turn_item(k, ITEMS - 1, project, attend)
                    if attend:
                        for i in range(1, TC):
                            output(k, i, project)

                norm.tensor(pe)
                pe.wait_ge(norm.hT_ready, norm.hT_done)
                pe.wait_ge(ctx_ready, 1)
                all_iterations(pe, iteration)


def latent_attention(nc, core, io, name):
    GROUPS, DH = 4, 96
    KEYS = SEQ + CTX
    KEY_CHUNKS = [P, P, CTX]
    W = HG * DH
    UNITS = HG * B * QC
    OUTS = UNITS // QC
    HALVES = T // D
    STEPS = HG * HALVES
    PER_STEP = UNITS // STEPS
    Q_STEPS = {c: ((c - HALVES) // HALVES, c % HALVES) for c in range(HALVES, STEPS)}
    WO_STEPS = {1: 0, 2: 1, 4: 2, 5: 3}
    TAIL = [("k", b) for b in range(B)] + [("q", HG - 1, i) for i in range(HALVES)]
    PROJ = [("q", *Q_STEPS[c]) for c in sorted(Q_STEPS)] + TAIL + [("out", i) for i in range(TC)]
    FIRST = [("v", i) for i in range(TC)] + [("vc", b) for b in range(B)] + [("k", b) for b in range(B)] \
        + [("q", h, i) for h in range(HG) for i in range(HALVES)]

    with ExitStack() as ctx:
        sb = lambda n, shape: ctx.enter_context(nc.sbuf_tensor(f"{name}_{n}", shape, F32))
        sem = lambda n: core.hold.enter_context(nc.semaphore(f"{name}_{n}"))
        hT = Pair(nc, ctx, f"{name}_hT", [P, KC, B * KEYS])
        raw = sb("raw", [P, KC, W + DH])
        w = Pair(nc, ctx, f"{name}_w", [P, KC, W + DH])
        raw_o = sb("raw_o", [P, HG // 2, D])
        raw_ctx = raw_o[:].rearrange("p h (k n) -> p (h k) n", n=B * CTX)[:, 0:KC, :]
        wo = Pair(nc, ctx, f"{name}_wo", [DH, HG, D])
        qT = Pair(nc, ctx, f"{name}_qT", [DH, HG, T])
        kT = Pair(nc, ctx, f"{name}_kT", [DH, B, KEYS])
        v = sb("v", [P, TC, W])
        vc = sb("vc", [CTX, B, W])
        vg = sb("vg", [P, TC, DH])
        vcg = sb("vcg", [CTX, B, DH])
        probs = sb("probs", [P, 4, KEYS])
        core.h = probs[:].rearrange("p a k -> p (a k)")[:, 0:2 * D].rearrange("p (a d) -> p a d", a=2)
        nmax = sb("nmax", [P, 4])
        sums = sb("sums", [P, 4])
        rsum = sb("rsum", [P, 4])
        probsT = sb("probsT", [P, 2, len(KEY_CHUNKS), SEQ])
        outT = Pair(nc, ctx, f"{name}_outT", [DH, HG, T])

        ctx_loaded = sem("ctx_loaded")
        ctx_hi_ready = sem("ctx_hi_ready")
        ctx_ready = sem("ctx_ready")
        w_loaded = sem("w_loaded")
        w_hi_ready = sem("w_hi_ready")
        w_ready = sem("w_ready")
        wo_loaded = sem("wo_loaded")
        wo_hi_ready = sem("wo_hi_ready")
        wo_ready = sem("wo_ready")
        proj_ready = sem("proj_ready")
        proj_hi_ready = sem("proj_hi_ready")
        proj_free = sem("proj_free")
        vg_ready = sem("vg_ready")
        turn_ready = sem("turn_ready")
        turn_free = sem("turn_free")
        score_ready = sem("score_ready")
        score_free = sem("score_free")
        max_ready = sem("max_ready")
        rsum_ready = sem("rsum_ready")
        probs_ready = sem("probs_ready")
        outp_ready = sem("outp_ready")
        out_hi_ready = sem("out_hi_ready")
        outp_free = sem("outp_free")

        column = lambda i: i // QC * KEYS + i % QC * P
        norm = Norm(core, pair=hT, column=column)
        w_dram = [io[f"L1_xattn_{n}"].rearrange("(k p) n -> p k n", p=P) for n in "qkv"]
        wo_dram = io["L1_xattn_o"].rearrange("(n p) d -> p n d", p=DH)
        batches = lambda tile: tile.rearrange("p k (b s) -> p k b s", s=KEYS)
        context = lambda tile: batches(tile)[:, :, :, SEQ:KEYS]
        by_batch = lambda tile: tile.rearrange("p k (b n) -> p k b n", n=CTX)

        first = lambda k: isinstance(k, int) and k < 0
        proj_base = lambda k: 0 if first(k) else len(FIRST) + k * len(PROJ)
        PAIRS = len(TAIL) + len(Q_STEPS)
        pair_base = lambda k: 0 if first(k) else (k + 1) * PAIRS
        unit = lambda s: (s // (B * QC), s // QC % B, s % QC)

        def order_of(k, project):
            return FIRST if first(k) else PROJ if project else [u for u in PROJ if u[0] == "out"]

        def proj_use(k, what, project):
            n = order_of(k, project).index(what)
            return proj_base(k) + n, core.proj[n % 2]

        def pair_use(k, what):
            return pair_base(k) + [u for u in order_of(k, True) if u[0] in "qk"].index(what)

        def pair_places(what, bank, tile):
            if what[0] == "k":
                return bank[0:DH, 0:KEYS], tile[1][:, what[1], :]
            return bank[0:DH, :], tile[0][:, what[1], what[2] * D:(what[2] + 1) * D]

        def all_iterations(engine, iteration):
            iteration(-1, True, False, True)
            with engine.Fori(0, GROUPS - 2) as k:
                iteration(k, True, True, True)
            iteration(GROUPS - 2, True, True, False)
            iteration(GROUPS - 1, False, True, False)

        with nc.Block() as block:

            @block.sync
            def _(sp):
                def load_w(g):
                    for j, (at, n) in enumerate(((0, W), (W, DH))):
                        sp.dma_start(raw[:, :, at:at + n], w_dram[j][:, :, ds(g * n, n)]).then_inc(w_loaded, 16)

                def load_wo(m):
                    sp.dma_start(raw_o[0:DH, :, :], wo_dram[:, ds(m * HG // 2, HG // 2), :]).then_inc(wo_loaded, 16)

                def next_wo(m):
                    sp.wait_ge(wo_ready, m * HG // 2)
                    load_wo(m)

                sp.dma_start(raw[:, :, 0:W], w_dram[2]).then_inc(w_loaded, 16)
                sp.dma_start(raw_ctx, io["ctxT"].rearrange("(k p) n -> p k n", p=P)).then_inc(ctx_loaded, 16)
                sp.wait_ge(w_ready, 1)
                load_w(0)
                sp.wait_ge(ctx_ready, 1)
                load_wo(0)
                sp.wait_ge(w_ready, 2)
                load_w(1)

                def loads(k):
                    next_wo(k * 2 + 1)
                    next_wo(k * 2 + 2)
                    sp.wait_ge(w_ready, k + 3)
                    load_w(k + 2)

                with sp.Fori(0, GROUPS - 2) as k:
                    loads(k)
                for m in range(2 * (GROUPS - 2) + 1, 2 * GROUPS):
                    next_wo(m)

            @block.gpsimd
            def _(pool):
                def split_w(n, cols):
                    pool.wait_ge(w_hi_ready, n + 1)
                    pool.tensor_tensor(w.lo[:, :, 0:cols], raw[:, :, 0:cols], w.hi[:, :, 0:cols].bitcast(F32),
                                       ALU.subtract).then_inc(w_ready, 1)

                def iteration(k, project, attend, split):
                    if attend:
                        for h in range(HG):
                            pool.wait_ge(wo_hi_ready, k * HG + h + 1)
                            pool.tensor_tensor(wo.lo[:, h, :], raw_o[0:DH, h % 2, :], wo.hi[:, h, :].bitcast(F32),
                                               ALU.subtract).then_inc(wo_ready, 1)
                    if split:
                        split_w(k + 3, W + DH)

                norm.gpsimd(pool)
                split_w(0, W)
                pool.wait_ge(ctx_hi_ready, 1)
                pool.tensor_tensor(context(hT.lo[:]), by_batch(raw_ctx), context(hT.hi[:]).bitcast(F32),
                                   ALU.subtract).then_inc(ctx_ready, 1)
                split_w(1, W + DH)
                all_iterations(pool, iteration)

            @block.vector
            def _(dve):
                dve.sem_inc(proj_free, RING)
                dve.sem_inc(outp_free, RING)
                norm.vector(dve)

                def copy_values(what):
                    n, bank = proj_use(-1, what, True)
                    dve.wait_ge(proj_ready, n + 1)
                    out = v[:, what[1], :] if what[0] == "v" else vc[:, what[1], :]
                    dve.tensor_copy(out, bank[0:P if what[0] == "v" else CTX, 0:W]).then_inc(proj_free, 1)

                def proj_lo(k, what):
                    _, bank = proj_use(k, what, True)
                    dve.wait_ge(proj_hi_ready, pair_use(k, what) + 1)
                    src, lo = pair_places(what, bank, (qT.lo, kT.lo))
                    _, hi = pair_places(what, bank, (qT.hi, kT.hi))
                    if what[0] == "k":
                        ins = dve.tensor_tensor(lo, src, hi.bitcast(F32), ALU.subtract)
                    else:
                        ins = dve.scalar_tensor_tensor(lo, src, float(DH) ** -0.5, hi.bitcast(F32),
                                                       ALU.mult, ALU.subtract)
                    ins.then_inc(proj_free, 1)

                def divide(k, s):
                    dve.wait_ge(score_free, k * UNITS + s + 1 + RING)
                    dve.reciprocal(rsum[:, s % 4:s % 4 + 1], sums[:, s % 4:s % 4 + 1]).then_inc(rsum_ready, 1)
                    dve.wait_ge(rsum_ready, k * UNITS + s + 1)
                    dve.tensor_scalar(probs[:, s % 4, :], probs[:, s % 4, :], rsum[:, s % 4:s % 4 + 1], None,
                                      ALU.mult).then_inc(probs_ready, 1)

                def out_lo(k, u):
                    h, b, _ = unit(2 * u)
                    dve.wait_ge(out_hi_ready, k * OUTS + u + 1)
                    at = slice(b * SEQ, (b + 1) * SEQ)
                    dve.tensor_tensor(outT.lo[:, h, at], core.outp[u % 2][0:DH, 0:SEQ],
                                      outT.hi[:, h, at].bitcast(F32), ALU.subtract).then_inc(outp_free, 1)

                def iteration(k, project, attend, split):
                    if not attend:
                        for what in FIRST:
                            if what[0] in "qk":
                                proj_lo(k, what)
                            else:
                                copy_values(what)
                        return
                    dve.tensor_copy(vg[:], v[:, :, ds(k * DH, DH)])
                    dve.tensor_copy(vcg[:], vc[:, :, ds(k * DH, DH)]).then_inc(vg_ready, 1)
                    for c in range(STEPS):
                        if project and c in Q_STEPS:
                            proj_lo(k, ("q", *Q_STEPS[c]))
                        for s in range(c * PER_STEP, (c + 1) * PER_STEP):
                            if s >= 1:
                                divide(k, s - 1)
                            dve.wait_ge(score_ready, k * UNITS + s + 1)
                            dve.tensor_reduce(nmax[:, s % 4:s % 4 + 1], core.score[s % 2][:, 0:KEYS],
                                              AX.X, ALU.max, negate=True).then_inc(max_ready, 1)
                            if s >= 5 and s % 2 == 1:
                                out_lo(k, (s - 5) // 2)
                    divide(k, UNITS - 1)
                    if project:
                        proj_lo(k, ("k", 0))
                    out_lo(k, OUTS - 2)
                    if project:
                        proj_lo(k, ("k", 1))
                    out_lo(k, OUTS - 1)
                    if project:
                        for what in TAIL[2:]:
                            proj_lo(k, what)
                    for i in range(TC):
                        n, bank = proj_use(k, ("out", i), project)
                        dve.wait_ge(proj_ready, n + 1)
                        dve.tensor_tensor(core.x[:, i, :], bank[:, :], core.x[:, i, :], ALU.add)\
                            .then_inc(proj_free, 1)

                all_iterations(dve, iteration)

            @block.scalar
            def _(act):
                act.sem_inc(turn_free, RING)
                act.sem_inc(score_free, RING)

                def proj_hi(k, what):
                    n, bank = proj_use(k, what, True)
                    act.wait_ge(proj_ready, n + 1)
                    src, hi = pair_places(what, bank, (qT.hi, kT.hi))
                    if what[0] == "k":
                        ins = act.copy(hi, src)
                    else:
                        ins = act.activation(hi, src, ACT.Copy, scale=float(DH) ** -0.5)
                    ins.then_inc(proj_hi_ready, 1)

                def split_w(n, cols):
                    act.wait_ge(w_loaded, 16 + n * 32)
                    act.copy(w.hi[:, :, 0:cols], raw[:, :, 0:cols]).then_inc(w_hi_ready, 1)

                def probs_out(k, s):
                    act.wait_ge(turn_ready, k * UNITS + s + 1)
                    qc, u, bank = s % QC, s // QC, core.turn[s % 2]
                    act.copy(probsT[:, u % 2, 0:2, qc * P:(qc + 1) * P],
                             bank[:, 0:2 * P].rearrange("p (k t) -> p k t", t=P))
                    act.copy(probsT[0:CTX, u % 2, 2, qc * P:(qc + 1) * P], bank[0:CTX, 2 * P:3 * P])\
                        .then_inc(turn_free, 1)

                def out_hi(k, u):
                    h, b, _ = unit(2 * u)
                    act.wait_ge(outp_ready, k * OUTS + u + 1)
                    act.copy(outT.hi[:, h, b * SEQ:(b + 1) * SEQ], core.outp[u % 2][0:DH, 0:SEQ])\
                        .then_inc(out_hi_ready, 1)

                def iteration(k, project, attend, split):
                    if not attend:
                        act.wait_ge(proj_ready, TC + B)
                        split_w(1, W + DH)
                        for what in FIRST[TC + B:]:
                            proj_hi(k, what)
                    else:
                        for c in range(STEPS):
                            if project and c in Q_STEPS:
                                proj_hi(k, ("q", *Q_STEPS[c]))
                            if c in WO_STEPS:
                                h = WO_STEPS[c]
                                if h == 0:
                                    act.wait_ge(proj_ready, proj_base(k))
                                if h % 2 == 0:
                                    act.wait_ge(wo_loaded, (k * 2 + h // 2 + 1) * 16)
                                act.copy(wo.hi[:, h, :], raw_o[0:DH, h % 2, :]).then_inc(wo_hi_ready, 1)
                            for s in range(c * PER_STEP, (c + 1) * PER_STEP):
                                if s >= 3:
                                    probs_out(k, s - 3)
                                act.wait_ge(max_ready, k * UNITS + s + 1)
                                act.activation(probs[:, s % 4, :], core.score[s % 2][:, 0:KEYS], ACT.Exp,
                                               bias=nmax[:, s % 4:s % 4 + 1],
                                               accum_out=sums[:, s % 4:s % 4 + 1]).then_inc(score_free, 1)
                                if s >= 5 and s % 2 == 1:
                                    out_hi(k, (s - 5) // 2)
                        probs_out(k, UNITS - 3)
                        probs_out(k, UNITS - 2)
                        if project:
                            proj_hi(k, ("k", 0))
                        out_hi(k, OUTS - 2)
                        probs_out(k, UNITS - 1)
                        if project:
                            proj_hi(k, ("k", 1))
                        out_hi(k, OUTS - 1)
                        if project:
                            for what in TAIL[2:]:
                                proj_hi(k, what)
                    if split:
                        split_w(k + 3, W + DH)

                split_w(0, W)
                act.wait_ge(ctx_loaded, 16)
                act.copy(context(hT.hi[:]), by_batch(raw_ctx)).then_inc(ctx_hi_ready, 1)
                norm.scalar(act)
                all_iterations(act, iteration)

            @block.tensor
            def _(pe):
                def project(k, what):
                    n, bank = proj_use(k, what, True)
                    pe.wait_ge(proj_free, n + 1)
                    kind = what[0]
                    for j in range(KC):
                        flags = dict(start=(j == 0), stop=(j == KC - 1))
                        if kind in ("v", "vc"):
                            size = P if kind == "v" else CTX
                            at = column(what[1]) if kind == "v" else what[1] * KEYS + SEQ
                            last = product(pe, bank[0:size, 0:W], hT.hi[:, j, at:at + size], hT.lo[:, j, at:at + size],
                                           w.hi[:, j, 0:W], w.lo[:, j, 0:W], **flags)
                        elif kind == "k":
                            at = slice(what[1] * KEYS, (what[1] + 1) * KEYS)
                            last = product(pe, bank[0:DH, 0:KEYS], w.hi[:, j, W:W + DH], w.lo[:, j, W:W + DH],
                                           hT.hi[:, j, at], hT.lo[:, j, at], **flags)
                        else:
                            h, i = what[1:]
                            cols = slice(h * DH, (h + 1) * DH)
                            per = B // HALVES
                            hi, lo = (batches(tile[:])[:, j, i * per:(i + 1) * per, 0:SEQ] for tile in (hT.hi, hT.lo))
                            last = product(pe, bank[0:DH, :], w.hi[:, j, cols], w.lo[:, j, cols], hi, lo, **flags)
                    last.then_inc(proj_ready, 1)

                def scores(k, s):
                    h, b, qc = unit(s)
                    t0 = b * SEQ + qc * P
                    pe.wait_ge(score_free, k * UNITS + s + 1)
                    product(pe, core.score[s % 2][:, 0:KEYS], qT.hi[:, h, t0:t0 + P], qT.lo[:, h, t0:t0 + P],
                            kT.hi[:, b, :], kT.lo[:, b, :], start=True, stop=True).then_inc(score_ready, 1)

                def probs_turn(k, s):
                    pe.wait_ge(probs_ready, k * UNITS + s + 1)
                    pe.wait_ge(turn_free, k * UNITS + s + 1)
                    for j, n in enumerate(KEY_CHUNKS):
                        last = pe.transpose(core.turn[s % 2][0:n, j * P:(j + 1) * P],
                                            probs[:, s % 4, j * P:j * P + n], core.ident[:])
                    last.then_inc(turn_ready, 1)

                def weigh(k, u):
                    h, b, _ = unit(2 * u)
                    if u == 0:
                        pe.wait_ge(vg_ready, k + 1)
                    pe.wait_ge(turn_free, k * UNITS + 2 * u + 2 + RING)
                    pe.wait_ge(outp_free, k * OUTS + u + 1)
                    for j, n in enumerate(KEY_CHUNKS):
                        values = vg[:, b * QC + j, :] if n == P else vcg[:, b, :]
                        last = pe.matmul(core.outp[u % 2][0:DH, 0:SEQ], values, probsT[0:n, u % 2, j, :],
                                         start=(j == 0), stop=(j == len(KEY_CHUNKS) - 1))
                    last.then_inc(outp_ready, 1)

                def output(k, i, project):
                    n, bank = proj_use(k, ("out", i), project)
                    if i == 0:
                        pe.wait_ge(wo_ready, (k + 1) * HG)
                        pe.wait_ge(outp_free, (k + 1) * OUTS + RING)
                    pe.wait_ge(proj_free, n + 1)
                    at = slice(i * P, (i + 1) * P)
                    for h in range(HG):
                        last = product(pe, bank[:, :], outT.hi[:, h, at], outT.lo[:, h, at],
                                       wo.hi[:, h, :], wo.lo[:, h, :], start=(h == 0), stop=(h == HG - 1))
                    last.then_inc(proj_ready, 1)

                def iteration(k, project_next, attend, split):
                    if not attend:
                        for what in FIRST:
                            if what == ("vc", 0):
                                pe.wait_ge(ctx_ready, 1)
                            if what == ("k", 0):
                                pe.wait_ge(w_ready, 2)
                            project(k, what)
                        pe.wait_ge(proj_free, len(FIRST) + RING)
                        return
                    pe.wait_ge(proj_free, proj_base(k) - TC + RING)
                    for c in range(STEPS):
                        if project_next and c in Q_STEPS:
                            if c == HALVES:
                                pe.wait_ge(w_ready, k + 3)
                            project(k, ("q", *Q_STEPS[c]))
                        for s in range(c * PER_STEP, (c + 1) * PER_STEP):
                            if s >= 3:
                                probs_turn(k, s - 3)
                            scores(k, s)
                            if s >= 5 and s % 2 == 1:
                                weigh(k, (s - 5) // 2)
                    probs_turn(k, UNITS - 3)
                    probs_turn(k, UNITS - 2)
                    if project_next:
                        project(k, ("k", 0))
                    weigh(k, OUTS - 2)
                    probs_turn(k, UNITS - 1)
                    if project_next:
                        project(k, ("k", 1))
                    weigh(k, OUTS - 1)
                    if project_next:
                        for what in TAIL[2:]:
                            project(k, what)
                    for i in range(TC):
                        output(k, i, project_next)

                norm.tensor(pe)
                pe.wait_ge(norm.hT_ready, norm.hT_done)
                pe.wait_ge(w_ready, 1)
                all_iterations(pe, iteration)


E = 8


class Router:

    def __init__(self, core, ctx, name, probabilities, logits):
        nc = core.nc
        self.c = core
        self.probabilities = probabilities
        self.source = logits
        sb = lambda n, shape, dt=F32: ctx.enter_context(nc.sbuf_tensor(f"{name}_{n}", shape, dt))
        sem = lambda n: core.hold.enter_context(nc.semaphore(f"{name}_{n}"))
        self.gate = sb("gate", [P, KC, E])
        self.ids = sb("ids", [P, E])
        self.logits = sb("logits", [P, TC, E])
        self.shifted = sb("shifted", [P, TC, E])
        self.row = sb("row", [P, TC])
        self.top = sb("top", [P, TC, 8])
        self.where = sb("where", [P, TC, 8], U32)
        self.wheref = sb("wheref", [P, TC, 2])
        self.share = sb("share", [P, TC, 2])
        self.chosen = sb("chosen", [P, 2, TC, E])
        self.weight = sb("weight", [P, TC, E])
        self.loaded = sem("gate_loaded")
        self.logits_ready = sem("logits_ready")
        self.exp_in_ready = sem("exp_in_ready")
        self.exp_ready = sem("exp_ready")
        self.step = sem("route_step")
        self.steps = 0

    def tensor(self, pe):
        c = self.c
        pe.wait_ge(self.loaded, 32)
        for i in range(TC):
            for k in range(KC):
                last = pe.matmul(self.source[:, i * E:(i + 1) * E], c.hT[:, k, i * P:(i + 1) * P],
                                 self.gate[:, k, :], start=(k == 0), stop=(k == KC - 1))
        last.then_inc(self.logits_ready, 1)

    def scalar(self, act):
        act.wait_ge(self.exp_in_ready, 1)
        if self.probabilities:
            act.activation(self.logits[:], self.shifted[:], ACT.Exp).then_inc(self.exp_ready, 1)
        else:
            act.activation(self.share[:, :, 1], self.row[:], ACT.Exp).then_inc(self.exp_ready, 1)

    def vector(self, dve):
        per_row = lambda a: a.unsqueeze(2).broadcast_to([P, TC, E])

        def link(ins):
            self.steps += 1
            ins.then_inc(self.step, 1)
            dve.wait_ge(self.step, self.steps)

        dve.wait_ge(self.logits_ready, 1)
        link(dve.tensor_copy(self.logits[:], self.source[:, 0:TC * E].rearrange("p (c e) -> p c e", e=E)))
        if self.probabilities:
            link(dve.tensor_reduce(self.row[:], self.logits[:], AX.X, ALU.max))
            dve.tensor_tensor(self.shifted[:], self.logits[:], per_row(self.row[:]), ALU.subtract)\
                .then_inc(self.exp_in_ready, 1)
            dve.wait_ge(self.exp_ready, 1)
            link(dve.tensor_reduce(self.row[:], self.logits[:], AX.X, ALU.add))
            link(dve.reciprocal(self.row[:], self.row[:]))
            link(dve.tensor_tensor(self.logits[:], self.logits[:], per_row(self.row[:]), ALU.mult))
        for i in range(TC):
            ins = dve.max(self.top[:, i, :], self.logits[:, i, :])
        link(ins)
        for i in range(TC):
            ins = dve.max_index(self.where[:, i, :], self.top[:, i, :], self.logits[:, i, :])
        link(ins)
        link(dve.tensor_copy(self.wheref[:], self.where[:, :, 0:2]))
        if self.probabilities:
            link(dve.tensor_tensor(self.row[:], self.top[:, :, 0], self.top[:, :, 1], ALU.add))
            link(dve.reciprocal(self.row[:], self.row[:]))
            for j in range(2):
                ins = dve.tensor_tensor(self.share[:, :, j], self.top[:, :, j], self.row[:], ALU.mult)
            link(ins)
        else:
            dve.tensor_tensor(self.row[:], self.top[:, :, 1], self.top[:, :, 0], ALU.subtract)\
                .then_inc(self.exp_in_ready, 1)
            dve.wait_ge(self.exp_ready, 1)
            link(dve.tensor_scalar(self.row[:], self.share[:, :, 1], 1.0, None, ALU.add))
            link(dve.reciprocal(self.share[:, :, 0], self.row[:]))
            link(dve.tensor_tensor(self.share[:, :, 1], self.share[:, :, 1], self.share[:, :, 0], ALU.mult))
        for j in range(2):
            link(dve.tensor_tensor(self.chosen[:, j, :, :], self.ids[:].unsqueeze(1).broadcast_to([P, TC, E]),
                                   per_row(self.wheref[:, :, j]), ALU.is_equal))
            link(dve.tensor_tensor(self.chosen[:, j, :, :], self.chosen[:, j, :, :],
                                   per_row(self.share[:, :, j]), ALU.mult))
        link(dve.tensor_tensor(self.weight[:], self.chosen[:, 0, :, :], self.chosen[:, 1, :, :], ALU.add))


def expert_mixture(nc, core, io, name):
    EARLY = 4
    LOGITS = (EARLY, EARLY + 1)
    HALVES = T // D
    with ExitStack() as ctx:
        sb = lambda n, shape: ctx.enter_context(nc.sbuf_tensor(f"{name}_{n}", shape, F32))
        sem = lambda n: core.hold.enter_context(nc.semaphore(f"{name}_{n}"))
        core.h = sb("h", [P, 2, D])
        hT = Pair(nc, ctx, f"{name}_hT", [P, KC, T])
        raw = sb("raw", [P, 2, KC, D])
        w = [Pair(nc, ctx, f"{name}_w{i}", [P, KC, D]) for i in range(2)]
        gate = Pair(nc, ctx, f"{name}_gates", [P, KC, E])
        logitsT = sb("logitsT", [E, T])
        raw_loaded = [sem(f"raw{i}_loaded") for i in range(2)]
        w_hi_ready = sem("w_hi_ready")
        w_ready = sem("w_ready")
        gate_ready = sem("gate_ready")
        logitsT_ready = sem("logitsT_ready")
        logitsT_copied = sem("logitsT_copied")
        out_ready = sem("out_ready")
        out_free = sem("out_free")
        norm = Norm(core, pair=hT)
        banks = [*core.proj, *core.score, *core.outp, *core.turn]
        route = Router(core, ctx, name, probabilities=False, logits=banks[TC - 2])
        FIRST = [i for i in range(TC) if i != TC - 2] + [TC - 2]

        with nc.Block() as block:

            @block.sync
            def _(sp):
                def load(e, par):
                    sp.dma_start(raw[:, par, :, :], io["L0_experts"][ds(e, 1)].rearrange("a (k p) n -> p (a k) n", p=P))\
                        .then_inc(raw_loaded[par], 16)

                load(0, 0)
                sp.dma_start(route.gate[:], io["L0_gate"].rearrange("(k p) e -> p k e", p=P)).then_inc(route.loaded, 16)
                sp.dma_start(route.ids[:], io["expert_ids"].partition_broadcast(P)).then_inc(route.loaded, 16)
                load(1, 1)
                with sp.Fori(1, E // 2) as i:
                    for par in range(2):
                        sp.wait_ge(w_ready, i * 2 + par - 1)
                        load(i * 2 + par, par)

            @block.gpsimd
            def _(pool):
                def split(e, par):
                    pool.wait_ge(w_hi_ready, e + 1)
                    pool.tensor_tensor(w[par].lo[:], raw[:, par, :, :], w[par].hi[:].bitcast(F32), ALU.subtract)\
                        .then_inc(w_ready, 1)

                norm.gpsimd(pool)
                pool.wait_ge(gate_ready, 1)
                pool.tensor_tensor(gate.lo[:], route.gate[:], gate.hi[:].bitcast(F32), ALU.subtract)\
                    .then_inc(gate_ready, 1)
                with pool.Fori(0, E // 2) as i:
                    for par in range(2):
                        split(i * 2 + par, par)

            @block.vector
            def _(dve):
                norm.vector(dve)
                route.vector(dve)

                def add(e, i):
                    dve.wait_ge(out_ready, e * TC + (FIRST.index(i) if isinstance(e, int) else i) + 1)
                    dve.scalar_tensor_tensor(core.x[:, i, :], banks[i][:, :], route.weight[:, i, ds(e, 1)],
                                             core.x[:, i, :], ALU.mult, ALU.add).then_inc(out_free, 1)

                for i in range(TC):
                    add(0, i)
                with dve.Fori(1, E) as e:
                    for i in range(TC):
                        add(e, i)

            @block.scalar
            def _(act):
                def split(e, par):
                    act.wait_ge(raw_loaded[par], (e - par) * 8 + 16 if not isinstance(e, int) else e // 2 * 16 + 16)
                    if not isinstance(e, int) or e >= 2:
                        act.wait_ge(out_ready, (e - 1) * TC)
                    act.copy(w[par].hi[:], raw[:, par, :, :]).then_inc(w_hi_ready, 1)

                split(0, 0)
                act.wait_ge(route.loaded, 32)
                act.copy(gate.hi[:], route.gate[:]).then_inc(gate_ready, 1)
                norm.scalar(act)
                split(1, 1)
                for i in range(HALVES):
                    act.wait_ge(logitsT_ready, i + 1)
                    act.copy(logitsT[:, i * D:(i + 1) * D], banks[LOGITS[i]][0:E, :]).then_inc(logitsT_copied, 1)
                route.scalar(act)
                with act.Fori(1, E // 2) as i:
                    for par in range(2):
                        split(i * 2 + par, par)

            @block.tensor
            def _(pe):
                def expert(par, i):
                    at = slice(i * P, (i + 1) * P)
                    for k in range(KC):
                        last = product(pe, banks[i][:, :], hT.hi[:, k, at], hT.lo[:, k, at], w[par].hi[:, k, :],
                                       w[par].lo[:, k, :], start=(k == 0), stop=(k == KC - 1))
                    last.then_inc(out_ready, 1)

                def early(i):
                    if 0 <= i - 1 < EARLY:
                        pe.wait_ge(norm.hT_ready, norm.n0 + i)
                        pe.wait_ge(w_ready, 1)
                        expert(0, i - 1)

                norm.tensor(pe, early)
                pe.wait_ge(norm.hT_ready, norm.hT_done)
                pe.wait_ge(gate_ready, 2)
                for i in range(HALVES):
                    tokens = slice(i * D, (i + 1) * D)
                    for k in range(KC):
                        last = product(pe, banks[LOGITS[i]][0:E, :], gate.hi[:, k, :], gate.lo[:, k, :],
                                       hT.hi[:, k, tokens], hT.lo[:, k, tokens], start=(k == 0), stop=(k == KC - 1))
                    last.then_inc(logitsT_ready, 1)
                pe.wait_ge(logitsT_copied, HALVES)
                for i in range(TC):
                    last = pe.transpose(route.source[:, i * E:(i + 1) * E], logitsT[:, i * P:(i + 1) * P],
                                        core.ident[0:E, 0:E])
                last.then_inc(route.logits_ready, 1)
                for i in FIRST[EARLY:]:
                    if i == TC - 2:
                        pe.wait_ge(route.step, 1)
                    expert(0, i)

                def experts(e, par):
                    pe.wait_ge(w_ready, e + 1)
                    for i in range(TC):
                        pe.wait_ge(out_free, (e - 1) * TC + i + 1)
                        expert(par, i)

                experts(1, 1)
                with pe.Fori(1, E // 2) as i:
                    for par in range(2):
                        experts(i * 2 + par, par)


def adapted_linear(nc, core, io, name, out):
    R = 16
    SCALING = 16.0 / R
    with ExitStack() as ctx:
        core.hT = ctx.enter_context(nc.sbuf_tensor(f"{name}_hT", [P, KC, T], F32))
        core.h = ctx.enter_context(nc.sbuf_tensor(f"{name}_h", [P, 2, D], F32))
        sb = lambda n, shape: ctx.enter_context(nc.sbuf_tensor(f"{name}_{n}", shape, F32))
        sem = lambda n: core.hold.enter_context(nc.semaphore(f"{name}_{n}"))
        w = sb("base", [P, KC, D])
        wa = sb("a", [P, KC, E * R])
        wb = sb("b", [E * R, D])
        bias = sb("bias", [P, D])
        low = sb("low", [P, 2, E * R])
        lowT = sb("lowT", [E * R, 2, P])
        w_loaded = sem("w_loaded")
        bias_loaded = sem("bias_loaded")
        down_ready = sem("down_ready")
        low_ready = sem("low_ready")
        turned = sem("turned")
        lowT_ready = sem("lowT_ready")
        out_ready = sem("out_ready")
        x_ready = sem("x_ready")
        stored = sem("stored")
        norm = Norm(core, bias[:, :], bias_loaded)
        route = Router(core, ctx, name, probabilities=True, logits=core.score[0])
        out_dram = out.rearrange("(c p) d -> c p d", p=P)

        with nc.Block() as block:

            @block.sync
            def _(sp):
                sp.dma_start(bias[:], io["L1_ffn_b_base"].partition_broadcast(P)).then_inc(bias_loaded, 16)
                sp.dma_start(route.gate[:], io["L1_gate"].rearrange("(k p) e -> p k e", p=P)).then_inc(route.loaded, 16)
                sp.dma_start(route.ids[:], io["expert_ids"].partition_broadcast(P)).then_inc(route.loaded, 16)
                sp.dma_start(wa[:], io["L1_A"].rearrange("(k p) n -> p k n", p=P)).then_inc(w_loaded, 16)
                sp.dma_start(wb[:], io["L1_B"]).then_inc(w_loaded, 16)
                sp.dma_start(w[:], io["L1_base"].rearrange("(k p) n -> p k n", p=P)).then_inc(w_loaded, 16)
                for i in range(TC):
                    sp.wait_ge(x_ready, i + 1)
                    sp.dma_start(out_dram[i], core.x[:, i, :]).then_inc(stored, 16)
                sp.wait_ge(stored, TC * 16)

            @block.gpsimd
            def _(pool):
                norm.gpsimd(pool)

            @block.vector
            def _(dve):
                norm.vector(dve)
                route.vector(dve)
                for i in range(TC + 1):
                    if i < TC:
                        dve.wait_ge(down_ready, i + 1)
                        dve.scalar_tensor_tensor(low[:, i % 2, :].rearrange("p (e r) -> p e r", r=R),
                                                 core.score[i % 2][:, 0:E * R].rearrange("p (e r) -> p e r", r=R),
                                                 SCALING, route.weight[:, i, :].unsqueeze(2).broadcast_to([P, E, R]),
                                                 ALU.mult, ALU.mult).then_inc(low_ready, 1)
                    if i >= 1:
                        dve.wait_ge(out_ready, i)
                        dve.tensor_tensor(core.x[:, i - 1, :], core.proj[(i - 1) % 2][:, :], core.x[:, i - 1, :],
                                          ALU.add).then_inc(x_ready, 1)

            @block.scalar
            def _(act):
                norm.scalar(act)
                route.scalar(act)
                for i in range(TC):
                    act.wait_ge(turned, i + 1)
                    act.copy(lowT[:, i % 2, :], core.turn[i % 2][:, 0:P]).then_inc(lowT_ready, 1)

            @block.tensor
            def _(pe):
                norm.tensor(pe)
                pe.wait_ge(norm.hT_ready, norm.hT_done)
                route.tensor(pe)
                pe.wait_ge(w_loaded, 48)

                def down(i):
                    if i == 0:
                        pe.wait_ge(route.exp_in_ready, 1)
                    if i >= 2:
                        pe.wait_ge(low_ready, i - 1)
                    for k in range(KC):
                        last = pe.matmul(core.score[i % 2][:, 0:E * R], core.hT[:, k, i * P:(i + 1) * P],
                                         wa[:, k, :], start=(k == 0), stop=(k == KC - 1))
                    last.then_inc(down_ready, 1)

                def base(i):
                    if i >= 2:
                        pe.wait_ge(x_ready, i - 1)
                    for k in range(KC):
                        pe.matmul(core.proj[i % 2][:, :], core.hT[:, k, i * P:(i + 1) * P], w[:, k, :],
                                  start=(k == 0), stop=False)

                down(0)
                for i in range(TC):
                    if i + 1 < TC:
                        down(i + 1)
                    base(i)
                    pe.wait_ge(low_ready, i + 1)
                    if i >= 2:
                        pe.wait_ge(lowT_ready, i - 1)
                    pe.transpose(core.turn[i % 2][:, 0:P], low[:, i % 2, :], core.ident[:]).then_inc(turned, 1)
                    pe.wait_ge(lowT_ready, i + 1)
                    pe.matmul(core.proj[i % 2][:, :], lowT[:, i % 2, :], wb[:, :], start=False, stop=True)\
                        .then_inc(out_ready, 1)


def head_attention(nc, core, io, name):
    H, DH = 32, 16
    PACK = P // H
    GROUP = P // B
    ROWS = DH + PACK
    PACKS = D // P
    TOKENS = PACKS * PACK
    BLOCKS = SEQ // TOKENS
    UNITS = BLOCKS * B
    HPC = P // DH
    HALVES = T // D
    BACK = D // P
    with ExitStack() as ctx:
        sb = lambda n, shape: ctx.enter_context(nc.sbuf_tensor(f"{name}_{n}", shape, F32))
        sem = lambda n: core.hold.enter_context(nc.semaphore(f"{name}_{n}"))
        hT = Pair(nc, ctx, f"{name}_hT", [P, KC, T])
        raw = sb("raw", [P, KC, D])
        w = Pair(nc, ctx, f"{name}_w", [P, KC, D])
        bias = sb("bias", [P, 3, KC])
        stage = sb("stage", [P, KC, T])
        spread = [sb(f"spread_{n}", [P, H, SEQ]) for n in "qkv"]
        context = spread[2]
        tags = sb("tags", [P, 2, TOKENS, H])
        slot = [sb(f"slot_{n}", [P, RING, TOKENS, H]) for n in "qkv"]
        values = sb("values", [P, RING, PACKS, B, GROUP])
        nmax = sb("nmax", [P, RING, PACKS])
        shifted, probsT = raw[:, 0:RING, :], raw[:, RING:2 * RING, :]
        probs = stage[:, 0, :].rearrange("p (r n) -> p r n", r=RING)
        part = stage[:, 1, 0:RING * B * BACK * DH]\
            .rearrange("p (r b h d) -> p r b h d", r=RING, b=B, h=BACK)
        core.h = probs
        rsum = sb("rsum", [P, RING, B, BACK])
        scratch = [nc.dram_tensor(f"{name}_scratch_{n}", (D, T), F32, kind="Internal").ap() for n in "qkv"]

        w_loaded = sem("w_loaded")
        w_hi_ready = sem("w_hi_ready")
        w_ready = sem("w_ready")
        bias_loaded = sem("bias_loaded")
        tags_loaded = sem("tags_loaded")
        zeroed = sem("zeroed")
        ones_ready = sem("ones_ready")
        proj_ready = sem("proj_ready")
        proj_free = sem("proj_free")
        to_dram = [sem(f"to_dram{c}") for c in range(KC)]
        spread_loaded = [sem(f"spread_{n}_loaded") for n in "qkv"]
        slot_ready = sem("slot_ready")
        v_turned = sem("v_turned")
        v_ready = sem("v_ready")
        score_ready = sem("score_ready")
        max_ready = sem("max_ready")
        shifted_ready = sem("shifted_ready")
        probs_ready = sem("probs_ready")
        probs_turned = sem("probs_turned")
        probsT_ready = sem("probsT_ready")
        out_ready = sem("out_ready")
        out_copied = sem("out_copied")
        back_ready = sem("back_ready")
        rsum_ready = sem("rsum_ready")
        part_ready = sem("part_ready")
        added = sem("added")
        norm = Norm(core, pair=hT)

        def block_of(t, tile):
            return tile[:, :, ds(t * TOKENS, TOKENS)].rearrange("p h t -> p t h")

        def packs(tile):
            return tile.rearrange("p (a k) -> p a k", a=PACKS)

        def each_unit(engine, step):
            for j in range(RING * B):
                step(0, j, True)
            with engine.Fori(1, BLOCKS // RING) as i:
                for j in range(RING * B):
                    step(i, j, False)

        def place(i, j):
            return i * RING * B + j, j % RING, i * RING + j // B, j // B % RING, j % B

        with nc.Block() as block:

            @block.sync
            def _(sp):
                def load_w(j):
                    sp.dma_start(raw[:], io[f"L1_attn_w{'qkv'[j]}"].rearrange("(k p) n -> p k n", p=P))\
                        .then_inc(w_loaded, 16)

                def spread_out(j, c):
                    sp.wait_ge(to_dram[c], 16 * (j + 1))
                    for b in range(B):
                        sp.dma_start(spread[j][b * GROUP:b * GROUP + DH, c * HPC:(c + 1) * HPC, :],
                                     scratch[j].rearrange("(h d) t -> d h t", d=DH)
                                     [:, c * HPC:(c + 1) * HPC, b * SEQ:(b + 1) * SEQ]).then_inc(spread_loaded[j], 16)

                load_w(0)
                for j, n in enumerate("qkv"):
                    sp.dma_start(bias[:, j, :], io[f"L1_attn_b{n}"]).then_inc(bias_loaded, 16)
                sp.dma_start(tags[:], io["tags"].rearrange("j p (t h) -> p j t h", h=H)).then_inc(tags_loaded, 16)
                sp.wait_ge(w_ready, KC)
                load_w(1)
                sp.wait_ge(zeroed, 3)
                last = None
                for j in range(3):
                    for c in range(KC):
                        sp.wait_ge(proj_free, (j * KC + c + 1) * HALVES + RING)
                        sp.dma_start(scratch[j][c * P:(c + 1) * P, :], stage[:, c, :]).then_inc(to_dram[c], 16)
                        if last:
                            spread_out(*last)
                        last = (j, c)
                    if j == 0:
                        sp.wait_ge(w_ready, 2 * KC)
                        load_w(2)
                spread_out(*last)

            @block.gpsimd
            def _(pool):
                norm.gpsimd(pool)
                for j in range(3):
                    pool.memset(spread[j][:], 0.0).then_inc(zeroed, 1)
                pool.memset(values[:], 0.0).then_inc(zeroed, 1)
                pool.wait_ge(zeroed, 4)
                for r in range(RING):
                    pool.memset(values[:, r, :, :, DH:DH + 1], 1.0).then_inc(ones_ready, 1)
                def fill_slots(i, j, peeled):
                    _, _, t, r, b = place(i, j)
                    if b:
                        return
                    pool.wait_ge(tags_loaded, 16)
                    if not peeled:
                        pool.wait_ge(score_ready, (t - 1) * B)
                    for n in range(2):
                        if peeled:
                            pool.wait_ge(spread_loaded[n], 16 * B * KC)
                        pool.tensor_tensor(slot[n][:, r, :, :], block_of(t, spread[n]), tags[:, n, :, :], ALU.add)
                    if peeled:
                        pool.wait_ge(spread_loaded[2], 16 * B * KC)
                    pool.tensor_copy(slot[2][:, r, :, :], block_of(t, spread[2])).then_inc(slot_ready, 1)

                each_unit(pool, fill_slots)

            @block.vector
            def _(dve):
                dve.sem_inc(proj_free, RING)
                norm.vector(dve)
                dve.wait_ge(bias_loaded, 48)

                def lower_w(j, c):
                    at = slice(c * P, (c + 1) * P)
                    dve.wait_ge(w_hi_ready, j * KC + c + 1)
                    dve.tensor_tensor(w.lo[:, :, at], raw[:, :, at], w.hi[:, :, at].bitcast(F32), ALU.subtract)\
                        .then_inc(w_ready, 1)

                for c in range(KC):
                    lower_w(0, c)
                for j in range(3):
                    scale = float(DH) ** -0.5 if j == 0 else 1.0
                    for c in range(KC):
                        if j >= 1:
                            dve.wait_ge(to_dram[c], 16 * j)
                        for i in range(HALVES):
                            n = (j * KC + c) * HALVES + i
                            dve.wait_ge(proj_ready, n + 1)
                            dve.tensor_scalar(stage[:, c, i * D:(i + 1) * D], core.proj[n % 2][:, :],
                                              bias[:, j, c:c + 1], scale, ALU.add, ALU.mult)\
                                .then_inc(proj_free, 1)
                        if j < 2:
                            lower_w(j + 1, c)

                def copy_out(t, r):
                    dve.wait_ge(tags_loaded, 16)
                    dve.wait_ge(out_ready, (t + 1) * B)
                    dve.tensor_copy(block_of(t, context), core.proj[r][:, :].rearrange("p (t h) -> p t h", h=H))\
                        .then_inc(out_copied, 1)

                def softmax(i, j, peeled):
                    u, ur, t, r, b = place(i, j)
                    dve.wait_ge(score_ready, u + 1)
                    dve.tensor_reduce(nmax[:, ur, :], packs(core.score[ur][:, :]), AX.X, ALU.max)\
                        .then_inc(max_ready, 1)
                    if b == B - 2 and not (peeled and j < B):
                        copy_out(t - 1, 1 - r)
                    dve.wait_ge(max_ready, u + 1)
                    dve.tensor_tensor(packs(shifted[:, ur, :]), packs(core.score[ur][:, :]),
                                      nmax[:, ur, :].unsqueeze(2).broadcast_to([P, PACKS, P]), ALU.subtract)\
                        .then_inc(shifted_ready, 1)

                each_unit(dve, softmax)
                copy_out(BLOCKS - 1, (BLOCKS - 1) % RING)
                for n in range(QC * H // BACK):
                    r, qc, h0 = n % RING, n % QC, n // QC * BACK
                    turned = core.turn[r][:, :].rearrange("p (h b s) -> p b h s", h=BACK, b=B)
                    dve.wait_ge(back_ready, n + 1)
                    dve.reciprocal(rsum[:, r, :, :], turned[:, :, :, DH]).then_inc(rsum_ready, 1)
                    dve.wait_ge(rsum_ready, n + 1)
                    dve.tensor_tensor(part[:, r, :, :, :], turned[:, :, :, 0:DH],
                                      rsum[:, r, :, :].unsqueeze(3).broadcast_to([P, B, BACK, DH]),
                                      ALU.mult).then_inc(part_ready, 1)
                    dve.wait_ge(part_ready, n + 1)
                    x = core.x[:].rearrange("p (b q) d -> p b q d", q=QC)[:, :, qc, h0 * DH:(h0 + BACK) * DH]
                    dve.tensor_tensor(x, x, part[:, r, :, :, :].rearrange("p b h d -> p b (h d)"), ALU.add)

            @block.scalar
            def _(act):
                def split_w(j, c):
                    if j:
                        act.wait_ge(proj_ready, ((j - 1) * KC + c + 1) * HALVES)
                    if c == 0:
                        act.wait_ge(w_loaded, 16 * (j + 1))
                    at = slice(c * P, (c + 1) * P)
                    act.copy(w.hi[:, :, at], raw[:, :, at]).then_inc(w_hi_ready, 1)

                for c in range(KC):
                    split_w(0, c)
                norm.scalar(act)
                for j in range(1, 3):
                    for c in range(KC):
                        split_w(j, c)
                act.wait_ge(ones_ready, RING)

                def turn_out(u, ur):
                    act.wait_ge(probs_turned, u + 1)
                    act.copy(probsT[:, ur, :], core.outp[ur][:, :]).then_inc(probsT_ready, 1)

                def softmax(i, j, peeled):
                    u, ur, t, r, b = place(i, j)
                    act.wait_ge(shifted_ready, u + 1)
                    act.activation(probs[:, ur, :], shifted[:, ur, :], ACT.Exp).then_inc(probs_ready, 1)
                    if not (peeled and j < 1):
                        turn_out(u - 1, 1 - ur)
                    if b == 0:
                        act.wait_ge(v_turned, t + 1)
                        if not peeled:
                            act.wait_ge(out_ready, (t - 1) * B)
                        act.copy(values[:, r, :, :, 0:DH],
                                 core.turn[r][:, :].rearrange("p (a b s) -> p a b s", a=PACKS, b=B)[:, :, :, 0:DH])\
                            .then_inc(v_ready, 1)

                each_unit(act, softmax)
                turn_out(UNITS - 1, (UNITS - 1) % RING)

            @block.tensor
            def _(pe):
                norm.tensor(pe)
                pe.wait_ge(norm.hT_ready, norm.hT_done)
                for j in range(3):
                    for c in range(KC):
                        pe.wait_ge(w_ready, j * KC + c + 1)
                        for i in range(HALVES):
                            n = (j * KC + c) * HALVES + i
                            pe.wait_ge(proj_free, n + 1)
                            for k in range(KC):
                                at, tokens = slice(c * P, (c + 1) * P), slice(i * D, (i + 1) * D)
                                last = product(pe, core.proj[n % 2][:, :], w.hi[:, k, at], w.lo[:, k, at],
                                               hT.hi[:, k, tokens], hT.lo[:, k, tokens],
                                               start=(k == 0), stop=(k == KC - 1))
                            last.then_inc(proj_ready, 1)

                def turn(u, ur, bank_used):
                    pe.wait_ge(probs_ready, u + 1)
                    if bank_used:
                        pe.wait_ge(probsT_ready, u - 1)
                    for a in range(PACKS):
                        last = pe.transpose(core.outp[ur][:, a * P:(a + 1) * P], probs[:, ur, a * P:(a + 1) * P],
                                            core.ident[:])
                    last.then_inc(probs_turned, 1)

                def weigh(u, ur, t, r, b, bank_used):
                    pe.wait_ge(probsT_ready, u + 1)
                    if b == 0:
                        pe.wait_ge(v_ready, t + 1)
                        if bank_used:
                            pe.wait_ge(out_copied, t - 1)
                    for a in range(PACKS):
                        last = pe.matmul(core.proj[r][b * GROUP:(b + 1) * GROUP, a * P:(a + 1) * P],
                                         values[:, r, a, b, :], probsT[:, ur, a * P:(a + 1) * P],
                                         start=True, stop=True)
                    last.then_inc(out_ready, 1)

                def scores(i, j, peeled):
                    u, ur, t, r, b = place(i, j)
                    if b == 0:
                        pe.wait_ge(slot_ready, t + 1)
                        if not peeled:
                            pe.wait_ge(v_ready, t - 1)
                        for a in range(PACKS):
                            last = pe.transpose(core.turn[r][:, a * P:(a + 1) * P],
                                                slot[2][:, r, a * PACK:(a + 1) * PACK, :].rearrange("p t h -> p (t h)"),
                                                core.ident[:])
                        last.then_inc(v_turned, 1)
                    if not (peeled and j < RING):
                        pe.wait_ge(shifted_ready, u - 1)
                    rows = slice(b * GROUP, b * GROUP + ROWS)
                    for a in range(PACKS):
                        q, k = (slot[n][rows, r, a * PACK:(a + 1) * PACK, :].rearrange("p t h -> p (t h)")
                                for n in range(2))
                        last = pe.matmul(core.score[ur][:, a * P:(a + 1) * P], q, k, start=True, stop=True)
                    last.then_inc(score_ready, 1)
                    if not (peeled and j < 1):
                        turn(u - 1, 1 - ur, not (peeled and j - 1 < RING))
                    if not (peeled and j < 2):
                        _, _, t2, r2, b2 = place(i, j - 2)
                        weigh(u - 2, ur, t2, r2, b2, not peeled)

                pe.wait_ge(proj_free, 3 * KC * HALVES + RING)
                each_unit(pe, scores)
                turn(UNITS - 1, (UNITS - 1) % RING, True)
                for u in (UNITS - 2, UNITS - 1):
                    weigh(u, u % RING, u // B, u // B % RING, u % B, True)
                pe.wait_ge(out_copied, BLOCKS)
                for n in range(QC * H // BACK):
                    qc, h0 = n % QC, n // QC * BACK
                    if n >= RING:
                        pe.wait_ge(part_ready, n - 1)
                    for h in range(BACK):
                        last = pe.transpose(core.turn[n % RING][:, h * P:(h + 1) * P],
                                            context[:, h0 + h, qc * P:(qc + 1) * P], core.ident[:])
                    last.then_inc(back_ready, 1)


def build_program(nc, io, out):
    with ExitStack() as ctx:
        core = Core(nc, ctx)
        self_attention(nc, core, io, "self", 1e-6)
        context_attention(nc, core, io, "context", 1e-5)
        expert_mixture(nc, core, io, "experts")
        head_attention(nc, core, io, "heads")
        latent_attention(nc, core, io, "latent")
        adapted_linear(nc, core, io, "adapted", out)


def layout(inputs):
    import numpy as np

    a = {n: np.asarray(v) for n, v in inputs.items()}
    flat = {n: a[n] for n in ("L0_attn_Wq", "L0_attn_bq", "L0_attn_Wk", "L0_attn_bk", "L0_attn_Wv",
                              "L0_attn_bv", "L0_attn_Wo", "L0_attn_bo", "L0_attn_gq", "L0_attn_gk")}
    flat["x"] = a["x"].reshape(T, D)
    flat["ident"] = np.eye(P, dtype=np.float32)
    flat["expert_ids"] = np.arange(E, dtype=np.float32)
    flat["ctxT"] = a["ctx_4096"].reshape(B * CTX, D).T
    flat["mask"] = a["mask_1x1xSxS2_ff0"].reshape(SEQ, CTX)
    for n in "qkvo":
        flat[f"L0_xattn_{n}"] = a[f"L0_xattn_{n}_proj_w"].T
        flat[f"L1_xattn_{n}"] = a[f"L1_xattn_W{n}"].T
        if n != "o":
            flat[f"L1_attn_w{n}"] = a[f"L1_attn_w{n}"].T
            flat[f"L1_attn_b{n}"] = a[f"L1_attn_b{n}"].reshape(KC, P).T
    tags = np.zeros((2, B, P // B, 4, 32), np.float32)
    for t in range(4):
        tags[0, :, 16 + t, t, :] = 1.0
        tags[1, :, 16 + t, :, :] = -1e30
        tags[1, :, 16 + t, t, :] = 0.0
    flat["tags"] = np.tile(tags.reshape(2, P, P), (1, 1, 4))
    flat["L0_xattn_gq"] = a["L0_xattn_q_norm_w"]
    flat["L0_xattn_gk"] = a["L0_xattn_k_norm_w"]
    flat["L0_gate"] = a["L0_ffn_gate_w"]
    flat["L0_experts"] = a["L0_ffn_expert_w"]
    flat["L1_gate"] = a["L1_ffn_W_gate"].T
    flat["L1_base"] = a["L1_ffn_W_base"].T
    flat["L1_ffn_b_base"] = a["L1_ffn_b_base"]
    flat["L1_A"] = a["L1_ffn_A"].reshape(-1, D).T
    flat["L1_B"] = a["L1_ffn_B"].transpose(0, 2, 1).reshape(-1, D)
    return {n: np.ascontiguousarray(v) for n, v in flat.items()}


def kernel(**inputs):
    import concourse.bacc as bacc
    from concourse.bass_utils import run_bass_kernel_spmd

    nc = bacc.Bacc("TRN2", target_bir_lowering=False, num_devices=1)
    arrays = {f"in_{n}_dram": v for n, v in layout(inputs).items()}
    io = {n[3:-5]: nc.dram_tensor(n, v.shape, mybir.dt.from_np(v.dtype), kind="ExternalInput").ap()
          for n, v in arrays.items()}
    out = nc.dram_tensor("out_dram", (T, D), F32, kind="ExternalOutput").ap()
    build_program(nc, io, out)
    result = run_bass_kernel_spmd(nc, [arrays], core_ids=[0])
    return result.results[0]["out_dram"].reshape(B, SEQ, D)
```

```python
from contextlib import ExitStack

import concourse.bass as bass
from concourse import mybir

F32 = mybir.dt.float32
F32R = mybir.dt.float32r
U32 = mybir.dt.uint32
ALU = mybir.AluOpType
ACT = mybir.ActivationFunctionType
AX = mybir.AxisListType
ds = bass.ds

P = 128
B, SEQ, D = 4, 256, 512
T = B * SEQ
TC = T // P
KC = D // P
CTX = 64
LN_EPS = 1e-5
QC = SEQ // P
HG = 4
RING = 2


class Core:

    def __init__(self, nc, ctx):
        self.nc = nc
        self.hold = ctx

        def sb(name, shape, dt=F32):
            return ctx.enter_context(nc.sbuf_tensor(name, shape, dt))

        self.x = sb("x_res", [P, TC, D])
        self.ident = sb("ident", [P, P])
        self.neg_half = sb("neg_half", [P, 32])
        self.mv = sb("ln_mean_var", [P, TC, 2])
        self.stats = sb("ln_stats", [P, TC, 6])
        self.vareps = sb("ln_var_eps", [P, TC])
        self.rstd = sb("ln_rstd", [P, TC])
        self.shift = sb("ln_shift", [P, TC])
        self.h = None
        self.norms = 0
        self.biases = 0
        self.bias_added = ctx.enter_context(nc.semaphore("ln_bias_added"))
        self.norm_sems = [ctx.enter_context(nc.semaphore(f"ln_{n}")) for n in
                          ("stats", "mean", "var_eps", "rstd", "shift", "h", "turned", "hi", "hT")]
        bank = lambda name: ctx.enter_context(nc.psum_tensor(name, [P, D], F32))
        self.proj = [bank(f"proj{i}") for i in range(RING)]
        self.score = [bank(f"score{i}") for i in range(RING)]
        self.turn = [bank(f"turn{i}") for i in range(RING)]
        self.outp = [bank(f"outp{i}") for i in range(RING)]


class Pair:

    def __init__(self, nc, ctx, name, shape):
        self.hi = ctx.enter_context(nc.sbuf_tensor(f"{name}_hi", shape, F32R))
        self.lo = ctx.enter_context(nc.sbuf_tensor(f"{name}_lo", shape, F32R))


def product(pe, out, a_hi, a_lo, b_hi, b_lo, start, stop):
    pe.matmul(out, a_hi, b_lo, start=start, stop=False)
    pe.matmul(out, a_lo, b_hi, start=False, stop=False)
    return pe.matmul(out, a_hi, b_hi, start=False, stop=stop)


class Norm:

    def __init__(self, core, pair, bias=None, bias_loaded=None, column=lambda i: i * P):
        self.c = core
        self.bias, self.bias_loaded = bias, bias_loaded
        self.pair = pair
        self.columns = lambda i: slice(column(i), column(i) + P)
        (self.stats_ready, self.mean_ready, self.var_eps_ready, self.rstd_ready, self.shift_ready, self.h_ready,
         self.turned, self.hi_ready, self.hT_ready) = core.norm_sems
        self.n0 = core.norms * TC
        self.hT_done = self.n0 + TC
        core.norms += 1
        if bias is not None:
            core.biases += 1
            self.biased = (core.biases - 1) * TC
        self.hT_chunks = lambda n: self.n0 + n

    def vector(self, dve, after=lambda i: None):
        c, n0 = self.c, self.n0

        def statistics(i):
            dve.bn_stats(c.stats[:, i, :], c.x[:, i, :]).then_inc(self.stats_ready, 1)
            dve.wait_ge(self.stats_ready, n0 + i + 1)
            dve.bn_aggr(c.mv[:, i, :], c.stats[:, i, :]).then_inc(self.mean_ready, 1)

        def lo(i):
            dve.wait_ge(self.hi_ready, n0 + i + 1)
            chunk = self.columns(i)
            dve.tensor_tensor(self.pair.lo[:, :, chunk], c.turn[i % 2][:].rearrange("p (k t) -> p k t", k=KC),
                              self.pair.hi[:, :, chunk].bitcast(F32), ALU.subtract).then_inc(self.hT_ready, 1)

        AHEAD = 3
        for i in range(TC + AHEAD):
            if i < TC:
                statistics(i)
            if i >= AHEAD:
                lo(i - AHEAD)
                after(i - AHEAD)

    def gpsimd(self, pool):
        c, n0 = self.c, self.n0
        for i in range(TC):
            pool.wait_ge(self.mean_ready, n0 + i + 1)
            pool.tensor_scalar(c.shift[:, i:i + 1], c.mv[:, i, 0:1], -1.0, None, ALU.mult)
            pool.tensor_scalar(c.vareps[:, i:i + 1], c.mv[:, i, 1:2], LN_EPS, None, ALU.add)\
                .then_inc(self.var_eps_ready, 1)
            pool.wait_ge(self.var_eps_ready, n0 + i + 1)
            pool.tensor_tensor(c.rstd[:, i:i + 1], c.vareps[:, i:i + 1], c.neg_half[:, 0:1], ALU.pow)\
                .then_inc(self.rstd_ready, 1)
            pool.wait_ge(self.rstd_ready, n0 + i + 1)
            pool.tensor_tensor(c.shift[:, i:i + 1], c.shift[:, i:i + 1], c.rstd[:, i:i + 1], ALU.mult)\
                .then_inc(self.shift_ready, 1)
        if self.bias is not None:
            pool.wait_ge(self.bias_loaded, 16)
            for i in range(TC):
                pool.wait_ge(self.h_ready, n0 + i + 1)
                pool.tensor_tensor(c.x[:, i, :], c.x[:, i, :], self.bias, ALU.add).then_inc(c.bias_added, 1)

    def tensor(self, pe, after=lambda i: None):
        c, n0 = self.c, self.n0
        for i in range(TC):
            pe.wait_ge(self.h_ready, n0 + i + 1)
            if i >= 2:
                pe.wait_ge(self.hT_ready, n0 + i - 1)
            for k in range(KC):
                last = pe.transpose(c.turn[i % 2][:, k * P:(k + 1) * P], c.h[:, i % 2, k * P:(k + 1) * P],
                                    c.ident[:])
            last.then_inc(self.turned, 1)
            after(i)

    def scalar(self, act, after=lambda i: None):
        c, n0 = self.c, self.n0
        for i in range(TC + 1):
            if i < TC:
                act.wait_ge(self.shift_ready, n0 + i + 1)
                if i >= 2:
                    act.wait_ge(self.turned, n0 + i - 1)
                act.activation(c.h[:, i % 2, :], c.x[:, i, :], ACT.Identity, bias=c.shift[:, i:i + 1],
                               scale=c.rstd[:, i:i + 1]).then_inc(self.h_ready, 1)
            if i >= 1:
                act.wait_ge(self.turned, n0 + i)
                act.copy(self.pair.hi[:, :, self.columns(i - 1)],
                         c.turn[(i - 1) % 2][:].rearrange("p (k t) -> p k t", k=KC)).then_inc(self.hi_ready, 1)
                after(i - 1)


def self_attention(nc, core, io, name, eps):
    HPG = 2
    GROUPS = 32 // HPG
    W = HPG * P
    UNITS = B * HPG * QC
    OUTS = UNITS // QC
    PIECES = KC
    FIRST_W = range(2, 2 + PIECES)
    OUT_STEPS = {4: 0, 5: 1, 6: 2, 7: 3}
    PROJ = []
    for c in range(TC):
        PROJ += [("qk", c), ("v", c)] + ([("out", OUT_STEPS[c])] if c in OUT_STEPS else [])
    PROJ += [("out", i) for i in range(len(OUT_STEPS), TC)]
    TURNS = []
    for c in range(TC):
        TURNS += [("qk", c - 2)] * (c >= 2)
        TURNS += [("probs", s - 2) for s in (2 * c, 2 * c + 1) if s >= 2]
    TURNS += [("probs", UNITS - 2), ("probs", UNITS - 1), ("qk", TC - 2), ("qk", TC - 1)]

    with ExitStack() as ctx:
        sb = lambda n, shape: ctx.enter_context(nc.sbuf_tensor(f"{name}_{n}", shape, F32))
        sem = lambda n: core.hold.enter_context(nc.semaphore(f"{name}_{n}"))
        hT = Pair(nc, ctx, f"{name}_hT", [P, KC, T])
        raw = sb("raw", [P, KC, 3 * W])
        raw_o = sb("raw_o", [P, HPG, D])
        w = Pair(nc, ctx, f"{name}_w", [P, 2, KC, 3 * W])
        wo = Pair(nc, ctx, f"{name}_wo", [P, HPG, D])
        bias = sb("bias", [P, 2, 3 * W])
        gains = sb("gains", [P, 2])
        gain = sb("gain", [P, 1])
        epsilon = sb("epsilon", [P, 2 * HPG])
        tok = sb("tok", [P, 3, 2 * W])
        sq = sb("sq", [P, 2 * W])
        ss = sb("ss", [P, 2, 2 * HPG])
        ms = sb("ms", [P, 2, 2 * HPG])
        rms = sb("rms", [P, 2, 2 * HPG])
        qT = sb("qT", [P, 2, HPG, T])
        bo = qT[:, 1, 0, 0:D]
        kT = sb("kT", [P, 2, HPG, T])
        v = sb("v", [P, 2, TC, W])
        probs = sb("probs", [P, 4, SEQ])
        core.h = probs[:].rearrange("p (a b) k -> p a (b k)", a=2)
        nmax = sb("nmax", [P, 4])
        sums = sb("sums", [P, 4])
        rsum = sb("rsum", [P, 4])
        probsT = sb("probsT", [P, 2, QC, SEQ])
        outT = Pair(nc, ctx, f"{name}_outT", [P, HPG, T])

        x_loaded = sem("x_loaded")
        const_ready = sem("const_ready")
        bo_loaded = sem("bo_loaded")
        gain_loaded = sem("gain_loaded")
        gain_ready = sem("gain_ready")
        raw_loaded = sem("raw_loaded")
        raw_o_loaded = sem("raw_o_loaded")
        bias_loaded = [sem(f"bias{i}_loaded") for i in range(2)]
        w_hi_ready = sem("w_hi_ready")
        w_ready = sem("w_ready")
        wo_hi_ready = sem("wo_hi_ready")
        wo_ready = sem("wo_ready")
        proj_ready = sem("proj_ready")
        proj_free = sem("proj_free")
        sq_ready = sem("sq_ready")
        ss_ready = sem("ss_ready")
        ms_ready = sem("ms_ready")
        rms_ready = sem("rms_ready")
        qk_normed = sem("qk_normed")
        turn_ready = sem("turn_ready")
        turn_free = sem("turn_free")
        score_ready = sem("score_ready")
        score_free = sem("score_free")
        max_ready = sem("max_ready")
        rsum_ready = sem("rsum_ready")
        probs_ready = sem("probs_ready")
        outp_ready = sem("outp_ready")
        out_hi_ready = sem("out_hi_ready")
        outp_free = sem("outp_free")

        norm = Norm(core, hT, bo, bo_loaded)
        w_dram = [io[n].rearrange("(k p) n -> p k n", p=P) for n in ("L0_attn_Wq", "L0_attn_Wk", "L0_attn_Wv")]
        b_dram = [io[n].partition_broadcast(P) for n in ("L0_attn_bq", "L0_attn_bk", "L0_attn_bv")]
        wo_dram = io["L0_attn_Wo"].rearrange("(n p) d -> p n d", p=P)

        proj_base = lambda k: 2 * TC + k * 3 * TC if not isinstance(k, int) or k >= 0 else 0

        def proj_use(k, what, project, attend):
            order = [u for u in PROJ if (u[0] == "out" and attend) or (u[0] != "out" and project)]
            n = order.index(what)
            return proj_base(k) + n, core.proj[n % 2]

        def turn_use(k, what, project, attend):
            order = [t for t in TURNS if (t[0] == "qk" and project) or (t[0] == "probs" and attend)]
            n = order.index(what)
            base = TC + k * len(TURNS) if not isinstance(k, int) or k >= 0 else 0
            return base + n, n % 2

        unit = lambda s: (s // (HPG * QC), s // QC % HPG, s % QC)

        def all_iterations(engine, iteration):
            iteration(-1, 1, True, False, True)
            with engine.Fori(0, (GROUPS - 2) // 2) as i:
                for par in range(2):
                    iteration(i * 2 + par, par, True, True, True)
            iteration(GROUPS - 2, 0, True, True, False)
            iteration(GROUPS - 1, 1, False, True, False)

        with nc.Block() as block:

            @block.sync
            def _(sp):
                def load_w(g):
                    for j in range(3):
                        sp.dma_start(raw[:, :, j * W:(j + 1) * W], w_dram[j][:, :, ds(g * W, W)])\
                            .then_inc(raw_loaded, 16)

                def load_bias(g, par):
                    for j in range(3):
                        sp.dma_start(bias[:, par, j * W:(j + 1) * W], b_dram[j][:, ds(g * W, W)])\
                            .then_inc(bias_loaded[par], 16)

                def load_wo(g):
                    sp.dma_start(raw_o[:], wo_dram[:, ds(g * HPG, HPG), :]).then_inc(raw_o_loaded, 16)

                sp.dma_start(core.x[:], io["x"].rearrange("(c p) d -> p c d", p=P)).then_inc(x_loaded, 16)
                sp.dma_start(core.ident[:], io["ident"]).then_inc(x_loaded, 16)
                load_w(0)
                sp.dma_start(bo, io["L0_attn_bo"].partition_broadcast(P)).then_inc(bo_loaded, 16)
                sp.dma_start(gains[:, 0:1], io["L0_attn_gq"].unsqueeze(1)).then_inc(gain_loaded, 16)
                sp.dma_start(gains[:, 1:2], io["L0_attn_gk"].unsqueeze(1)).then_inc(gain_loaded, 16)
                load_bias(0, 0)
                load_bias(1, 1)
                load_wo(0)

                def loads(k, par, more_w, more_bias):
                    if more_bias:
                        sp.wait_ge(proj_free, proj_base(k) + RING)
                        load_bias(k + 2, par)
                    if more_w:
                        sp.wait_ge(w_ready, (k + 3) * PIECES)
                        load_w(k + 3)
                    sp.wait_ge(wo_ready, k + 1)
                    load_wo(k + 1)

                for g in (1, 2):
                    sp.wait_ge(w_ready, g * PIECES)
                    load_w(g)
                with sp.Fori(0, (GROUPS - 4) // 2) as i:
                    for par in range(2):
                        loads(i * 2 + par, par, True, True)
                loads(GROUPS - 4, 0, True, True)
                loads(GROUPS - 3, 1, False, True)
                loads(GROUPS - 2, 0, False, False)

            @block.gpsimd
            def _(pool):
                pool.memset(core.neg_half[:], -0.5).then_inc(const_ready, 1)
                pool.memset(epsilon[:], eps).then_inc(const_ready, 1)
                pool.wait_ge(const_ready, 2)

                def split_w(g, par, piece):
                    pool.wait_ge(w_hi_ready, g * PIECES + piece + 1)
                    pool.tensor_tensor(w.lo[:, par, piece, :], raw[:, piece, :], w.hi[:, par, piece, :].bitcast(F32),
                                       ALU.subtract).then_inc(w_ready, 1)

                def iteration(k, par, project, attend, split):
                    for c in range(TC):
                        if project:
                            n = (k + 1) * TC + c
                            pool.wait_ge(ss_ready, n + 1)
                            pool.tensor_tensor(ms[:, c % 2, :], ss[:, c % 2, :], epsilon[:], ALU.add)\
                                .then_inc(ms_ready, 1)
                            pool.wait_ge(ms_ready, n + 1)
                            pool.tensor_tensor(rms[:, c % 2, :], ms[:, c % 2, :], core.neg_half[:, 0:2 * HPG],
                                               ALU.pow).then_inc(rms_ready, 1)
                        if split and c < PIECES:
                            split_w(k + 2, par, c)
                        if attend and c == 1:
                            pool.wait_ge(wo_hi_ready, k + 1)
                            pool.tensor_tensor(wo.lo[:], raw_o[:], wo.hi[:].bitcast(F32), ALU.subtract)\
                                .then_inc(wo_ready, 1)

                norm.gpsimd(pool)
                all_iterations(pool, iteration)

            @block.vector
            def _(dve):
                dve.wait_ge(x_loaded, 32)
                dve.sem_inc(proj_free, RING)
                dve.sem_inc(outp_free, RING)

                def first_w(i):
                    if i in FIRST_W:
                        piece = FIRST_W.index(i)
                        dve.wait_ge(w_hi_ready, piece + 1)
                        dve.tensor_tensor(w.lo[:, 0, piece, :], raw[:, piece, :], w.hi[:, 0, piece, :].bitcast(F32),
                                          ALU.subtract).then_inc(w_ready, 1)

                norm.vector(dve, first_w)
                dve.wait_ge(gain_loaded, 32)
                dve.scalar_tensor_tensor(gain[:], gains[:, 0:1], float(P) ** -0.5, gains[:, 1:2],
                                         ALU.mult, ALU.mult).then_inc(gain_ready, 1)

                def normalise(k, c):
                    dve.wait_ge(rms_ready, (k + 1) * TC + c + 1)
                    t = tok[:, c % 3, :].rearrange("p (h d) -> p h d", d=P)
                    dve.tensor_tensor(t, t, rms[:, c % 2, :].unsqueeze(2).broadcast_to([P, 2 * HPG, P]),
                                      ALU.mult).then_inc(qk_normed, 1)

                def divide(k, s):
                    dve.wait_ge(score_free, k * UNITS + s + 1 + RING)
                    dve.reciprocal(rsum[:, s % 4:s % 4 + 1], sums[:, s % 4:s % 4 + 1]).then_inc(rsum_ready, 1)
                    dve.wait_ge(rsum_ready, k * UNITS + s + 1)
                    dve.tensor_scalar(probs[:, s % 4, :], probs[:, s % 4, :], rsum[:, s % 4:s % 4 + 1], None,
                                      ALU.mult).then_inc(probs_ready, 1)

                def out_lo(k, u):
                    b, h, _ = unit(2 * u)
                    dve.wait_ge(out_hi_ready, k * OUTS + u + 1)
                    at = slice(b * SEQ, (b + 1) * SEQ)
                    dve.tensor_tensor(outT.lo[:, h, at], core.outp[u % 2][:, 0:SEQ],
                                      outT.hi[:, h, at].bitcast(F32), ALU.subtract).then_inc(outp_free, 1)

                def iteration(k, par, project, attend, split):
                    for c in range(TC):
                        if attend and c:
                            divide(k, 2 * c - 1)
                        if attend and c - 1 in OUT_STEPS:
                            add_out(k, OUT_STEPS[c - 1], project)
                        if project:
                            if c == 0:
                                dve.wait_ge(bias_loaded[1 - par], 48 * bias_round(k, par))
                            n, bank = proj_use(k, ("qk", c), project, attend)
                            dve.wait_ge(proj_ready, n + 1)
                            dve.tensor_tensor(tok[:, c % 3, :], bank[:, :], bias[:, 1 - par, 0:2 * W],
                                              ALU.add).then_inc(proj_free, 1)
                            n, bank = proj_use(k, ("v", c), project, attend)
                            dve.wait_ge(proj_ready, n + 1)
                            dve.tensor_tensor(v[:, 1 - par, c, :], bank[:, 0:W],
                                              bias[:, 1 - par, 2 * W:3 * W], ALU.add).then_inc(proj_free, 1)
                            dve.wait_ge(sq_ready, (k + 1) * TC + c + 1)
                            dve.tensor_reduce(ss[:, c % 2, :], sq[:].rearrange("p (h d) -> p h d", d=P),
                                              AX.X, ALU.add).then_inc(ss_ready, 1)
                            if c >= 1:
                                normalise(k, c - 1)
                        if attend:
                            for s in (2 * c, 2 * c + 1):
                                if s % 2:
                                    divide(k, s - 1)
                                dve.wait_ge(score_ready, k * UNITS + s + 1)
                                dve.tensor_reduce(nmax[:, s % 4:s % 4 + 1], core.score[s % 2][:, 0:SEQ],
                                                  AX.X, ALU.max, negate=True).then_inc(max_ready, 1)
                                if s >= 5 and s % 2 == 1:
                                    out_lo(k, (s - 5) // 2)
                    if attend:
                        divide(k, UNITS - 1)
                        add_out(k, OUT_STEPS[TC - 1], project)
                        out_lo(k, OUTS - 2)
                        add_out(k, len(OUT_STEPS), project)
                    if project:
                        normalise(k, TC - 1)
                    if not attend:
                        dve.wait_ge(core.bias_added, norm.biased + TC)
                    if attend:
                        out_lo(k, OUTS - 1)
                        for i in range(len(OUT_STEPS) + 1, TC):
                            add_out(k, i, project)

                def add_out(k, i, project):
                    n, bank = proj_use(k, ("out", i), project, True)
                    dve.wait_ge(proj_ready, n + 1)
                    dve.tensor_tensor(core.x[:, i, :], bank[:, :], core.x[:, i, :], ALU.add).then_inc(proj_free, 1)

                def bias_round(k, par):
                    if isinstance(k, int):
                        return (k + 1) // 2 + 1
                    return (k - par) // 2 + 1 + par

                all_iterations(dve, iteration)

            @block.scalar
            def _(act):
                act.sem_inc(turn_free, RING)
                act.sem_inc(score_free, RING)

                def split_w(g, par, piece):
                    if piece == 0:
                        act.wait_ge(raw_loaded, (g + 1) * 48)
                    act.copy(w.hi[:, par, piece, :], raw[:, piece, :]).then_inc(w_hi_ready, 1)

                def qk_out(k, c, par, project, attend):
                    n, bank = turn_use(k, ("qk", c), project, attend)
                    act.wait_ge(turn_ready, n + 1)
                    at = slice(c * P, (c + 1) * P)
                    q, kk = (core.turn[bank][:, j * W:(j + 1) * W].rearrange("p (h t) -> p h t", t=P) for j in range(2))
                    act.activation(qT[:, 1 - par, :, at], q, ACT.Copy, scale=gain[:, 0:1])
                    act.copy(kT[:, 1 - par, :, at], kk).then_inc(turn_free, 1)

                def probs_out(k, s, project, attend):
                    n, bank = turn_use(k, ("probs", s), project, attend)
                    act.wait_ge(turn_ready, n + 1)
                    qc = s % QC
                    act.copy(probsT[:, s // QC % 2, :, qc * P:(qc + 1) * P],
                             core.turn[bank][:, 0:SEQ].rearrange("p (k t) -> p k t", t=P)).then_inc(turn_free, 1)

                def out_hi(k, u):
                    b, h, _ = unit(2 * u)
                    act.wait_ge(outp_ready, k * OUTS + u + 1)
                    act.copy(outT.hi[:, h, b * SEQ:(b + 1) * SEQ], core.outp[u % 2][:, 0:SEQ])\
                        .then_inc(out_hi_ready, 1)

                def iteration(k, par, project, attend, split):
                    for c in range(TC):
                        if project:
                            n, _ = proj_use(k, ("qk", c), project, attend)
                            act.wait_ge(proj_free, n + 1 + RING)
                            if not (isinstance(k, int) and k < 0 and c == 0):
                                act.wait_ge(ss_ready, (k + 1) * TC + c)
                            act.activation(sq[:], tok[:, c % 3, :], ACT.Square,
                                           scale=float(P) ** -0.5).then_inc(sq_ready, 1)
                            if c >= 2:
                                qk_out(k, c - 2, par, project, attend)
                        if attend:
                            for s in (2 * c, 2 * c + 1):
                                if s >= 2:
                                    probs_out(k, s - 2, project, attend)
                                if s >= 5 and s % 2 == 1:
                                    out_hi(k, (s - 5) // 2)
                                act.wait_ge(max_ready, k * UNITS + s + 1)
                                act.activation(probs[:, s % 4, :], core.score[s % 2][:, 0:SEQ], ACT.Exp,
                                               bias=nmax[:, s % 4:s % 4 + 1],
                                               accum_out=sums[:, s % 4:s % 4 + 1]).then_inc(score_free, 1)
                        if split and c < PIECES:
                            split_w(k + 2, par, c)
                        if attend and c == 1:
                            act.wait_ge(raw_o_loaded, (k + 1) * 16)
                            act.copy(wo.hi[:], raw_o[:]).then_inc(wo_hi_ready, 1)
                    if attend:
                        probs_out(k, UNITS - 2, project, attend)
                        out_hi(k, OUTS - 2)
                        probs_out(k, UNITS - 1, project, attend)
                        out_hi(k, OUTS - 1)
                    if project:
                        for c in (TC - 2, TC - 1):
                            qk_out(k, c, par, project, attend)

                norm.scalar(act, lambda i: split_w(0, 0, FIRST_W.index(i)) if i in FIRST_W else None)
                act.wait_ge(gain_ready, 1)
                all_iterations(act, iteration)

            @block.tensor
            def _(pe):
                def project_chunk(k, c, par, project, attend):
                    at = slice(c * P, (c + 1) * P)
                    if not attend:
                        pe.wait_ge(norm.hT_ready, norm.hT_chunks(c + 1))
                    for what, cols in (("qk", slice(0, 2 * W)), ("v", slice(2 * W, 3 * W))):
                        n, bank = proj_use(k, (what, c), project, attend)
                        pe.wait_ge(proj_free, n + 1)
                        out = bank[:, 0:cols.stop - cols.start]
                        for i in range(KC):
                            last = product(pe, out, hT.hi[:, i, at], hT.lo[:, i, at],
                                           w.hi[:, 1 - par, i, cols], w.lo[:, 1 - par, i, cols],
                                           start=(i == 0), stop=(i == KC - 1))
                        last.then_inc(proj_ready, 1)

                def qk_turn(k, c, project, attend):
                    n, bank = turn_use(k, ("qk", c), project, attend)
                    pe.wait_ge(qk_normed, (k + 1) * TC + c + 1)
                    pe.wait_ge(turn_free, n + 1)
                    for h in range(2 * HPG):
                        last = pe.transpose(core.turn[bank][:, h * P:(h + 1) * P],
                                            tok[:, c % 3, h * P:(h + 1) * P], core.ident[:])
                    last.then_inc(turn_ready, 1)

                def scores(k, s, par):
                    b, h, qc = unit(s)
                    t0 = b * SEQ + qc * P
                    pe.wait_ge(score_free, k * UNITS + s + 1)
                    pe.matmul(core.score[s % 2][:, 0:SEQ], qT[:, par, h, t0:t0 + P],
                              kT[:, par, h, b * SEQ:(b + 1) * SEQ], start=True, stop=True).then_inc(score_ready, 1)

                def probs_turn(k, s, project, attend):
                    n, bank = turn_use(k, ("probs", s), project, attend)
                    pe.wait_ge(probs_ready, k * UNITS + s + 1)
                    pe.wait_ge(turn_free, n + 1)
                    for i in range(QC):
                        last = pe.transpose(core.turn[bank][:, i * P:(i + 1) * P],
                                            probs[:, s % 4, i * P:(i + 1) * P], core.ident[:])
                    last.then_inc(turn_ready, 1)

                def weigh(k, u, par, project, attend):
                    b, h, _ = unit(2 * u)
                    n, _ = turn_use(k, ("probs", 2 * u + 1), project, attend)
                    pe.wait_ge(turn_free, n + 1 + RING)
                    pe.wait_ge(outp_free, k * OUTS + u + 1)
                    for i in range(QC):
                        last = pe.matmul(core.outp[u % 2][:, 0:SEQ], v[:, par, QC * b + i, h * P:(h + 1) * P],
                                         probsT[:, u % 2, i, :], start=(i == 0), stop=(i == QC - 1))
                    last.then_inc(outp_ready, 1)

                def output(k, i, project):
                    if i % QC == 0:
                        pe.wait_ge(outp_free, k * OUTS + (i // QC + 1) * HPG + RING)
                    if i == 0:
                        pe.wait_ge(wo_ready, k + 1)
                    n, bank = proj_use(k, ("out", i), project, True)
                    pe.wait_ge(proj_free, n + 1)
                    at = slice(i * P, (i + 1) * P)
                    for h in range(HPG):
                        last = product(pe, bank[:, :], outT.hi[:, h, at], outT.lo[:, h, at],
                                       wo.hi[:, h, :], wo.lo[:, h, :], start=(h == 0), stop=(h == HPG - 1))
                    last.then_inc(proj_ready, 1)

                def iteration(k, par, project, attend, split):
                    if project:
                        pe.wait_ge(w_ready, (k + 2) * PIECES)
                    for c in range(TC):
                        if project:
                            project_chunk(k, c, par, project, attend)
                            if c >= 2:
                                qk_turn(k, c - 2, project, attend)
                        if attend:
                            if c == 0:
                                pe.wait_ge(turn_free, turn_base(k) + RING)
                                pe.wait_ge(proj_free, proj_base(k) + RING)
                            for s in (2 * c, 2 * c + 1):
                                scores(k, s, par)
                                if s >= 2:
                                    probs_turn(k, s - 2, project, attend)
                                if s >= 4 and s % 2 == 0:
                                    weigh(k, (s - 4) // 2, par, project, attend)
                            if c in OUT_STEPS:
                                output(k, OUT_STEPS[c], project)
                    if attend:
                        probs_turn(k, UNITS - 2, project, attend)
                        weigh(k, OUTS - 2, par, project, attend)
                        output(k, len(OUT_STEPS), project)
                        probs_turn(k, UNITS - 1, project, attend)
                        output(k, len(OUT_STEPS) + 1, project)
                        weigh(k, OUTS - 1, par, project, attend)
                    if project:
                        for c in (TC - 2, TC - 1):
                            qk_turn(k, c, project, attend)
                    if attend:
                        for i in range(len(OUT_STEPS) + 2, TC):
                            output(k, i, project)

                def turn_base(k):
                    return TC + k * len(TURNS)

                norm.tensor(pe)
                all_iterations(pe, iteration)


def context_attention(nc, core, io, name, eps):
    GROUPS = 8
    W = HG * P
    KCH = B * CTX // P
    ITEMS = KCH + TC
    ROWS = B * QC
    PIECES = KC
    FIRST_W = range(2, 2 + PIECES)
    SCORES = {2 * h: h for h in range(HG)}
    PROBS = {2 * h + 3: h for h in range(HG)}
    WEIGH = {2 * h + 4: h for h in range(HG - 1)}
    TURNS = []
    for c in range(ITEMS):
        TURNS += [("item", c - 2)] * (c >= 2)
        TURNS += [("probs", PROBS[c])] if c in PROBS else []
    TURNS += [("item", ITEMS - 2), ("item", ITEMS - 1)]

    with ExitStack() as ctx:
        sb = lambda n, shape: ctx.enter_context(nc.sbuf_tensor(f"{name}_{n}", shape, F32))
        sem = lambda n: core.hold.enter_context(nc.semaphore(f"{name}_{n}"))
        hT = Pair(nc, ctx, f"{name}_hT", [P, KC, T])
        ctxT = Pair(nc, ctx, f"{name}_ctxT", [P, KC, B * CTX])
        w = Pair(nc, ctx, f"{name}_w", [P, KC, W + 2 * P])
        raw = sb("raw", [P, KC, W + 2 * P])
        raw_o = sb("raw_o", [P, HG, D])
        wo = Pair(nc, ctx, f"{name}_wo", [P, HG, D])
        mask = sb("mask", [P, B // 2, QC, 2, CTX])
        gains = sb("gains", [P, 2])
        gain = sb("gain", [P, 1])
        epsilon = sb("epsilon", [P, HG])
        tok = sb("tok", [P, 3, W])
        sq = sb("sq", [P, W])
        ss = sb("ss", [P, 2, HG])
        ms = sb("ms", [P, 2, HG])
        rms = sb("rms", [P, 2, HG])
        qT = sb("qT", [P, 2, HG, T])
        raw_ctx = qT[:, 1, 0, :].rearrange("p (k n) -> p k n", k=KC)
        kT = sb("kT", [P, 2, B * CTX])
        v = sb("v", [P, 2, KCH, P])
        logits = sb("logits", [P, ROWS * CTX])
        exps = sb("exps", [P, 2, ROWS * CTX])
        core.h = exps
        top = sb("top", [P, 2, ROWS])
        total = sb("total", [P, 2, ROWS])
        turned = sb("turned", [P, B // 2, SEQ])
        outT = Pair(nc, ctx, f"{name}_outT", [P, HG, T])

        ctx_loaded = sem("ctx_loaded")
        ctx_hi_ready = sem("ctx_hi_ready")
        ctx_ready = sem("ctx_ready")
        consts_loaded = sem("consts_loaded")
        gain_ready = sem("gain_ready")
        w_loaded = sem("w_loaded")
        wo_loaded = sem("wo_loaded")
        w_hi_ready = sem("w_hi_ready")
        w_ready = sem("w_ready")
        wo_hi_ready = sem("wo_hi_ready")
        wo_ready = sem("wo_ready")
        proj_ready = sem("proj_ready")
        item_free = sem("item_free")
        out_free = sem("out_free")
        sq_ready = sem("sq_ready")
        ss_ready = sem("ss_ready")
        ms_ready = sem("ms_ready")
        rms_ready = sem("rms_ready")
        normed = sem("normed")
        turn_ready = sem("turn_ready")
        turn_free = sem("turn_free")
        score_ready = sem("score_ready")
        score_free = sem("score_free")
        max_ready = sem("max_ready")
        shifted_ready = sem("shifted_ready")
        exps_ready = sem("exps_ready")
        total_ready = sem("total_ready")
        rsum_ready = sem("rsum_ready")
        probs_ready = sem("probs_ready")
        outp_ready = sem("outp_ready")
        out_hi_ready = sem("out_hi_ready")
        outp_free = sem("outp_free")

        norm = Norm(core, hT)
        w_dram = [io[f"L0_xattn_{n}"].rearrange("(k p) n -> p k n", p=P) for n in "qkv"]
        wo_dram = io["L0_xattn_o"].rearrange("(n p) d -> p n d", p=P)

        heads = lambda n: 1 if n < KCH else HG
        proj_base = lambda k: ITEMS + k * (ITEMS + TC) if not isinstance(k, int) or k >= 0 else 0
        out_use = lambda k, i, project: proj_base(k) + (ITEMS if project else 0) + i

        def turn_use(k, what, project, attend):
            order = [t for t in TURNS if (t[0] == "item" and project) or (t[0] == "probs" and attend)]
            n = order.index(what)
            base = ITEMS + k * len(TURNS) if not isinstance(k, int) or k >= 0 else 0
            return base + n, n % 2

        def all_iterations(engine, iteration):
            iteration(-1, 1, True, False, True)
            with engine.Fori(0, (GROUPS - 2) // 2) as i:
                for par in range(2):
                    iteration(i * 2 + par, par, True, True, True)
            iteration(GROUPS - 2, 0, True, True, False)
            iteration(GROUPS - 1, 1, False, True, False)

        with nc.Block() as block:

            @block.sync
            def _(sp):
                def load_w(g):
                    for j, (at, n) in enumerate(((0, W), (W, P), (W + P, P))):
                        sp.dma_start(raw[:, :, at:at + n], w_dram[j][:, :, ds(g * n, n)]).then_inc(w_loaded, 16)

                def load_wo(g):
                    sp.dma_start(raw_o[:], wo_dram[:, ds(g * HG, HG), :]).then_inc(wo_loaded, 16)

                sp.dma_start(raw_ctx, io["ctxT"].rearrange("(k p) n -> p k n", p=P)).then_inc(ctx_loaded, 16)
                load_w(0)
                sp.dma_start(gains[:, 0:1], io["L0_xattn_gq"].unsqueeze(1)).then_inc(consts_loaded, 16)
                sp.dma_start(gains[:, 1:2], io["L0_xattn_gk"].unsqueeze(1)).then_inc(consts_loaded, 16)
                for a in range(B // 2):
                    for b in range(2):
                        sp.dma_start(mask[:, a, :, b, :], io["mask"].rearrange("(c p) k -> p c k", p=P))\
                            .then_inc(consts_loaded, 16)
                load_wo(0)

                def loads(k):
                    sp.wait_ge(w_ready, (k + 2) * PIECES)
                    load_w(k + 2)
                    sp.wait_ge(wo_ready, (k + 1) * HG)
                    load_wo(k + 1)

                sp.wait_ge(w_ready, PIECES)
                load_w(1)
                with sp.Fori(0, GROUPS - 2) as k:
                    loads(k)
                sp.wait_ge(wo_ready, (GROUPS - 1) * HG)
                load_wo(GROUPS - 1)

            @block.gpsimd
            def _(pool):
                pool.memset(epsilon[:], eps).then_inc(ms_ready, 1)
                pool.wait_ge(ms_ready, 1)
                norm.gpsimd(pool)

                def split_w(g, pieces):
                    for piece in pieces:
                        pool.wait_ge(w_hi_ready, g * PIECES + piece + 1)
                        pool.tensor_tensor(w.lo[:, piece, :], raw[:, piece, :], w.hi[:, piece, :].bitcast(F32),
                                           ALU.subtract).then_inc(w_ready, 1)

                def iteration(k, par, project, attend, split):
                    for c in range(ITEMS):
                        if project:
                            n, hs = (k + 1) * ITEMS + c, heads(c)
                            pool.wait_ge(ss_ready, n + 1)
                            pool.tensor_tensor(ms[:, c % 2, 0:hs], ss[:, c % 2, 0:hs], epsilon[:, 0:hs], ALU.add)\
                                .then_inc(ms_ready, 1)
                            pool.wait_ge(ms_ready, n + 2)
                            pool.tensor_tensor(rms[:, c % 2, 0:hs], ms[:, c % 2, 0:hs], core.neg_half[:, 0:hs],
                                               ALU.pow).then_inc(rms_ready, 1)
                        if attend and c < HG:
                            pool.wait_ge(wo_hi_ready, k * HG + c + 1)
                            pool.tensor_tensor(wo.lo[:, c, :], raw_o[:, c, :], wo.hi[:, c, :].bitcast(F32),
                                               ALU.subtract).then_inc(wo_ready, 1)
                    if split:
                        split_w(k + 2, range(PIECES if attend else PIECES // 2))

                all_iterations(pool, iteration)

            @block.vector
            def _(dve):
                dve.sem_inc(out_free, RING)
                rows = lambda a: a.rearrange("p (r k) -> p r k", k=CTX)
                each = lambda a: a.unsqueeze(2).broadcast_to([P, ROWS, CTX])

                def lower_w(g, piece):
                    dve.wait_ge(w_hi_ready, g * PIECES + piece + 1)
                    dve.tensor_tensor(w.lo[:, piece, :], raw[:, piece, :], w.hi[:, piece, :].bitcast(F32),
                                      ALU.subtract).then_inc(w_ready, 1)

                def first_split(i):
                    if i == FIRST_W[0] - 1:
                        dve.wait_ge(ctx_hi_ready, 1)
                        dve.tensor_tensor(ctxT.lo[:], raw_ctx, ctxT.hi[:].bitcast(F32), ALU.subtract)\
                            .then_inc(ctx_ready, 1)
                    if i in FIRST_W:
                        lower_w(0, FIRST_W.index(i))

                norm.vector(dve, first_split)
                dve.wait_ge(consts_loaded, 32 + 16 * B)
                dve.scalar_tensor_tensor(gain[:], gains[:, 0:1], float(P) ** -0.5, gains[:, 1:2],
                                         ALU.mult, ALU.mult).then_inc(gain_ready, 1)

                def normalise(k, c):
                    hs = heads(c)
                    dve.wait_ge(rms_ready, (k + 1) * ITEMS + c + 1)
                    t = tok[:, c % 3, 0:hs * P].rearrange("p (h d) -> p h d", d=P)
                    dve.tensor_tensor(t, t, rms[:, c % 2, 0:hs].unsqueeze(2).broadcast_to([P, hs, P]),
                                      ALU.mult).then_inc(normed, 1)

                def shift(k, h):
                    s = h % 2
                    dve.wait_ge(score_ready, k * HG + h + 1)
                    dve.tensor_tensor(logits[:], core.score[s][:, :],
                                      mask[:].rearrange("p a q b k -> p (a q b k)"), ALU.add).then_inc(score_free, 1)
                    dve.wait_ge(score_free, k * HG + h + 1 + RING)
                    dve.tensor_reduce(top[:, s, :], rows(logits[:]), AX.X, ALU.max).then_inc(max_ready, 1)
                    dve.wait_ge(max_ready, k * HG + h + 1)
                    dve.tensor_tensor(rows(logits[:]), rows(logits[:]), each(top[:, s, :]),
                                      ALU.subtract).then_inc(shifted_ready, 1)

                def divide(k, h):
                    s = h % 2
                    dve.wait_ge(exps_ready, k * HG + h + 1)
                    dve.tensor_reduce(total[:, s, :], rows(exps[:, s, :]), AX.X, ALU.add).then_inc(total_ready, 1)
                    dve.wait_ge(total_ready, k * HG + h + 1)
                    dve.reciprocal(total[:, s, :], total[:, s, :]).then_inc(rsum_ready, 1)
                    dve.wait_ge(rsum_ready, k * HG + h + 1)
                    dve.tensor_tensor(rows(exps[:, s, :]), rows(exps[:, s, :]), each(total[:, s, :]),
                                      ALU.mult).then_inc(probs_ready, 1)

                def out_lo(k, h):
                    dve.wait_ge(out_hi_ready, k * HG + h + 1)
                    hi, lo = (o[:, h, :].rearrange("p (a b t) -> p a b t", a=B // 2, b=2) for o in (outT.hi, outT.lo))
                    for b in range(2):
                        last = dve.tensor_tensor(lo[:, :, b, :], core.outp[b][:, :].rearrange("p (a t) -> p a t", t=SEQ),
                                                 hi[:, :, b, :].bitcast(F32), ALU.subtract)
                    last.then_inc(outp_free, 1)

                def iteration(k, par, project, attend, split):
                    for c in range(ITEMS):
                        if project:
                            hs = heads(c)
                            dve.wait_ge(sq_ready, (k + 1) * ITEMS + c + 1)
                            dve.tensor_reduce(ss[:, c % 2, 0:hs], sq[:, 0:hs * P].rearrange("p (h d) -> p h d", d=P),
                                              AX.X, ALU.add).then_inc(ss_ready, 1)
                            if c >= 1:
                                normalise(k, c - 1)
                        if attend:
                            if c in SCORES:
                                shift(k, SCORES[c])
                            if c - 1 in SCORES:
                                divide(k, SCORES[c - 1])
                            if c in WEIGH:
                                out_lo(k, WEIGH[c])
                    if project:
                        normalise(k, ITEMS - 1)
                    if attend:
                        out_lo(k, HG - 1)
                    if not attend:
                        for piece in range(PIECES // 2, PIECES):
                            lower_w(1, piece)
                    if attend:
                        for i in range(TC):
                            dve.wait_ge(proj_ready, out_use(k, i, project) + 1)
                            dve.tensor_tensor(core.x[:, i, :], core.proj[i % 2][:, :], core.x[:, i, :],
                                              ALU.add).then_inc(out_free, 1)

                all_iterations(dve, iteration)

            @block.scalar
            def _(act):
                act.sem_inc(turn_free, RING)
                act.sem_inc(score_free, RING)
                act.sem_inc(outp_free, 1)

                def split_w(g, pieces=range(PIECES)):
                    if pieces[0] == 0:
                        act.wait_ge(w_loaded, (g + 1) * 48)
                    for piece in pieces:
                        act.copy(w.hi[:, piece, :], raw[:, piece, :]).then_inc(w_hi_ready, 1)

                def item_out(k, c, par):
                    act.wait_ge(proj_ready, proj_base(k) + c + 1)
                    hs = heads(c)
                    if c < KCH:
                        act.copy(v[:, 1 - par, c, :], core.proj[c % 2][:, P:2 * P])
                    act.copy(tok[:, c % 3, 0:hs * P], core.proj[c % 2][:, 0:hs * P]).then_inc(item_free, 1)
                    act.wait_ge(item_free, (k + 1) * ITEMS + c + 1)
                    if not (isinstance(k, int) and k < 0 and c == 0):
                        act.wait_ge(ss_ready, (k + 1) * ITEMS + c)
                    act.activation(sq[:, 0:hs * P], tok[:, c % 3, 0:hs * P], ACT.Square,
                                   scale=float(P) ** -0.5).then_inc(sq_ready, 1)

                def turn_out(k, c, par, project, attend):
                    n, bank = turn_use(k, ("item", c), project, attend)
                    act.wait_ge(turn_ready, n + 1)
                    if c < KCH:
                        ins = act.copy(kT[:, 1 - par, c * P:(c + 1) * P], core.turn[bank][:, 0:P])
                    else:
                        ins = act.activation(qT[:, 1 - par, :, (c - KCH) * P:(c - KCH + 1) * P],
                                             core.turn[bank][:, :].rearrange("p (h t) -> p h t", t=P),
                                             ACT.Copy, scale=gain[:, 0:1])
                    ins.then_inc(turn_free, 1)

                def out_hi(k, h):
                    act.wait_ge(outp_ready, k * HG + h + 1)
                    hi = outT.hi[:, h, :].rearrange("p (a b t) -> p a b t", a=B // 2, b=2)
                    for b in range(2):
                        last = act.copy(hi[:, :, b, :], core.outp[b][:, :].rearrange("p (a t) -> p a t", t=SEQ))
                    last.then_inc(out_hi_ready, 1)

                def iteration(k, par, project, attend, split):
                    for c in range(ITEMS):
                        if project:
                            item_out(k, c, par)
                            if c >= 2:
                                turn_out(k, c - 2, par, project, attend)
                        if attend and c < HG:
                            if c == 0:
                                act.wait_ge(proj_ready, proj_base(k))
                                act.wait_ge(wo_loaded, (k + 1) * 16)
                            act.copy(wo.hi[:, c, :], raw_o[:, c, :]).then_inc(wo_hi_ready, 1)
                        if attend:
                            if c in PROBS:
                                h = PROBS[c]
                                n, bank = turn_use(k, ("probs", h), project, attend)
                                act.wait_ge(turn_ready, n + 1)
                                act.copy(turned[:].rearrange("p a q -> p (a q)"), core.turn[bank][:, :])\
                                    .then_inc(turn_free, 1)
                            if c in SCORES:
                                h = SCORES[c]
                                act.wait_ge(shifted_ready, k * HG + h + 1)
                                act.activation(exps[:, h % 2, :], logits[:], ACT.Exp).then_inc(exps_ready, 1)
                            if c in WEIGH:
                                out_hi(k, WEIGH[c])
                    if project:
                        turn_out(k, ITEMS - 2, par, project, attend)
                    if attend:
                        out_hi(k, HG - 1)
                    if project:
                        turn_out(k, ITEMS - 1, par, project, attend)
                    if split:
                        split_w(k + 2)

                def first_split(i):
                    if i == FIRST_W[0] - 1:
                        act.wait_ge(ctx_loaded, 16)
                        act.copy(ctxT.hi[:], raw_ctx).then_inc(ctx_hi_ready, 1)
                    if i in FIRST_W:
                        split_w(0, [FIRST_W.index(i)])

                norm.scalar(act, first_split)
                act.wait_ge(gain_ready, 1)
                all_iterations(act, iteration)

            @block.tensor
            def _(pe):
                def project_item(k, c):
                    if not (isinstance(k, int) and k < 0 and c < RING):
                        pe.wait_ge(item_free, (k + 1) * ITEMS + c - 1)
                    if c < RING and not (isinstance(k, int) and k < 0):
                        pe.wait_ge(out_free, k * TC + c + 1)
                    src, i, cols = (ctxT, c, slice(W, W + 2 * P)) if c < KCH else (hT, c - KCH, slice(0, W))
                    at = slice(i * P, (i + 1) * P)
                    if src is hT and isinstance(k, int) and k < 0:
                        pe.wait_ge(norm.hT_ready, norm.hT_chunks(i + 1))
                    for j in range(KC):
                        last = product(pe, core.proj[c % 2][:, 0:cols.stop - cols.start], src.hi[:, j, at],
                                       src.lo[:, j, at], w.hi[:, j, cols], w.lo[:, j, cols],
                                       start=(j == 0), stop=(j == KC - 1))
                    last.then_inc(proj_ready, 1)

                def turn_item(k, c, project, attend):
                    n, bank = turn_use(k, ("item", c), project, attend)
                    pe.wait_ge(normed, (k + 1) * ITEMS + c + 1)
                    pe.wait_ge(turn_free, n + 1)
                    for h in range(heads(c)):
                        last = pe.transpose(core.turn[bank][:, h * P:(h + 1) * P],
                                            tok[:, c % 3, h * P:(h + 1) * P], core.ident[:])
                    last.then_inc(turn_ready, 1)

                def scores(k, h, par):
                    pe.wait_ge(score_free, k * HG + h + 1)
                    for b in range(B):
                        for qc in range(QC):
                            t0 = b * SEQ + qc * P
                            at = ((b // 2 * QC + qc) * 2 + b % 2) * CTX
                            last = pe.matmul(core.score[h % 2][:, at:at + CTX], qT[:, par, h, t0:t0 + P],
                                             kT[:, par, b * CTX:(b + 1) * CTX], start=True, stop=True)
                    last.then_inc(score_ready, 1)

                def turn_probs(k, h, project, attend):
                    n, bank = turn_use(k, ("probs", h), project, attend)
                    pe.wait_ge(probs_ready, k * HG + h + 1)
                    pe.wait_ge(turn_free, n + 1)
                    for a in range(B // 2 * QC):
                        last = pe.transpose(core.turn[bank][:, a * P:(a + 1) * P],
                                            exps[:, h % 2, a * P:(a + 1) * P], core.ident[:])
                    last.then_inc(turn_ready, 1)

                def weigh(k, h, par, project, attend):
                    n, _ = turn_use(k, ("probs", h), project, attend)
                    pe.wait_ge(turn_free, n + 1 + RING)
                    pe.wait_ge(outp_free, k * HG + h + 1)
                    for b in range(B):
                        rows = slice(b % 2 * CTX, (b % 2 + 1) * CTX)
                        last = pe.matmul(core.outp[b % 2][:, b // 2 * SEQ:(b // 2 + 1) * SEQ],
                                         v[rows, par, b // 2, :], turned[rows, b // 2, :],
                                         start=True, stop=True)
                    last.then_inc(outp_ready, 1)

                def output(k, i, project, heads=range(HG)):
                    if heads[0] == 0:
                        if i == 0:
                            pe.wait_ge(wo_ready, (k + 1) * HG)
                        if project and i < RING:
                            pe.wait_ge(item_free, (k + 2) * ITEMS + i - 1)
                        pe.wait_ge(out_free, k * TC + i + 1)
                    at = slice(i * P, (i + 1) * P)
                    for h in heads:
                        if i == 0:
                            pe.wait_ge(outp_free, k * HG + h + 2)
                        last = product(pe, core.proj[i % 2][:, :], outT.hi[:, h, at], outT.lo[:, h, at],
                                       wo.hi[:, h, :], wo.lo[:, h, :], start=(h == 0), stop=(h == HG - 1))
                    if h == HG - 1:
                        last.then_inc(proj_ready, 1)

                def iteration(k, par, project, attend, split):
                    if project:
                        pe.wait_ge(w_ready, (k + 2) * PIECES)
                    for c in range(ITEMS):
                        if project:
                            project_item(k, c)
                            if c >= 2:
                                turn_item(k, c - 2, project, attend)
                        if attend:
                            if c == 0:
                                pe.wait_ge(turn_free, ITEMS + k * len(TURNS) + RING)
                            if c in PROBS:
                                turn_probs(k, PROBS[c], project, attend)
                            if c in SCORES:
                                scores(k, SCORES[c], par)
                            if c in WEIGH:
                                weigh(k, WEIGH[c], par, project, attend)
                    if attend:
                        output(k, 0, project, range(HG - 1))
                    if project:
                        turn_item(k, ITEMS - 2, project, attend)
                    if attend:
                        weigh(k, HG - 1, par, project, attend)
                    if project:
                        turn_item(k, ITEMS - 1, project, attend)
                    if attend:
                        output(k, 1, project, range(HG - 1))
                        for i in range(2):
                            output(k, i, project, range(HG - 1, HG))
                    if attend:
                        for i in range(2, TC):
                            output(k, i, project)

                norm.tensor(pe)
                pe.wait_ge(ctx_ready, 1)
                all_iterations(pe, iteration)


def latent_attention(nc, core, io, name):
    GROUPS, DH = 4, 96
    KEYS = SEQ + CTX
    KEY_CHUNKS = [P, P, CTX]
    W = HG * DH
    UNITS = HG * B * QC
    OUTS = UNITS // QC
    HALVES = T // D
    STEPS = HG * HALVES
    PER_STEP = UNITS // STEPS
    Q_STEPS = {c: ((c - HALVES) // HALVES, c % HALVES) for c in range(HALVES, STEPS)}
    WO_STEPS = {1: 0, 2: 1, 4: 2, 5: 3}
    HEAD = [("q", HG - 1, i) for i in range(HALVES)]
    TAIL = [("k", b) for b in range(B)]
    PROJ = HEAD + [("q", *Q_STEPS[c]) for c in sorted(Q_STEPS)] + TAIL + [("out", i) for i in range(TC)]
    FIRST = [("v", i) for i in range(TC)] + [("vc", b) for b in range(B)] + [("k", b) for b in range(B)] \
        + [("q", h, i) for h in range(HG - 1) for i in range(HALVES)]

    with ExitStack() as ctx:
        sb = lambda n, shape: ctx.enter_context(nc.sbuf_tensor(f"{name}_{n}", shape, F32))
        sem = lambda n: core.hold.enter_context(nc.semaphore(f"{name}_{n}"))
        hT = Pair(nc, ctx, f"{name}_hT", [P, KC, B * KEYS])
        raw = sb("raw", [P, KC, W + DH])
        w = Pair(nc, ctx, f"{name}_w", [P, KC, W + DH])
        raw_o = sb("raw_o", [P, HG // 2, D])
        raw_ctx = raw_o[:].rearrange("p h (k n) -> p (h k) n", n=B * CTX)[:, 0:KC, :]
        wo = Pair(nc, ctx, f"{name}_wo", [DH, HG, D])
        qT = Pair(nc, ctx, f"{name}_qT", [DH, HG, T])
        kT = Pair(nc, ctx, f"{name}_kT", [DH, B, KEYS])
        v = sb("v", [P, TC, W])
        vc = sb("vc", [CTX, B, W])
        vg = sb("vg", [P, TC, DH])
        vcg = sb("vcg", [CTX, B, DH])
        probs = sb("probs", [P, 4, KEYS])
        core.h = probs[:].rearrange("p a k -> p (a k)")[:, 0:2 * D].rearrange("p (a d) -> p a d", a=2)
        nmax = sb("nmax", [P, 4])
        sums = sb("sums", [P, 4])
        rsum = sb("rsum", [P, 4])
        probsT = sb("probsT", [P, 2, len(KEY_CHUNKS), SEQ])
        outT = Pair(nc, ctx, f"{name}_outT", [DH, HG, T])

        ctx_loaded = sem("ctx_loaded")
        ctx_hi_ready = sem("ctx_hi_ready")
        ctx_ready = sem("ctx_ready")
        w_loaded = sem("w_loaded")
        w_hi_ready = sem("w_hi_ready")
        w_ready = sem("w_ready")
        wo_loaded = sem("wo_loaded")
        wo_hi_ready = sem("wo_hi_ready")
        wo_ready = sem("wo_ready")
        proj_ready = sem("proj_ready")
        proj_hi_ready = sem("proj_hi_ready")
        proj_free = sem("proj_free")
        vg_ready = sem("vg_ready")
        turn_ready = sem("turn_ready")
        turn_free = sem("turn_free")
        score_ready = sem("score_ready")
        score_free = sem("score_free")
        max_ready = sem("max_ready")
        rsum_ready = sem("rsum_ready")
        probs_ready = sem("probs_ready")
        outp_ready = sem("outp_ready")
        out_hi_ready = sem("out_hi_ready")
        outp_free = sem("outp_free")

        column = lambda i: i // QC * KEYS + i % QC * P
        norm = Norm(core, hT, column=column)
        w_dram = [io[f"L1_xattn_{n}"].rearrange("(k p) n -> p k n", p=P) for n in "qkv"]
        wo_dram = io["L1_xattn_o"].rearrange("(n p) d -> p n d", p=DH)
        batches = lambda tile: tile.rearrange("p k (b s) -> p k b s", s=KEYS)
        context = lambda tile: batches(tile)[:, :, :, SEQ:KEYS]
        by_batch = lambda tile: tile.rearrange("p k (b n) -> p k b n", n=CTX)

        split_before = lambda g: 3 + (g - 1) * KC
        first = lambda k: isinstance(k, int) and k < 0
        proj_base = lambda k: 0 if first(k) else len(FIRST) + k * len(PROJ)
        PAIRS = len(HEAD) + len(TAIL) + len(Q_STEPS)
        pair_base = lambda k: 0 if first(k) else (k + 1) * PAIRS - len(HEAD)
        unit = lambda s: (s // (B * QC), s // QC % B, s % QC)

        def order_of(k, project):
            return FIRST if first(k) else PROJ if project else [u for u in PROJ if u[0] == "out" or u in HEAD]

        def proj_use(k, what, project):
            n = order_of(k, project).index(what)
            return proj_base(k) + n, core.proj[n % 2]

        def pair_use(k, what):
            return pair_base(k) + [u for u in order_of(k, True) if u[0] in "qk"].index(what)

        def pair_places(what, bank, tile):
            if what[0] == "k":
                return bank[0:DH, 0:KEYS], tile[1][:, what[1], :]
            return bank[0:DH, :], tile[0][:, what[1], what[2] * D:(what[2] + 1) * D]

        def all_iterations(engine, iteration):
            iteration(-1, True, False)
            with engine.Fori(0, GROUPS - 2) as k:
                iteration(k, True, True)
            iteration(GROUPS - 2, True, True)
            iteration(GROUPS - 1, False, True)

        with nc.Block() as block:

            @block.sync
            def _(sp):
                def load_w(g):
                    for j, (at, n) in enumerate(((0, W), (W, DH))):
                        sp.dma_start(raw[:, :, at:at + n], w_dram[j][:, :, ds(g * n, n)]).then_inc(w_loaded, 16)

                def load_wo(m):
                    sp.dma_start(raw_o[0:DH, :, :], wo_dram[:, ds(m * HG // 2, HG // 2), :]).then_inc(wo_loaded, 16)

                def next_wo(m):
                    sp.wait_ge(wo_ready, m * HG // 2)
                    load_wo(m)

                sp.dma_start(raw[:, :, 0:W], w_dram[2]).then_inc(w_loaded, 16)
                sp.dma_start(raw_ctx, io["ctxT"].rearrange("(k p) n -> p k n", p=P)).then_inc(ctx_loaded, 16)
                sp.wait_ge(w_ready, 1)
                load_w(0)
                sp.wait_ge(ctx_ready, 1)
                load_wo(0)
                sp.wait_ge(w_ready, 3)
                load_w(1)

                def loads(k):
                    next_wo(k * 2 + 1)
                    next_wo(k * 2 + 2)
                    sp.wait_ge(w_ready, split_before(k + 2))
                    load_w(k + 2)

                with sp.Fori(0, GROUPS - 2) as k:
                    loads(k)
                for m in range(2 * (GROUPS - 2) + 1, 2 * GROUPS):
                    next_wo(m)

            @block.gpsimd
            def _(pool):
                def split_w(n, cols):
                    pool.wait_ge(w_hi_ready, n + 1)
                    pool.tensor_tensor(w.lo[:, :, cols], raw[:, :, cols], w.hi[:, :, cols].bitcast(F32),
                                       ALU.subtract).then_inc(w_ready, 1)

                def iteration(k, project, attend):
                    if attend:
                        if project:
                            for j in range(KC):
                                pool.wait_ge(w_hi_ready, split_before(k + 1) + j + 1)
                                pool.tensor_tensor(w.lo[:, j, :], raw[:, j, :], w.hi[:, j, :].bitcast(F32),
                                                   ALU.subtract).then_inc(w_ready, 1)
                        for h in range(HG):
                            pool.wait_ge(wo_hi_ready, k * HG + h + 1)
                            pool.tensor_tensor(wo.lo[:, h, :], raw_o[0:DH, h % 2, :], wo.hi[:, h, :].bitcast(F32),
                                               ALU.subtract).then_inc(wo_ready, 1)

                norm.gpsimd(pool)
                split_w(1, slice(W, W + DH))
                split_w(2, slice(0, W))
                all_iterations(pool, iteration)

            @block.vector
            def _(dve):
                dve.sem_inc(proj_free, RING)
                dve.sem_inc(outp_free, RING)

                def first_split(i):
                    if i == 2:
                        dve.wait_ge(w_hi_ready, 1)
                        dve.tensor_tensor(w.lo[:, :, 0:W], raw[:, :, 0:W], w.hi[:, :, 0:W].bitcast(F32), ALU.subtract)\
                            .then_inc(w_ready, 1)
                    if i == 4:
                        dve.wait_ge(ctx_hi_ready, 1)
                        dve.tensor_tensor(context(hT.lo[:]), by_batch(raw_ctx), context(hT.hi[:]).bitcast(F32),
                                          ALU.subtract).then_inc(ctx_ready, 1)

                norm.vector(dve, first_split)

                def copy_values(what):
                    n, bank = proj_use(-1, what, True)
                    dve.wait_ge(proj_ready, n + 1)
                    out = v[:, what[1], :] if what[0] == "v" else vc[:, what[1], :]
                    dve.tensor_copy(out, bank[0:P if what[0] == "v" else CTX, 0:W]).then_inc(proj_free, 1)

                def proj_lo(k, what):
                    _, bank = proj_use(k, what, True)
                    dve.wait_ge(proj_hi_ready, pair_use(k, what) + 1)
                    src, lo = pair_places(what, bank, (qT.lo, kT.lo))
                    _, hi = pair_places(what, bank, (qT.hi, kT.hi))
                    if what[0] == "k":
                        ins = dve.tensor_tensor(lo, src, hi.bitcast(F32), ALU.subtract)
                    else:
                        ins = dve.scalar_tensor_tensor(lo, src, float(DH) ** -0.5, hi.bitcast(F32),
                                                       ALU.mult, ALU.subtract)
                    ins.then_inc(proj_free, 1)

                def divide(k, s):
                    dve.wait_ge(score_free, k * UNITS + s + 1 + RING)
                    dve.reciprocal(rsum[:, s % 4:s % 4 + 1], sums[:, s % 4:s % 4 + 1]).then_inc(rsum_ready, 1)
                    dve.wait_ge(rsum_ready, k * UNITS + s + 1)
                    dve.tensor_scalar(probs[:, s % 4, :], probs[:, s % 4, :], rsum[:, s % 4:s % 4 + 1], None,
                                      ALU.mult).then_inc(probs_ready, 1)

                def out_lo(k, u):
                    h, b, _ = unit(2 * u)
                    dve.wait_ge(out_hi_ready, k * OUTS + u + 1)
                    at = slice(b * SEQ, (b + 1) * SEQ)
                    dve.tensor_tensor(outT.lo[:, h, at], core.outp[u % 2][0:DH, 0:SEQ],
                                      outT.hi[:, h, at].bitcast(F32), ALU.subtract).then_inc(outp_free, 1)

                def iteration(k, project, attend):
                    if not attend:
                        for what in FIRST:
                            if what[0] in "qk":
                                proj_lo(k, what)
                            else:
                                copy_values(what)
                        return
                    dve.tensor_copy(vg[:], v[:, :, ds(k * DH, DH)])
                    dve.tensor_copy(vcg[:], vc[:, :, ds(k * DH, DH)]).then_inc(vg_ready, 1)
                    for c in range(STEPS):
                        if project and c in Q_STEPS:
                            proj_lo(k, ("q", *Q_STEPS[c]))
                        for s in range(c * PER_STEP, (c + 1) * PER_STEP):
                            dve.wait_ge(score_ready, k * UNITS + s + 1)
                            dve.tensor_reduce(nmax[:, s % 4:s % 4 + 1], core.score[s % 2][:, 0:KEYS],
                                              AX.X, ALU.max, negate=True).then_inc(max_ready, 1)
                            if s >= 1:
                                divide(k, s - 1)
                            if s < len(HEAD):
                                proj_lo(k, HEAD[s])
                            if s >= 5 and s % 2 == 1:
                                out_lo(k, (s - 5) // 2)
                    divide(k, UNITS - 1)
                    if project:
                        proj_lo(k, ("k", 0))
                    out_lo(k, OUTS - 2)
                    if project:
                        proj_lo(k, ("k", 1))
                    out_lo(k, OUTS - 1)
                    if project:
                        for what in TAIL[2:]:
                            proj_lo(k, what)
                    for i in range(TC):
                        n, bank = proj_use(k, ("out", i), project)
                        dve.wait_ge(proj_ready, n + 1)
                        dve.tensor_tensor(core.x[:, i, :], bank[:, :], core.x[:, i, :], ALU.add)\
                            .then_inc(proj_free, 1)

                all_iterations(dve, iteration)

            @block.scalar
            def _(act):
                act.sem_inc(turn_free, RING)
                act.sem_inc(score_free, RING)

                def proj_hi(k, what):
                    n, bank = proj_use(k, what, True)
                    act.wait_ge(proj_ready, n + 1)
                    src, hi = pair_places(what, bank, (qT.hi, kT.hi))
                    if what[0] == "k":
                        ins = act.copy(hi, src)
                    else:
                        ins = act.activation(hi, src, ACT.Copy, scale=float(DH) ** -0.5)
                    ins.then_inc(proj_hi_ready, 1)

                def split_w(loads, cols):
                    act.wait_ge(w_loaded, 16 + loads * 32)
                    act.copy(w.hi[:, :, cols], raw[:, :, cols]).then_inc(w_hi_ready, 1)

                def probs_out(k, s):
                    act.wait_ge(turn_ready, k * UNITS + s + 1)
                    qc, u, bank = s % QC, s // QC, core.turn[s % 2]
                    act.copy(probsT[:, u % 2, 0:2, qc * P:(qc + 1) * P],
                             bank[:, 0:2 * P].rearrange("p (k t) -> p k t", t=P))
                    act.copy(probsT[0:CTX, u % 2, 2, qc * P:(qc + 1) * P], bank[0:CTX, 2 * P:3 * P])\
                        .then_inc(turn_free, 1)

                def out_hi(k, u):
                    h, b, _ = unit(2 * u)
                    act.wait_ge(outp_ready, k * OUTS + u + 1)
                    act.copy(outT.hi[:, h, b * SEQ:(b + 1) * SEQ], core.outp[u % 2][0:DH, 0:SEQ])\
                        .then_inc(out_hi_ready, 1)

                def iteration(k, project, attend):
                    if not attend:
                        split_w(1, slice(W, W + DH))
                        act.wait_ge(proj_ready, TC + B)
                        split_w(1, slice(0, W))
                        for what in FIRST[TC + B:]:
                            proj_hi(k, what)
                    else:
                        for c in range(STEPS):
                            if project and c in Q_STEPS:
                                proj_hi(k, ("q", *Q_STEPS[c]))
                            if c in WO_STEPS:
                                h = WO_STEPS[c]
                                if h == 0:
                                    act.wait_ge(proj_ready, proj_base(k))
                                if h % 2 == 0:
                                    act.wait_ge(wo_loaded, (k * 2 + h // 2 + 1) * 16)
                                act.copy(wo.hi[:, h, :], raw_o[0:DH, h % 2, :]).then_inc(wo_hi_ready, 1)
                            for s in range(c * PER_STEP, (c + 1) * PER_STEP):
                                if s >= 3:
                                    probs_out(k, s - 3)
                                act.wait_ge(max_ready, k * UNITS + s + 1)
                                act.activation(probs[:, s % 4, :], core.score[s % 2][:, 0:KEYS], ACT.Exp,
                                               bias=nmax[:, s % 4:s % 4 + 1],
                                               accum_out=sums[:, s % 4:s % 4 + 1]).then_inc(score_free, 1)
                                if s < len(HEAD):
                                    proj_hi(k, HEAD[s])
                                j = s - len(HEAD)
                                if 0 <= j < KC and project:
                                    if j == 0:
                                        act.wait_ge(w_loaded, 16 + (k + 2) * 32)
                                    act.copy(w.hi[:, j, :], raw[:, j, :]).then_inc(w_hi_ready, 1)
                                if s >= 5 and s % 2 == 1:
                                    out_hi(k, (s - 5) // 2)
                        probs_out(k, UNITS - 3)
                        probs_out(k, UNITS - 2)
                        if project:
                            proj_hi(k, ("k", 0))
                        out_hi(k, OUTS - 2)
                        probs_out(k, UNITS - 1)
                        if project:
                            proj_hi(k, ("k", 1))
                        out_hi(k, OUTS - 1)
                        if project:
                            for what in TAIL[2:]:
                                proj_hi(k, what)

                def first_split(i):
                    if i == 2:
                        split_w(0, slice(0, W))
                    if i == 4:
                        act.wait_ge(ctx_loaded, 16)
                        act.copy(context(hT.hi[:]), by_batch(raw_ctx)).then_inc(ctx_hi_ready, 1)

                norm.scalar(act, first_split)
                all_iterations(act, iteration)

            @block.tensor
            def _(pe):
                def project(k, what):
                    n, bank = proj_use(k, what, True)
                    pe.wait_ge(proj_free, n + 1)
                    kind = what[0]
                    for j in range(KC):
                        flags = dict(start=(j == 0), stop=(j == KC - 1))
                        if kind in ("v", "vc"):
                            size = P if kind == "v" else CTX
                            at = column(what[1]) if kind == "v" else what[1] * KEYS + SEQ
                            last = product(pe, bank[0:size, 0:W], hT.hi[:, j, at:at + size], hT.lo[:, j, at:at + size],
                                           w.hi[:, j, 0:W], w.lo[:, j, 0:W], **flags)
                        elif kind == "k":
                            at = slice(what[1] * KEYS, (what[1] + 1) * KEYS)
                            last = product(pe, bank[0:DH, 0:KEYS], w.hi[:, j, W:W + DH], w.lo[:, j, W:W + DH],
                                           hT.hi[:, j, at], hT.lo[:, j, at], **flags)
                        else:
                            h, i = what[1:]
                            cols = slice(h * DH, (h + 1) * DH)
                            per = B // HALVES
                            hi, lo = (batches(tile[:])[:, j, i * per:(i + 1) * per, 0:SEQ] for tile in (hT.hi, hT.lo))
                            last = product(pe, bank[0:DH, :], w.hi[:, j, cols], w.lo[:, j, cols], hi, lo, **flags)
                    last.then_inc(proj_ready, 1)

                def scores(k, s):
                    h, b, qc = unit(s)
                    t0 = b * SEQ + qc * P
                    pe.wait_ge(score_free, k * UNITS + s + 1)
                    product(pe, core.score[s % 2][:, 0:KEYS], qT.hi[:, h, t0:t0 + P], qT.lo[:, h, t0:t0 + P],
                            kT.hi[:, b, :], kT.lo[:, b, :], start=True, stop=True).then_inc(score_ready, 1)

                def probs_turn(k, s):
                    pe.wait_ge(probs_ready, k * UNITS + s + 1)
                    pe.wait_ge(turn_free, k * UNITS + s + 1)
                    for j, n in enumerate(KEY_CHUNKS):
                        last = pe.transpose(core.turn[s % 2][0:n, j * P:(j + 1) * P],
                                            probs[:, s % 4, j * P:j * P + n], core.ident[:])
                    last.then_inc(turn_ready, 1)

                def weigh(k, u):
                    h, b, _ = unit(2 * u)
                    if u == 0:
                        pe.wait_ge(vg_ready, k + 1)
                    pe.wait_ge(turn_free, k * UNITS + 2 * u + 2 + RING)
                    pe.wait_ge(outp_free, k * OUTS + u + 1)
                    for j, n in enumerate(KEY_CHUNKS):
                        values = vg[:, b * QC + j, :] if n == P else vcg[:, b, :]
                        last = pe.matmul(core.outp[u % 2][0:DH, 0:SEQ], values, probsT[0:n, u % 2, j, :],
                                         start=(j == 0), stop=(j == len(KEY_CHUNKS) - 1))
                    last.then_inc(outp_ready, 1)

                def output(k, i, project):
                    n, bank = proj_use(k, ("out", i), project)
                    if i == 0:
                        pe.wait_ge(wo_ready, (k + 1) * HG)
                        pe.wait_ge(outp_free, (k + 1) * OUTS + RING)
                    pe.wait_ge(proj_free, n + 1)
                    at = slice(i * P, (i + 1) * P)
                    for h in range(HG):
                        last = product(pe, bank[:, :], outT.hi[:, h, at], outT.lo[:, h, at],
                                       wo.hi[:, h, :], wo.lo[:, h, :], start=(h == 0), stop=(h == HG - 1))
                    last.then_inc(proj_ready, 1)

                def iteration(k, project_next, attend):
                    if not attend:
                        for what in FIRST:
                            if what[0] == "v":
                                pe.wait_ge(norm.hT_ready, norm.hT_chunks(what[1] + 1))
                            if what == ("vc", 0):
                                pe.wait_ge(ctx_ready, 1)
                            if what == ("k", 0):
                                pe.wait_ge(w_ready, 2)
                            if what == ("q", 0, 0):
                                pe.wait_ge(w_ready, 3)
                            project(k, what)
                        pe.wait_ge(proj_free, len(FIRST) + RING)
                        return
                    pe.wait_ge(proj_free, proj_base(k) - TC + RING)
                    for c in range(STEPS):
                        if project_next and c in Q_STEPS:
                            if c == HALVES:
                                pe.wait_ge(w_ready, split_before(k + 2))
                            project(k, ("q", *Q_STEPS[c]))
                        for s in range(c * PER_STEP, (c + 1) * PER_STEP):
                            if s >= 3:
                                probs_turn(k, s - 3)
                            if s == (HG - 1) * B * QC:
                                pe.wait_ge(proj_free, proj_base(k) + len(HEAD) + RING)
                            scores(k, s)
                            if s < len(HEAD):
                                project(k, HEAD[s])
                            if s >= 5 and s % 2 == 1:
                                weigh(k, (s - 5) // 2)
                    probs_turn(k, UNITS - 3)
                    probs_turn(k, UNITS - 2)
                    if project_next:
                        project(k, ("k", 0))
                    weigh(k, OUTS - 2)
                    probs_turn(k, UNITS - 1)
                    if project_next:
                        project(k, ("k", 1))
                    weigh(k, OUTS - 1)
                    if project_next:
                        for what in TAIL[2:]:
                            project(k, what)
                    for i in range(TC):
                        output(k, i, project_next)

                norm.tensor(pe)
                pe.wait_ge(w_ready, 1)
                all_iterations(pe, iteration)


E = 8


class Router:

    def __init__(self, core, ctx, name, probabilities, logits=None, loads=1):
        nc = core.nc
        self.c = core
        self.probabilities = probabilities
        self.source = logits
        self.loads = loads
        sb = lambda n, shape, dt=F32: ctx.enter_context(nc.sbuf_tensor(f"{name}_{n}", shape, dt))
        sem = lambda n: core.hold.enter_context(nc.semaphore(f"{name}_{n}"))
        self.ids = sb("ids", [P, E])
        self.logits = sb("logits", [P, TC, E])
        self.shifted = sb("shifted", [P, TC, E])
        self.row = sb("row", [P, TC])
        self.top = sb("top", [P, TC, 8])
        self.where = sb("where", [P, TC, 8], U32)
        self.wheref = sb("wheref", [P, TC, 2])
        self.share = sb("share", [P, TC, 2])
        self.chosen = sb("chosen", [P, 2, TC, E])
        self.weight = sb("weight", [P, TC, E])
        self.loaded = sem("ids_loaded")
        self.logits_ready = sem("logits_ready") if logits else None
        self.exp_in_ready = sem("exp_in_ready")
        self.exp_ready = sem("exp_ready")
        self.step = sem("route_step")
        self.steps = 0

    def scalar(self, act):
        act.wait_ge(self.exp_in_ready, 1)
        if self.probabilities:
            act.activation(self.logits[:], self.shifted[:], ACT.Exp).then_inc(self.exp_ready, 1)
        else:
            act.activation(self.share[:, :, 1], self.row[:], ACT.Exp).then_inc(self.exp_ready, 1)

    def vector(self, dve):
        per_row = lambda a: a.unsqueeze(2).broadcast_to([P, TC, E])

        def link(ins):
            self.steps += 1
            ins.then_inc(self.step, 1)
            dve.wait_ge(self.step, self.steps)

        if self.source:
            dve.wait_ge(self.logits_ready, 1)
            link(dve.tensor_copy(self.logits[:], self.source[:, 0:TC * E].rearrange("p (c e) -> p c e", e=E)))
        if self.probabilities:
            link(dve.tensor_reduce(self.row[:], self.logits[:], AX.X, ALU.max))
            dve.tensor_tensor(self.shifted[:], self.logits[:], per_row(self.row[:]), ALU.subtract)\
                .then_inc(self.exp_in_ready, 1)
            dve.wait_ge(self.exp_ready, 1)
            link(dve.tensor_reduce(self.row[:], self.logits[:], AX.X, ALU.add))
            link(dve.reciprocal(self.row[:], self.row[:]))
            link(dve.tensor_tensor(self.logits[:], self.logits[:], per_row(self.row[:]), ALU.mult))
        for i in range(TC):
            ins = dve.max(self.top[:, i, :], self.logits[:, i, :])
        link(ins)
        for i in range(TC):
            ins = dve.max_index(self.where[:, i, :], self.top[:, i, :], self.logits[:, i, :])
        link(ins)
        link(dve.tensor_copy(self.wheref[:], self.where[:, :, 0:2]))
        if self.probabilities:
            link(dve.tensor_tensor(self.row[:], self.top[:, :, 0], self.top[:, :, 1], ALU.add))
            link(dve.reciprocal(self.row[:], self.row[:]))
            for j in range(2):
                ins = dve.tensor_tensor(self.share[:, :, j], self.top[:, :, j], self.row[:], ALU.mult)
            link(ins)
        else:
            dve.tensor_tensor(self.row[:], self.top[:, :, 1], self.top[:, :, 0], ALU.subtract)\
                .then_inc(self.exp_in_ready, 1)
            dve.wait_ge(self.exp_ready, 1)
            link(dve.tensor_scalar(self.row[:], self.share[:, :, 1], 1.0, None, ALU.add))
            link(dve.reciprocal(self.share[:, :, 0], self.row[:]))
            link(dve.tensor_tensor(self.share[:, :, 1], self.share[:, :, 1], self.share[:, :, 0], ALU.mult))
        dve.wait_ge(self.loaded, 16 * self.loads)
        for j in range(2):
            link(dve.tensor_tensor(self.chosen[:, j, :, :], self.ids[:].unsqueeze(1).broadcast_to([P, TC, E]),
                                   per_row(self.wheref[:, :, j]), ALU.is_equal))
            link(dve.tensor_tensor(self.chosen[:, j, :, :], self.chosen[:, j, :, :],
                                   per_row(self.share[:, :, j]), ALU.mult))
        link(dve.tensor_tensor(self.weight[:], self.chosen[:, 0, :, :], self.chosen[:, 1, :, :], ALU.add))


def expert_mixture(nc, core, io, name):
    EARLY = 4
    LAG = 3
    LOGITS = (EARLY, EARLY + 1)
    HALVES = T // D
    with ExitStack() as ctx:
        sb = lambda n, shape: ctx.enter_context(nc.sbuf_tensor(f"{name}_{n}", shape, F32))
        sem = lambda n: core.hold.enter_context(nc.semaphore(f"{name}_{n}"))
        core.h = sb("h", [P, 2, D])
        hT = Pair(nc, ctx, f"{name}_hT", [P, KC, T])
        raw = sb("raw", [P, 2, KC, D])
        w = [Pair(nc, ctx, f"{name}_w{i}", [P, KC, D]) for i in range(2)]
        raw_gate = sb("raw_gate", [P, KC, E])
        gate = Pair(nc, ctx, f"{name}_gate", [P, KC, E])
        logitsT = sb("logitsT", [E, T])
        raw_loaded = [sem(f"raw{i}_loaded") for i in range(2)]
        w_hi_ready = sem("w_hi_ready")
        w_ready = sem("w_ready")
        gate_ready = sem("gate_ready")
        logitsT_ready = sem("logitsT_ready")
        logitsT_copied = sem("logitsT_copied")
        out_ready = sem("out_ready")
        out_free = sem("out_free")
        norm = Norm(core, hT)
        banks = [*core.proj, *core.score, *core.outp, *core.turn]
        route = Router(core, ctx, name, probabilities=False, logits=banks[TC - 2], loads=2)
        FIRST = [i for i in range(TC) if i != TC - 2] + [TC - 2]

        with nc.Block() as block:

            @block.sync
            def _(sp):
                def load(e, par):
                    sp.dma_start(raw[:, par, :, :], io["L0_experts"][ds(e, 1)].rearrange("a (k p) n -> p (a k) n", p=P))\
                        .then_inc(raw_loaded[par], 16)

                load(0, 0)
                sp.dma_start(raw_gate[:], io["L0_gate"].rearrange("(k p) e -> p k e", p=P)).then_inc(route.loaded, 16)
                sp.dma_start(route.ids[:], io["expert_ids"].partition_broadcast(P)).then_inc(route.loaded, 16)
                load(1, 1)
                with sp.Fori(1, E // 2) as i:
                    for par in range(2):
                        sp.wait_ge(w_ready, i * 2 + par - 1)
                        load(i * 2 + par, par)

            @block.gpsimd
            def _(pool):
                def split(e, par):
                    pool.wait_ge(w_hi_ready, e + 1)
                    pool.tensor_tensor(w[par].lo[:], raw[:, par, :, :], w[par].hi[:].bitcast(F32), ALU.subtract)\
                        .then_inc(w_ready, 1)

                norm.gpsimd(pool)
                pool.wait_ge(gate_ready, 1)
                pool.tensor_tensor(gate.lo[:], raw_gate[:], gate.hi[:].bitcast(F32), ALU.subtract)\
                    .then_inc(gate_ready, 1)
                split(1, 1)
                with pool.Fori(1, E // 2) as i:
                    for par in range(2):
                        split(i * 2 + par, par)

            @block.vector
            def _(dve):
                def first_split(i):
                    if i == 1:
                        dve.wait_ge(w_hi_ready, 1)
                        dve.tensor_tensor(w[0].lo[:], raw[:, 0, :, :], w[0].hi[:].bitcast(F32), ALU.subtract)\
                            .then_inc(w_ready, 1)

                norm.vector(dve, first_split)
                route.vector(dve)

                def add(e, i):
                    dve.wait_ge(out_ready, e * TC + (FIRST.index(i) if isinstance(e, int) else i) + 1)
                    dve.scalar_tensor_tensor(core.x[:, i, :], banks[i][:, :], route.weight[:, i, ds(e, 1)],
                                             core.x[:, i, :], ALU.mult, ALU.add).then_inc(out_free, 1)

                for i in range(TC):
                    add(0, i)
                with dve.Fori(1, E) as e:
                    for i in range(TC):
                        add(e, i)

            @block.scalar
            def _(act):
                def split(e, par):
                    act.wait_ge(raw_loaded[par], (e - par) * 8 + 16 if not isinstance(e, int) else e // 2 * 16 + 16)
                    if not isinstance(e, int) or e >= 2:
                        act.wait_ge(out_ready, (e - 1) * TC)
                    act.copy(w[par].hi[:], raw[:, par, :, :]).then_inc(w_hi_ready, 1)

                def first_split(i):
                    if i == 1:
                        split(0, 0)
                    if i == 2:
                        act.wait_ge(route.loaded, 32)
                        act.copy(gate.hi[:], raw_gate[:]).then_inc(gate_ready, 1)

                norm.scalar(act, first_split)
                split(1, 1)
                for i in range(HALVES):
                    act.wait_ge(logitsT_ready, i + 1)
                    act.copy(logitsT[:, i * D:(i + 1) * D], banks[LOGITS[i]][0:E, :]).then_inc(logitsT_copied, 1)
                route.scalar(act)
                with act.Fori(1, E // 2) as i:
                    for par in range(2):
                        split(i * 2 + par, par)

            @block.tensor
            def _(pe):
                def expert(par, i):
                    at = slice(i * P, (i + 1) * P)
                    for k in range(KC):
                        last = product(pe, banks[i][:, :], hT.hi[:, k, at], hT.lo[:, k, at], w[par].hi[:, k, :],
                                       w[par].lo[:, k, :], start=(k == 0), stop=(k == KC - 1))
                    last.then_inc(out_ready, 1)

                def early(i):
                    if 0 <= i - LAG < EARLY:
                        pe.wait_ge(norm.hT_ready, norm.n0 + i - LAG + 1)
                        pe.wait_ge(w_ready, 1)
                        expert(0, i - LAG)

                norm.tensor(pe, early)
                pe.wait_ge(norm.hT_ready, norm.hT_done)
                pe.wait_ge(gate_ready, 2)
                for i in range(HALVES):
                    tokens = slice(i * D, (i + 1) * D)
                    for k in range(KC):
                        last = product(pe, banks[LOGITS[i]][0:E, :], gate.hi[:, k, :], gate.lo[:, k, :],
                                       hT.hi[:, k, tokens], hT.lo[:, k, tokens], start=(k == 0), stop=(k == KC - 1))
                    last.then_inc(logitsT_ready, 1)
                pe.wait_ge(logitsT_copied, HALVES)
                for i in range(TC):
                    last = pe.transpose(route.source[:, i * E:(i + 1) * E], logitsT[:, i * P:(i + 1) * P],
                                        core.ident[0:E, 0:E])
                last.then_inc(route.logits_ready, 1)
                for i in FIRST[EARLY:]:
                    if i == TC - 2:
                        pe.wait_ge(route.step, 1)
                    expert(0, i)

                def experts(e, par):
                    pe.wait_ge(w_ready, e + 1)
                    for i in range(TC):
                        pe.wait_ge(out_free, (e - 1) * TC + i + 1)
                        expert(par, i)

                experts(1, 1)
                with pe.Fori(1, E // 2) as i:
                    for par in range(2):
                        experts(i * 2 + par, par)


def adapted_linear(nc, core, io, name, out):
    R = 16
    SCALING = 16.0 / R
    LOW, GATE, COLS = D, D + E * R, D + E * R + E
    HALF = COLS // 2
    DEPTH = 3
    EARLY = TC - DEPTH
    FIRST_W = range(1, 1 + KC)
    with ExitStack() as ctx:
        sb = lambda n, shape: ctx.enter_context(nc.sbuf_tensor(f"{name}_{n}", shape, F32))
        sem = lambda n: core.hold.enter_context(nc.semaphore(f"{name}_{n}"))
        core.h = sb("h", [P, 2, D])
        hT = Pair(nc, ctx, f"{name}_hT", [P, KC, T])
        raw = sb("raw", [P, KC, COLS])
        w = Pair(nc, ctx, f"{name}_w", [P, KC, COLS])
        wb = sb("b", [E * R, D])
        bias = sb("bias", [P, D])
        low = sb("low", [P, TC, E * R])
        lowT = sb("lowT", [E * R, 2, P])
        w_loaded = sem("w_loaded")
        wb_loaded = sem("wb_loaded")
        bias_loaded = sem("bias_loaded")
        w_hi_ready = sem("w_hi_ready")
        w_ready = sem("w_ready")
        base_ready = sem("base_ready")
        base_free = sem("base_free")
        low_ready = sem("low_ready")
        turned = sem("turned")
        lowT_ready = sem("lowT_ready")
        out_ready = sem("out_ready")
        x_ready = sem("x_ready")
        stored = sem("stored")
        norm = Norm(core, hT, bias[:, :], bias_loaded)
        route = Router(core, ctx, name, probabilities=True)
        banks = [(core.proj[0], core.score[0]), (core.proj[1], core.score[1]), (core.outp[0], core.outp[1])]
        out_dram = out.rearrange("(c p) d -> c p d", p=P)

        with nc.Block() as block:

            @block.sync
            def _(sp):
                sp.dma_start(bias[:], io["L1_ffn_b_base"].partition_broadcast(P)).then_inc(bias_loaded, 16)
                for n, at, to in (("L1_base", 0, LOW), ("L1_A", LOW, GATE), ("L1_gate", GATE, COLS)):
                    sp.dma_start(raw[:, :, at:to], io[n].rearrange("(k p) n -> p k n", p=P)).then_inc(w_loaded, 16)
                sp.dma_start(route.ids[:], io["expert_ids"].partition_broadcast(P)).then_inc(route.loaded, 16)
                sp.dma_start(wb[:], io["L1_B"]).then_inc(wb_loaded, 16)
                for i in range(TC):
                    sp.wait_ge(x_ready, i + 1)
                    sp.dma_start(out_dram[i], core.x[:, i, :]).then_inc(stored, 16)
                sp.wait_ge(stored, TC * 16)

            @block.gpsimd
            def _(pool):
                norm.gpsimd(pool)

            @block.vector
            def _(dve):
                def lower_w(i):
                    if i in FIRST_W:
                        j = FIRST_W.index(i)
                        dve.wait_ge(w_hi_ready, j + 1)
                        dve.tensor_tensor(w.lo[:, j, :], raw[:, j, :], w.hi[:, j, :].bitcast(F32), ALU.subtract)\
                            .then_inc(w_ready, 1)

                norm.vector(dve, lower_w)
                for i in range(TC):
                    left, right = banks[i % DEPTH]
                    dve.wait_ge(base_ready, i + 1)
                    dve.tensor_copy(route.logits[:, i, :], right[:, GATE - HALF:COLS - HALF])
                    dve.tensor_copy(low[:, i, :], right[:, LOW - HALF:GATE - HALF])
                    dve.wait_ge(core.bias_added, norm.biased + i + 1)
                    for x, result in ((core.x[:, i, 0:HALF], left[:, 0:HALF]),
                                      (core.x[:, i, HALF:D], right[:, 0:D - HALF])):
                        last = dve.tensor_tensor(x, result, x, ALU.add)
                    last.then_inc(base_free, 1)
                dve.wait_ge(base_free, TC)
                route.vector(dve)
                for i in range(TC + 2):
                    if i < TC:
                        features = low[:, i, :].rearrange("p (e r) -> p e r", r=R)
                        dve.scalar_tensor_tensor(features, features, SCALING,
                                                 route.weight[:, i, :].unsqueeze(2).broadcast_to([P, E, R]),
                                                 ALU.mult, ALU.mult).then_inc(low_ready, 1)
                    if i >= 2:
                        dve.wait_ge(out_ready, i - 1)
                        dve.tensor_tensor(core.x[:, i - 2, :], core.proj[i % 2][:, :], core.x[:, i - 2, :],
                                          ALU.add).then_inc(x_ready, 1)

            @block.scalar
            def _(act):
                def split_w(i):
                    if i in FIRST_W:
                        j = FIRST_W.index(i)
                        act.wait_ge(w_loaded, 48)
                        act.copy(w.hi[:, j, :], raw[:, j, :]).then_inc(w_hi_ready, 1)

                norm.scalar(act, split_w)
                route.scalar(act)
                for i in range(TC):
                    act.wait_ge(turned, i + 1)
                    if i >= 2:
                        act.wait_ge(out_ready, i - 1)
                    act.copy(lowT[:, i % 2, :], core.turn[i % 2][:, 0:P]).then_inc(lowT_ready, 1)

            @block.tensor
            def _(pe):
                def base(i):
                    pe.wait_ge(norm.hT_ready, norm.n0 + i + 1)
                    pe.wait_ge(w_ready, KC)
                    if i >= DEPTH:
                        pe.wait_ge(base_free, i - DEPTH + 1)
                    at = slice(i * P, (i + 1) * P)
                    for bank, cols in zip(banks[i % DEPTH], (slice(0, HALF), slice(HALF, COLS))):
                        for k in range(KC):
                            last = product(pe, bank[:, 0:HALF], hT.hi[:, k, at], hT.lo[:, k, at],
                                           w.hi[:, k, cols], w.lo[:, k, cols], start=(k == 0), stop=(k == KC - 1))
                    last.then_inc(base_ready, 1)

                norm.tensor(pe, lambda i: base(i - EARLY) if i >= EARLY else None)
                for i in range(DEPTH, TC):
                    base(i)
                pe.wait_ge(base_free, TC)
                pe.wait_ge(wb_loaded, 16)
                for i in range(TC + 1):
                    if i < TC:
                        pe.wait_ge(low_ready, i + 1)
                        if i >= 2:
                            pe.wait_ge(lowT_ready, i - 1)
                        pe.transpose(core.turn[i % 2][:, 0:P], low[:, i, :], core.ident[:]).then_inc(turned, 1)
                    if i >= 1:
                        pe.wait_ge(lowT_ready, i)
                        if i >= 3:
                            pe.wait_ge(x_ready, i - 2)
                        pe.matmul(core.proj[(i - 1) % 2][:, :], lowT[:, (i - 1) % 2, :], wb[:, :],
                                  start=True, stop=True).then_inc(out_ready, 1)


def head_attention(nc, core, io, name):
    H, DH = 32, 16
    PACK = P // H
    GROUP = P // B
    ROWS = DH + PACK
    PACKS = D // P
    TOKENS = PACKS * PACK
    BLOCKS = SEQ // TOKENS
    UNITS = BLOCKS * B
    HPC = P // DH
    LAG, DEEP = 2, 4
    IDLE_PRODUCTS = 44
    HALVES = T // D
    BACK = D // P
    FIRST_W = range(2, 2 + KC)
    with ExitStack() as ctx:
        sb = lambda n, shape: ctx.enter_context(nc.sbuf_tensor(f"{name}_{n}", shape, F32))
        sem = lambda n: core.hold.enter_context(nc.semaphore(f"{name}_{n}"))
        hT = Pair(nc, ctx, f"{name}_hT", [P, KC, T])
        raw = sb("raw", [P, KC, D])
        w = Pair(nc, ctx, f"{name}_w", [P, KC, D])
        bias = sb("bias", [P, 3, KC])
        stage = sb("stage", [P, KC, T])
        spread = [sb(f"spread_{n}", [P, H, SEQ]) for n in "qkv"]
        context = spread[2]
        tags = sb("tags", [P, 2, TOKENS, H])
        slot = [sb(f"slot_{n}", [P, RING, TOKENS, H]) for n in "qkv"]
        values = sb("values", [P, RING, PACKS, B, GROUP])
        nmax = sb("nmax", [P, RING, PACKS])
        shifted = raw
        probs = stage[:, 0:DEEP // RING, :].rearrange("p a (r n) -> p (a r) n", r=RING)
        probsT = stage[:, DEEP // RING, :].rearrange("p (r n) -> p r n", r=RING)
        part = stage[:, DEEP // RING + 1, 0:RING * B * BACK * DH]\
            .rearrange("p (r b h d) -> p r b h d", r=RING, b=B, h=BACK)
        core.h = probs[:, 0:RING, :]
        rsum = sb("rsum", [P, RING, B, BACK])
        scratch = [nc.dram_tensor(f"{name}_scratch_{n}", (D, T), F32, kind="Internal").ap() for n in "qkv"]

        w_loaded = sem("w_loaded")
        w_hi_ready = sem("w_hi_ready")
        w_ready = sem("w_ready")
        consts_loaded = sem("consts_loaded")
        zeroed = sem("zeroed")
        ones_ready = sem("ones_ready")
        proj_ready = sem("proj_ready")
        proj_free = sem("proj_free")
        to_dram = [sem(f"to_dram{c}") for c in range(KC)]
        spread_loaded = [sem(f"spread_{n}_loaded") for n in "qkv"]
        slot_ready = sem("slot_ready")
        v_turned = sem("v_turned")
        v_ready = sem("v_ready")
        score_ready = sem("score_ready")
        max_ready = sem("max_ready")
        shifted_ready = sem("shifted_ready")
        probs_ready = sem("probs_ready")
        probs_turned = sem("probs_turned")
        probsT_ready = sem("probsT_ready")
        out_ready = sem("out_ready")
        out_copied = sem("out_copied")
        back_ready = sem("back_ready")
        rsum_ready = sem("rsum_ready")
        part_ready = sem("part_ready")
        norm = Norm(core, hT)

        def block_of(t, tile):
            return tile[:, :, ds(t * TOKENS, TOKENS)].rearrange("p h t -> p t h")

        def packs(tile):
            return tile.rearrange("p (a k) -> p a k", a=PACKS)

        def each_unit(engine, step):
            for j in range(RING * B):
                step(0, j, True)
            with engine.Fori(1, BLOCKS // RING) as i:
                for j in range(RING * B):
                    step(i, j, False)

        def place(i, j):
            return i * RING * B + j, j % RING, i * RING + j // B, j // B % RING, j % B

        with nc.Block() as block:

            @block.sync
            def _(sp):
                def load_w(j):
                    sp.dma_start(raw[:], io[f"L1_attn_w{'qkv'[j]}"].rearrange("(k p) n -> p k n", p=P))\
                        .then_inc(w_loaded, 16)

                def spread_out(j, c):
                    sp.wait_ge(to_dram[c], 16 * (j + 1))
                    for b in range(B):
                        sp.dma_start(spread[j][b * GROUP:b * GROUP + DH, c * HPC:(c + 1) * HPC, :],
                                     scratch[j].rearrange("(h d) t -> d h t", d=DH)
                                     [:, c * HPC:(c + 1) * HPC, b * SEQ:(b + 1) * SEQ]).then_inc(spread_loaded[j], 16)

                load_w(0)
                for j, n in enumerate("qkv"):
                    sp.dma_start(bias[:, j, :], io[f"L1_attn_b{n}"]).then_inc(consts_loaded, 16)
                sp.dma_start(tags[:], io["tags"].rearrange("j p (t h) -> p j t h", h=H)).then_inc(consts_loaded, 16)
                sp.wait_ge(w_ready, KC)
                load_w(1)
                sp.wait_ge(zeroed, 3)
                last = None
                for j in range(3):
                    for c in range(KC):
                        sp.wait_ge(proj_free, (j * KC + c + 1) * HALVES + RING)
                        sp.dma_start(scratch[j][c * P:(c + 1) * P, :], stage[:, c, :]).then_inc(to_dram[c], 16)
                        if last:
                            spread_out(*last)
                        last = (j, c)
                    if j == 0:
                        sp.wait_ge(w_ready, 2 * KC)
                        load_w(2)
                spread_out(*last)

            @block.gpsimd
            def _(pool):
                norm.gpsimd(pool)
                for j in range(3):
                    pool.memset(spread[j][:], 0.0).then_inc(zeroed, 1)
                pool.memset(values[:], 0.0).then_inc(zeroed, 1)
                pool.wait_ge(zeroed, 4)
                for r in range(RING):
                    pool.memset(values[:, r, :, :, DH:DH + 1], 1.0).then_inc(ones_ready, 1)
                def fill_slots(i, j, peeled):
                    _, _, t, r, b = place(i, j)
                    if b:
                        return
                    pool.wait_ge(consts_loaded, 64)
                    if not peeled:
                        pool.wait_ge(score_ready, (t - 1) * B)
                    for n in range(2):
                        if peeled:
                            pool.wait_ge(spread_loaded[n], 16 * B * KC)
                        pool.tensor_tensor(slot[n][:, r, :, :], block_of(t, spread[n]), tags[:, n, :, :], ALU.add)
                    if peeled:
                        pool.wait_ge(spread_loaded[2], 16 * B * KC)
                    pool.tensor_copy(slot[2][:, r, :, :], block_of(t, spread[2])).then_inc(slot_ready, 1)

                each_unit(pool, fill_slots)

            @block.vector
            def _(dve):
                dve.sem_inc(proj_free, RING)

                def lower_w(j, c):
                    at = slice(c * P, (c + 1) * P)
                    dve.wait_ge(w_hi_ready, j * KC + c + 1)
                    dve.tensor_tensor(w.lo[:, :, at], raw[:, :, at], w.hi[:, :, at].bitcast(F32), ALU.subtract)\
                        .then_inc(w_ready, 1)

                norm.vector(dve, lambda i: lower_w(0, FIRST_W.index(i)) if i in FIRST_W else None)
                dve.wait_ge(consts_loaded, 64)
                for j in range(3):
                    scale = float(DH) ** -0.5 if j == 0 else 1.0
                    for c in range(KC):
                        if j >= 1:
                            dve.wait_ge(to_dram[c], 16 * j)
                        for i in range(HALVES):
                            n = (j * KC + c) * HALVES + i
                            dve.wait_ge(proj_ready, n + 1)
                            dve.tensor_scalar(stage[:, c, i * D:(i + 1) * D], core.proj[n % 2][:, :],
                                              bias[:, j, c:c + 1], scale, ALU.add, ALU.mult)\
                                .then_inc(proj_free, 1)
                        if j < 2:
                            lower_w(j + 1, c)

                def softmax(i, j, peeled):
                    u, ur, t, r, b = place(i, j)
                    dve.wait_ge(score_ready, u + 1)
                    dve.tensor_reduce(nmax[:, ur, :], packs(core.score[ur][:, :]), AX.X, ALU.max)\
                        .then_inc(max_ready, 1)
                    dve.wait_ge(max_ready, u + 1)
                    dve.tensor_tensor(packs(shifted[:, j % DEEP, :]), packs(core.score[ur][:, :]),
                                      nmax[:, ur, :].unsqueeze(2).broadcast_to([P, PACKS, P]), ALU.subtract)\
                        .then_inc(shifted_ready, 1)

                each_unit(dve, softmax)
                for n in range(QC * H // BACK):
                    r, qc, h0 = n % RING, n % QC, n // QC * BACK
                    turned = core.turn[r][:, :].rearrange("p (h b s) -> p b h s", h=BACK, b=B)
                    dve.wait_ge(back_ready, n + 1)
                    dve.reciprocal(rsum[:, r, :, :], turned[:, :, :, DH]).then_inc(rsum_ready, 1)
                    dve.wait_ge(rsum_ready, n + 1)
                    dve.tensor_tensor(part[:, r, :, :, :], turned[:, :, :, 0:DH],
                                      rsum[:, r, :, :].unsqueeze(3).broadcast_to([P, B, BACK, DH]),
                                      ALU.mult).then_inc(part_ready, 1)
                    dve.wait_ge(part_ready, n + 1)
                    x = core.x[:].rearrange("p (b q) d -> p b q d", q=QC)[:, :, qc, h0 * DH:(h0 + BACK) * DH]
                    dve.tensor_tensor(x, x, part[:, r, :, :, :].rearrange("p b h d -> p b (h d)"), ALU.add)

            @block.scalar
            def _(act):
                def split_w(j, c):
                    if j:
                        act.wait_ge(proj_ready, ((j - 1) * KC + c + 1) * HALVES)
                    if c == 0:
                        act.wait_ge(w_loaded, 16 * (j + 1))
                    at = slice(c * P, (c + 1) * P)
                    act.copy(w.hi[:, :, at], raw[:, :, at]).then_inc(w_hi_ready, 1)

                norm.scalar(act, lambda i: split_w(0, FIRST_W.index(i)) if i in FIRST_W else None)
                for j in range(1, 3):
                    for c in range(KC):
                        split_w(j, c)
                act.wait_ge(ones_ready, RING)

                def copy_out(t, r):
                    act.wait_ge(out_ready, (t + 1) * B)
                    act.copy(block_of(t, context), core.proj[r][:, :].rearrange("p (t h) -> p t h", h=H))\
                        .then_inc(out_copied, 1)

                def turn_out(u, ur):
                    act.wait_ge(probs_turned, u + 1)
                    act.copy(probsT[:, ur, :], core.outp[ur][:, :]).then_inc(probsT_ready, 1)

                def softmax(i, j, peeled):
                    u, ur, t, r, b = place(i, j)
                    if not (peeled and j < LAG):
                        turn_out(u - LAG, ur)
                    if b == B - 1 and not (peeled and j < B):
                        copy_out(t - 1, 1 - r)
                    if b == 0:
                        act.wait_ge(v_turned, t + 1)
                        if not peeled:
                            act.wait_ge(out_ready, (t - 1) * B)
                        act.copy(values[:, r, :, :, 0:DH],
                                 core.turn[r][:, :].rearrange("p (a b s) -> p a b s", a=PACKS, b=B)[:, :, :, 0:DH])\
                            .then_inc(v_ready, 1)
                    act.wait_ge(shifted_ready, u + 1)
                    act.activation(probs[:, j % DEEP, :], shifted[:, j % DEEP, :], ACT.Exp).then_inc(probs_ready, 1)

                each_unit(act, softmax)
                for u in range(UNITS - LAG, UNITS):
                    turn_out(u, u % RING)
                copy_out(BLOCKS - 1, (BLOCKS - 1) % RING)

            @block.tensor
            def _(pe):
                norm.tensor(pe)
                pe.wait_ge(norm.hT_ready, norm.hT_done)
                for j in range(3):
                    for c in range(KC):
                        pe.wait_ge(w_ready, j * KC + c + 1)
                        for i in range(HALVES):
                            n = (j * KC + c) * HALVES + i
                            pe.wait_ge(proj_free, n + 1)
                            for k in range(KC):
                                at, tokens = slice(c * P, (c + 1) * P), slice(i * D, (i + 1) * D)
                                last = product(pe, core.proj[n % 2][:, :], w.hi[:, k, at], w.lo[:, k, at],
                                               hT.hi[:, k, tokens], hT.lo[:, k, tokens],
                                               start=(k == 0), stop=(k == KC - 1))
                            last.then_inc(proj_ready, 1)

                def turn(u, j, ur, bank_used):
                    pe.wait_ge(probs_ready, u + 1)
                    if bank_used:
                        pe.wait_ge(probsT_ready, u - 1)
                    for a in range(PACKS):
                        last = pe.transpose(core.outp[ur][:, a * P:(a + 1) * P], probs[:, j % DEEP, a * P:(a + 1) * P],
                                            core.ident[:])
                    last.then_inc(probs_turned, 1)

                def weigh(u, ur, t, r, b, bank_used):
                    pe.wait_ge(probsT_ready, u + 1)
                    if b == 0:
                        pe.wait_ge(v_ready, t + 1)
                        if bank_used:
                            pe.wait_ge(out_copied, t - 1)
                    for a in range(PACKS):
                        last = pe.matmul(core.proj[r][b * GROUP:(b + 1) * GROUP, a * P:(a + 1) * P],
                                         values[:, r, a, b, :], probsT[:, ur, a * P:(a + 1) * P],
                                         start=True, stop=True)
                    last.then_inc(out_ready, 1)

                def scores(i, j, peeled):
                    u, ur, t, r, b = place(i, j)
                    if b == 0:
                        pe.wait_ge(slot_ready, t + 1)
                        if not peeled:
                            pe.wait_ge(v_ready, t - 1)
                        for a in range(PACKS):
                            last = pe.transpose(core.turn[r][:, a * P:(a + 1) * P],
                                                slot[2][:, r, a * PACK:(a + 1) * PACK, :].rearrange("p t h -> p (t h)"),
                                                core.ident[:])
                        last.then_inc(v_turned, 1)
                    if not (peeled and j < RING):
                        pe.wait_ge(shifted_ready, u - 1)
                    rows = slice(b * GROUP, b * GROUP + ROWS)
                    for a in range(PACKS):
                        q, k = (slot[n][rows, r, a * PACK:(a + 1) * PACK, :].rearrange("p t h -> p (t h)")
                                for n in range(2))
                        last = pe.matmul(core.score[ur][:, a * P:(a + 1) * P], q, k, start=True, stop=True)
                    last.then_inc(score_ready, 1)
                    if not (peeled and j < LAG):
                        turn(u - LAG, j - LAG, ur, not (peeled and j - LAG < RING))
                    if not (peeled and j < LAG + 1):
                        _, _, t2, r2, b2 = place(i, j - LAG - 1)
                        weigh(u - LAG - 1, 1 - ur, t2, r2, b2, not peeled)

                with pe.Fori(0, IDLE_PRODUCTS // 4):
                    for _ in range(4):
                        pe.matmul(core.score[0][:, :], w.hi[:, 0, 0:P], hT.hi[:, 0, 0:D], start=True, stop=True)
                pe.wait_ge(proj_free, 3 * KC * HALVES + RING)
                each_unit(pe, scores)
                for u in range(UNITS - LAG, UNITS + 1):
                    if u < UNITS:
                        turn(u, u, u % RING, True)
                    weigh(u - 1, (u - 1) % RING, (u - 1) // B, (u - 1) // B % RING, (u - 1) % B, True)
                pe.wait_ge(out_copied, BLOCKS)
                for n in range(QC * H // BACK):
                    qc, h0 = n % QC, n // QC * BACK
                    if n >= RING:
                        pe.wait_ge(part_ready, n - 1)
                    for h in range(BACK):
                        last = pe.transpose(core.turn[n % RING][:, h * P:(h + 1) * P],
                                            context[:, h0 + h, qc * P:(qc + 1) * P], core.ident[:])
                    last.then_inc(back_ready, 1)


def build_program(nc, io, out):
    with ExitStack() as ctx:
        core = Core(nc, ctx)
        self_attention(nc, core, io, "self", 1e-6)
        context_attention(nc, core, io, "context", 1e-5)
        expert_mixture(nc, core, io, "experts")
        head_attention(nc, core, io, "heads")
        latent_attention(nc, core, io, "latent")
        adapted_linear(nc, core, io, "adapted", out)


def layout(inputs):
    import numpy as np

    a = {n: np.asarray(v) for n, v in inputs.items()}
    flat = {n: a[n] for n in ("L0_attn_Wq", "L0_attn_bq", "L0_attn_Wk", "L0_attn_bk", "L0_attn_Wv",
                              "L0_attn_bv", "L0_attn_Wo", "L0_attn_bo", "L0_attn_gq", "L0_attn_gk")}
    flat["x"] = a["x"].reshape(T, D)
    flat["ident"] = np.eye(P, dtype=np.float32)
    flat["expert_ids"] = np.arange(E, dtype=np.float32)
    flat["ctxT"] = a["ctx_4096"].reshape(B * CTX, D).T
    flat["mask"] = a["mask_1x1xSxS2_ff0"].reshape(SEQ, CTX)
    for n in "qkvo":
        flat[f"L0_xattn_{n}"] = a[f"L0_xattn_{n}_proj_w"].T
        flat[f"L1_xattn_{n}"] = a[f"L1_xattn_W{n}"].T
        if n != "o":
            flat[f"L1_attn_w{n}"] = a[f"L1_attn_w{n}"].T
            flat[f"L1_attn_b{n}"] = a[f"L1_attn_b{n}"].reshape(KC, P).T
    tags = np.zeros((2, B, P // B, 4, 32), np.float32)
    for t in range(4):
        tags[0, :, 16 + t, t, :] = 1.0
        tags[1, :, 16 + t, :, :] = -1e30
        tags[1, :, 16 + t, t, :] = 0.0
    flat["tags"] = np.tile(tags.reshape(2, P, P), (1, 1, 4))
    flat["L0_xattn_gq"] = a["L0_xattn_q_norm_w"]
    flat["L0_xattn_gk"] = a["L0_xattn_k_norm_w"]
    flat["L0_gate"] = a["L0_ffn_gate_w"]
    flat["L0_experts"] = a["L0_ffn_expert_w"]
    flat["L1_gate"] = a["L1_ffn_W_gate"].T
    flat["L1_base"] = a["L1_ffn_W_base"].T
    flat["L1_ffn_b_base"] = a["L1_ffn_b_base"]
    flat["L1_A"] = a["L1_ffn_A"].reshape(-1, D).T
    flat["L1_B"] = a["L1_ffn_B"].transpose(0, 2, 1).reshape(-1, D)
    return {n: np.ascontiguousarray(v) for n, v in flat.items()}


def kernel(**inputs):
    import concourse.bacc as bacc
    from concourse.bass_utils import run_bass_kernel_spmd

    nc = bacc.Bacc("TRN2", target_bir_lowering=False, num_devices=1)
    arrays = {f"in_{n}_dram": v for n, v in layout(inputs).items()}
    io = {n[3:-5]: nc.dram_tensor(n, v.shape, mybir.dt.from_np(v.dtype), kind="ExternalInput").ap()
          for n, v in arrays.items()}
    out = nc.dram_tensor("out_dram", (T, D), F32, kind="ExternalOutput").ap()
    build_program(nc, io, out)
    result = run_bass_kernel_spmd(nc, [arrays], core_ids=[0])
    return result.results[0]["out_dram"].reshape(B, SEQ, D)
```
